# Optimizing a Trainium2 kernel written in Bass

```python
import numpy as np
import jax
import jax.numpy as jnp

def _softmax(x, axis=-1):
    return jax.nn.softmax(x, axis=axis)

def _gelu(x):
    return jax.nn.gelu(x, approximate=True)

def _silu(x):
    return jax.nn.silu(x)

def _sigmoid(x):
    return jax.nn.sigmoid(x)

def _layernorm(x, axis=-1, eps=1e-05):
    m = jnp.mean(x, axis=axis, keepdims=True)
    v = jnp.var(x, axis=axis, keepdims=True)
    return (x - m) / jnp.sqrt(v + eps)

def _scatter_add(tgt, idx, src, axis=0):
    return tgt.at[idx].add(src)

def _segment_sum(src, seg, n):
    return jax.ops.segment_sum(src, seg, n)
kernel_name = 'mk_pixart_resid_d1_seqx_r2_b1ee68'

def setup_inputs(seed: int=0):
    np.random.seed(seed)
    _w = jnp.asarray

    def _rec_inputs():
        import jax
        import jax.numpy as jnp
        _rk = jax.random.key(seed)
        x = -0.0002928 + 1 * jax.random.normal(jax.random.fold_in(_rk, 1), (4, 1024, 512), jnp.float32)
        _lenS = 1024 - jax.random.randint(jax.random.fold_in(_rk, 7), (4,), 0, max(1, 1024 // 4) + 1, jnp.int32)
        _lenS2 = 64 - jax.random.randint(jax.random.fold_in(_rk, 8), (4,), 0, max(1, 64 // 4) + 1, jnp.int32)
        _ctx_1024P = jax.random.normal(jax.random.fold_in(_rk, 11), (4, 16, 512), jnp.float32)
        _ctx_1024c = jax.random.dirichlet(jax.random.fold_in(_rk, 511), 0.3 * jnp.ones((16,), jnp.float32), (4, 64))
        _ctx_1024t = jnp.einsum('bsk,bkd->bsd', _ctx_1024c, _ctx_1024P)
        _ctx_1024t = _ctx_1024t * jax.lax.rsqrt(jnp.mean(jnp.square(_ctx_1024t)) + 1e-12) * 0.953939
        ctx_1024 = -1.39393e-06 + 0.999914 * (_ctx_1024t + 0.3 * jax.random.normal(jax.random.fold_in(_rk, 611), (4, 64, 512), jnp.float32))
        condB_tau = jax.random.uniform(jax.random.fold_in(_rk, 12), (4,), jnp.float32, 0.0, 1.23395)
        fside_BxS2_0 = -0.00205293 + 0.99739 * jax.random.normal(jax.random.fold_in(_rk, 13), (4, 64), jnp.float32)
        return (x, ctx_1024, condB_tau, fside_BxS2_0)
    x, ctx_1024, condB_tau, fside_BxS2_0 = _rec_inputs()

    def _L0_xcond_setup():
        import jax, jax.numpy as jnp
        import numpy as np
        B, S, D, H = (2, 1024, 512, 16)
        DK = D // H

        def _split_heads(x):
            b, s, _ = x.shape
            return x.reshape(b, s, H, DK).transpose(0, 2, 1, 3)
        key = jax.random.key(seed)
        ks = jax.random.split(key, 14)
        inp = {'query': jax.random.normal(ks[0], (B, S, D), jnp.float32), 'key': jax.random.normal(ks[1], (B, S, D), jnp.float32), 'value': jax.random.normal(ks[2], (B, S, D), jnp.float32), 'tau': jax.random.uniform(ks[3], (B, 1), jnp.float32, 0.5, 1.5), 'delta': jax.random.normal(ks[4], (B, S), jnp.float32)}
        sc = 1.0 / np.sqrt(D)
        for i, name in enumerate(['q', 'k', 'v', 'o']):
            inp[f'W{name}'] = jax.random.normal(ks[5 + 2 * i], (D, D), jnp.float32) * sc
            inp[f'b{name}'] = jax.random.normal(ks[6 + 2 * i], (D,), jnp.float32) * 0.01
        return inp
    _L0_xcond_all = _L0_xcond_setup()
    _L0_xcond_in = {k: v for k, v in _L0_xcond_all.items() if k in ('Wq', 'bq', 'Wk', 'bk', 'Wv', 'bv', 'Wo', 'bo')}
    del _L0_xcond_all

    def _L0_ffn_setup():
        import jax, jax.numpy as jnp
        import numpy as np
        D_MODEL = 512
        HIDDEN = 512
        NUM_EXPERTS = 8
        TOP_K = 2
        key = jax.random.key(seed)
        ks = jax.random.split(key, 10)
        s = 0.02
        return {'x': jax.random.normal(ks[0], (2, 1024, D_MODEL), dtype=jnp.float32), 'gate_w': jax.random.normal(ks[1], (NUM_EXPERTS, D_MODEL), dtype=jnp.float32) * s, 'up_w': jax.random.normal(ks[2], (NUM_EXPERTS, D_MODEL, HIDDEN), dtype=jnp.float32) * s, 'up_b': jnp.zeros((NUM_EXPERTS, HIDDEN), dtype=jnp.float32), 'down_w': jax.random.normal(ks[3], (NUM_EXPERTS, HIDDEN, D_MODEL), dtype=jnp.float32) * s, 'down_b': jnp.zeros((NUM_EXPERTS, D_MODEL), dtype=jnp.float32), 'sh_up_w': jax.random.normal(ks[4], (D_MODEL, HIDDEN), dtype=jnp.float32) * s, 'sh_up_b': jnp.zeros((HIDDEN,), dtype=jnp.float32), 'sh_down_w': jax.random.normal(ks[5], (HIDDEN, D_MODEL), dtype=jnp.float32) * s, 'sh_down_b': jnp.zeros((D_MODEL,), dtype=jnp.float32)}
    _L0_ffn_all = _L0_ffn_setup()
    _L0_ffn_in = {k: v for k, v in _L0_ffn_all.items() if k in ('gate_w', 'up_w', 'up_b', 'down_w', 'down_b', 'sh_up_w', 'sh_up_b', 'sh_down_w', 'sh_down_b')}
    del _L0_ffn_all
    return {'x': x, 'ctx_1024': ctx_1024, 'condB_tau': condB_tau, 'fside_BxS2_0': fside_BxS2_0, 'L0_xcond_Wq': _L0_xcond_in['Wq'], 'L0_xcond_bq': _L0_xcond_in['bq'], 'L0_xcond_Wk': _L0_xcond_in['Wk'], 'L0_xcond_bk': _L0_xcond_in['bk'], 'L0_xcond_Wv': _L0_xcond_in['Wv'], 'L0_xcond_bv': _L0_xcond_in['bv'], 'L0_xcond_Wo': _L0_xcond_in['Wo'], 'L0_xcond_bo': _L0_xcond_in['bo'], 'L0_ffn_gate_w': _L0_ffn_in['gate_w'], 'L0_ffn_up_w': _L0_ffn_in['up_w'], 'L0_ffn_up_b': _L0_ffn_in['up_b'], 'L0_ffn_down_w': _L0_ffn_in['down_w'], 'L0_ffn_down_b': _L0_ffn_in['down_b'], 'L0_ffn_sh_up_w': _L0_ffn_in['sh_up_w'], 'L0_ffn_sh_up_b': _L0_ffn_in['sh_up_b'], 'L0_ffn_sh_down_w': _L0_ffn_in['sh_down_w'], 'L0_ffn_sh_down_b': _L0_ffn_in['sh_down_b']}

def reference(x, ctx_1024, condB_tau, fside_BxS2_0, L0_xcond_Wq, L0_xcond_bq, L0_xcond_Wk, L0_xcond_bk, L0_xcond_Wv, L0_xcond_bv, L0_xcond_Wo, L0_xcond_bo, L0_ffn_gate_w, L0_ffn_up_w, L0_ffn_up_b, L0_ffn_down_w, L0_ffn_down_b, L0_ffn_sh_up_w, L0_ffn_sh_up_b, L0_ffn_sh_down_w, L0_ffn_sh_down_b):
    import jax
    import jax.numpy as jnp

    def _L0_xcond_ref(query, key, value, tau, delta, Wq, bq, Wk, bk, Wv, bv, Wo, bo):
        import jax, jax.numpy as jnp
        import numpy as np
        B, S, D, H = (2, 1024, 512, 16)
        DK = D // H

        def _split_heads(x):
            b, s, _ = x.shape
            return x.reshape(b, s, H, DK).transpose(0, 2, 1, 3)
        q = _split_heads(query @ Wq.T + bq)
        k = _split_heads(key @ Wk.T + bk)
        v = _split_heads(value @ Wv.T + bv)
        scores = jnp.einsum('bhqd,bhkd->bhqk', q, k)
        scores = scores * tau[:, :, None, None] + delta[:, None, None, :]
        scores = scores / jnp.sqrt(jnp.asarray(DK, scores.dtype))
        p_attn = jax.nn.softmax(scores, axis=-1)
        x = jnp.einsum('bhqk,bhkd->bhqd', p_attn, v)
        x = x.transpose(0, 2, 1, 3).reshape(query.shape[0], -1, H * DK)
        return x @ Wo.T + bo

    def _L0_ffn_ref(x, gate_w, up_w, up_b, down_w, down_b, sh_up_w, sh_up_b, sh_down_w, sh_down_b):
        import jax, jax.numpy as jnp
        import numpy as np
        D_MODEL = 512
        HIDDEN = 512
        NUM_EXPERTS = 8
        TOP_K = 2
        b, s, d = x.shape
        xf = x.reshape(-1, d)
        shared = jax.nn.silu(x @ sh_up_w + sh_up_b) @ sh_down_w + sh_down_b
        logits = xf @ gate_w.T
        scores = jax.nn.softmax(logits, axis=-1)
        topk_w, topk_i = jax.lax.top_k(scores, TOP_K)
        topk_w = topk_w / (topk_w.sum(axis=-1, keepdims=True) + 1e-20)
        comb = (jax.nn.one_hot(topk_i, NUM_EXPERTS, dtype=xf.dtype) * topk_w[..., None]).sum(axis=1)
        h = jnp.einsum('nd,edh->neh', xf, up_w) + up_b
        h = jax.nn.silu(h)
        ye = jnp.einsum('neh,ehd->ned', h, down_w) + down_b
        y = jnp.einsum('ned,ne->nd', ye, comb).reshape(b, s, d)
        return y + shared
    x = x + _L0_xcond_ref(_layernorm(x, axis=-1), ctx_1024, ctx_1024, condB_tau[:, None], fside_BxS2_0, L0_xcond_Wq, L0_xcond_bq, L0_xcond_Wk, L0_xcond_bk, L0_xcond_Wv, L0_xcond_bv, L0_xcond_Wo, L0_xcond_bo)
    x = x + _L0_ffn_ref(_layernorm(x, axis=-1), L0_ffn_gate_w, L0_ffn_up_w, L0_ffn_up_b, L0_ffn_down_w, L0_ffn_down_b, L0_ffn_sh_up_w, L0_ffn_sh_up_b, L0_ffn_sh_down_w, L0_ffn_sh_down_b)
    return x

_drawn_inputs = setup_inputs


def setup_inputs(seed=0):
    import zlib

    import numpy as np

    out = dict(_drawn_inputs(seed))
    spreads = {'L0_ffn_up_b': (0.0, 0.517),
     'L0_ffn_down_b': (0.0, 0.1),
     'L0_ffn_sh_up_b': (0.0, 0.385),
     'L0_ffn_sh_down_b': (0.0, 0.1)}
    factors = {'L0_xcond_bq': 28.271, 'L0_xcond_bk': 64.0, 'L0_xcond_bv': 5.303, 'L0_xcond_bo': 4.624}
    for name, (base, spread) in spreads.items():
        noise = np.random.default_rng([zlib.crc32(name.encode()), seed]).standard_normal(out[name].shape)
        drawn = base * np.exp(spread * noise) if base else spread * noise
        out[name] = jnp.asarray(drawn.astype(out[name].dtype))
    for name, factor in factors.items():
        out[name] = (out[name] * factor).astype(out[name].dtype)
    return out
```

```python
from contextlib import ExitStack

import numpy as np

import concourse.bass as bass
from concourse import mybir

F32 = mybir.dt.float32
F16 = mybir.dt.float16
BF16 = mybir.dt.bfloat16
I32 = mybir.dt.int32
ALU = mybir.AluOpType
ACT = mybir.ActivationFunctionType
AX = mybir.AxisListType

P = 128
B, S, D, H, SK = 4, 1024, 512, 16, 64
DK = D // H
KB = D // P
TOKENS = B * S
TILES = TOKENS // P
TB = S // P
PAIRS = H // 2
QUADS = H // 4
VW = 2 * DK + 2
E = 8
PLACES = E + 1
TOPK = 2
SLOTS = TOKENS * TOPK // P + E
WSCALE = 16.0
EPS = 1e-5
EARLY = 4
META = 24
ROW = D + META
XROW = 2 * D
HI, LO = 0, 1
PRODUCTS = ((HI, HI), (HI, LO), (LO, HI))


def build_program(nc, x, ctxT, tau, delta, wqT, wkT, wvT, woT, bq, bk, bv, bo,
                  gateT, ffn_w, up_b, down_b, out, stop_after=None):
    ctx = ExitStack()
    with ctx:
        def sb(name, shape, dt=F32):
            return ctx.enter_context(nc.sbuf_tensor(name, shape, dt))

        def sem(name):
            return ctx.enter_context(nc.semaphore(name))

        xrows = nc.dram_tensor("xrows", [TILES, P, XROW], F32).ap()
        sorted_rows = nc.dram_tensor("sorted_rows", [SLOTS * P, ROW], F32).ap()

        PLACE_W = 4 * KB * D // 2
        ATT0 = EARLY * PLACE_W
        FFN0 = PLACES * PLACE_W
        ARENA = 51620
        arena = sb("arena", [P, ARENA])
        small = sb("small", [P, 1300])
        cuts = {"small": 0}

        def cut(tensor, key, words, dt=F32):
            a = cuts[key]
            cuts[key] = a + words
            v = tensor[:, a:a + words]
            return v if dt == F32 else v.bitcast(dt)

        def keep(words, dt=F32):
            return cut(small, "small", words, dt)

        weights = arena[:, 0:FFN0].bitcast(F16).rearrange(
            "p (e m h k n) -> p e m h k n", e=PLACES, m=2, h=2, k=KB)
        ident = keep(P // 2, F16)
        upb = keep(PLACES * KB)
        zero_row = keep(ROW)
        logits = keep(TILES * E).rearrange("p (t e) -> p t e", e=E)
        slot_place = keep(SLOTS, I32)
        gate = keep(2 * KB * E // 2, F16).rearrange("p (h k e) -> p h k e", h=2, k=KB)
        tau_k = keep(B)
        bq_c = keep(KB)
        bk_c = keep(KB)
        upb_raw = keep(PLACES * KB)
        stat1 = keep(2 * 6).rearrange("p (i c) -> p i c", i=2)
        mv1 = keep(2 * 2).rearrange("p (i c) -> p i c", i=2)
        rstd1 = keep(2)
        root1 = keep(2 * 2).rearrange("p (i c) -> p i c", i=2)
        root2 = keep(2).rearrange("p (i c) -> p i c", i=1)
        var1 = keep(2)
        var2 = keep(1)
        eps_c = keep(1)
        stat2 = keep(6)
        mv2 = keep(2)
        rstd2 = keep(1)
        rowmax = keep(2 * H).rearrange("p (i h) -> p i h", i=2)
        rden = keep(H)
        ones3 = keep(P // 2, BF16)[0:3, :]

        cuts["att"] = ATT0

        def att(words, dt=F32):
            return cut(arena, "att", words, dt)

        wq = att(KB * D, F16).rearrange("p (h k n) -> p h k n", h=2, k=KB)
        wo = att(KB * D, F16).rearrange("p (h k n) -> p h k n", h=2, k=KB)
        kblk = att(B * QUADS * 4 * SK).rearrange("p (b g n) -> p b g n", b=B, g=QUADS)
        vblk = att(3 * B * PAIRS * VW // 2, BF16).rearrange("p (s b r n) -> p s b r n", s=3, b=B, r=PAIRS)
        delta3 = att(B * SK // 2, BF16)[0:3, :].rearrange("p (b n) -> p b n", b=B)
        bo_b = att(D)
        xT = att(2 * KB * S // 2, F16).rearrange("p (h k t) -> p h k t", h=2, k=KB)
        qT = att(2 * KB * 4 * P).rearrange("p (i k t) -> p i k t", i=2, k=KB)
        xin = att(2 * D).rearrange("p (i n) -> p i n", i=2)
        xn1 = att(2 * D).rearrange("p (i n) -> p i n", i=2)
        xhl = att(2 * D, F16).rearrange("p (i h n) -> p i h n", i=2, h=2)
        prob = att(2 * H * SK).rearrange("p (i n) -> p i n", i=2)
        phl = att(2 * H * SK, F16).rearrange("p (i h n) -> p i h n", i=2, h=2)
        pT = att(H * SK, F16).rearrange("p (h r t) -> p h r t", h=2, r=PAIRS)
        xres = att(2 * D).rearrange("p (i n) -> p i n", i=2)
        att_o = att(D)
        ohl = att(D, F16).rearrange("p (h n) -> p h n", h=2)
        oT = att(D, F16).rearrange("p (h k t) -> p h k t", h=2, k=KB)
        xrow = att(2 * XROW).rearrange("p (i n) -> p i n", i=2)
        xn2 = att(D)
        nT = att(D, F16).rearrange("p (h k t) -> p h k t", h=2, k=KB)
        wstage = att(2 * D).rearrange("p (i n) -> p i n", i=2)
        assert cuts["att"] <= ARENA, cuts["att"]

        cuts["pro"] = 0

        def pro(words, dt=F32):
            return cut(arena, "pro", words, dt)

        wk_f = pro(KB * D).rearrange("p (k n) -> p k n", k=KB)
        wv_f = pro(KB * D).rearrange("p (k n) -> p k n", k=KB)
        wq_f = pro(KB * D).rearrange("p (k n) -> p k n", k=KB)
        wo_f = pro(KB * D).rearrange("p (k n) -> p k n", k=KB)
        gate_f = pro(KB * E).rearrange("p (k e) -> p k e", k=KB)
        ctx_f = pro(KB * B * SK).rearrange("p (k b n) -> p k b n", k=KB, b=B)
        ctx_2 = pro(KB * B * 2 * SK).rearrange("p (k b d n) -> p k b d n", k=KB, b=B, d=2)
        k_f = pro(KB * B * SK).rearrange("p (k b n) -> p k b n", k=KB, b=B)
        v_f = pro(B * D).rearrange("p (b r n) -> p b r n", b=B, r=PAIRS)
        bv_b = pro(D)
        tau_b = pro(B)
        delta_f = pro(B * SK)
        delta_p = pro(B * SK // 2, BF16)
        delta_s = pro(B * SK)
        assert cuts["pro"] <= ATT0

        cuts["ffn"] = FFN0

        def ffn(words, dt=F32):
            return cut(arena, "ffn", words, dt)

        downb = ffn(PLACES * D).rearrange("p (e n) -> p e n", e=PLACES)
        NROW = 3
        RBUF = D + ROW + 2
        rows = ffn(NROW * RBUF).rearrange("p (i n) -> p i n", i=NROW)
        eT = ffn(2 * D, F16).rearrange("p (i h k t) -> p i h k t", i=2, h=2, k=KB)
        pre = ffn(2 * D).rearrange("p (i n) -> p i n", i=2)
        hid = ffn(D)
        hhl = ffn(2 * D, F16).rearrange("p (i h n) -> p i h n", i=2, h=2)
        wbias = ffn(D)
        yout = ffn(2 * D).rearrange("p (i n) -> p i n", i=2)
        estage = ffn(2 * D).rearrange("p (i n) -> p i n", i=2)
        meta = ffn(TILES * (META + 2)).rearrange("p (t n) -> p t n", t=TILES)
        cuts["rt"] = (PLACES - 2) * PLACE_W

        def rt(a=TILES, c=E, dt=F32):
            v = cut(arena, "rt", a * c // (2 if dt == F16 else 1), dt)
            return v.rearrange("p (a c) -> p a c", a=a) if c > 1 else v

        assert cuts["ffn"] <= ARENA, cuts["ffn"]
        row_hl = [rows[:, i, D:2 * D].bitcast(F16).rearrange("p (h n) -> p h n", h=2) for i in range(NROW)]

        psum = ctx.enter_context(nc.psum_tensor("psum", [P, 8, 512], F32))
        scores_ps = [psum[:, 2 * i:2 * i + 2, :].rearrange("p a n -> p (a n)") for i in range(2)]
        probT_ps = [a.bitcast(F16).rearrange("p (h r t) -> p h r t", h=2, r=PAIRS) for a in scores_ps]
        att_ps = psum[:, 4:6, :].rearrange("p a n -> p (a n)").rearrange("p (r n) -> p r n", r=PAIRS)
        gate_ps = psum[:, 4, VW:VW + E]
        turn_ps = psum[:, 6, :]
        turn16_ps = turn_ps.bitcast(F16).rearrange("p (h k t) -> p h k t", h=2, k=KB)
        proj_ps = psum[:, 7, :]
        eturn16_ps = [psum[:, 0 + i, :].bitcast(F16).rearrange("p (h k t) -> p h k t", h=2, k=KB) for i in range(2)]
        up_ps = [psum[:, 2 + i, :] for i in range(2)]
        down_ps = [psum[:, 4 + i, :] for i in range(2)]

        def s2(name):
            return [sem(f"{name}0"), sem(f"{name}1")]

        id0, id_ready, consts_ready = sem("id0"), sem("id_ready"), sem("consts_ready")
        kv_loaded, q_loaded, misc_loaded, small_loaded, o_loaded = (
            sem("kv_loaded"), sem("q_loaded"), sem("misc_loaded"), sem("small_loaded"), sem("o_loaded"))
        ctx2_ready, k_mm, k_read, kblk_ready, v_mm, v_read = (
            sem("ctx2_ready"), sem("k_mm"), sem("k_read"), sem("kblk_ready"), sem("v_mm"), sem("v_read"))
        vblk_ready, pro_dve, pro_act, w_scaled, w_split, tau_ready, delta_ready, pro_pe = (
            sem("vblk_ready"), sem("pro_dve"), sem("pro_act"), sem("w_scaled"), sem("w_split"),
            sem("tau_ready"), sem("delta_ready"), sem("pro_pe"))
        prefilled, trash_zeroed = sem("prefilled"), sem("trash_zeroed")
        xin_loaded = s2("xin_loaded")
        ln1_stats, ln1_mv, ln1_rstd, ln1_done = sem("ln1_stats"), sem("ln1_mv"), sem("ln1_rstd"), sem("ln1_done")
        ln1_guess, ln1_steps, ln2_guess, ln2_steps, ln1_log, ln2_log = (
            sem("ln1_guess"), sem("ln1_steps"), sem("ln2_guess"), sem("ln2_steps"), sem("ln1_log"), sem("ln2_log"))
        xhi_done, xlo_done, xturn_done, xT_ready = sem("xhi_done"), sem("xlo_done"), sem("xturn_done"), sem("xT_ready")
        q_mm, q_ready = sem("q_mm"), sem("q_ready")
        scores_done, max_done, sub_done, exp_done, plo_done = (
            sem("scores_done"), sem("max_done"), sem("sub_done"), sem("exp_done"), sem("plo_done"))
        pturn_done, pT_ready, att_done, rden_done, norm_done = (
            sem("pturn_done"), sem("pT_ready"), sem("att_done"), sem("rden_done"), sem("norm_done"))
        ohi_done, olo_done, oturn_done, oT_ready, proj_done = (
            sem("ohi_done"), sem("olo_done"), sem("oturn_done"), sem("oT_ready"), sem("proj_done"))
        xres_loaded = s2("xres_loaded")
        xres_biased, x1_done, ln2_stats, ln2_mv, ln2_rstd, ln2_done = (
            sem("xres_biased"), sem("x1_done"), sem("ln2_stats"), sem("ln2_mv"), sem("ln2_rstd"), sem("ln2_done"))
        nhi_done, nlo_done, nturn_done, nT_ready, gate_done, logits_ready = (
            sem("nhi_done"), sem("nlo_done"), sem("nturn_done"), sem("nT_ready"), sem("gate_done"), sem("logits_ready"))
        xrow_stored = s2("xrow_stored")
        wstage_loaded = s2("wstage_loaded")
        wst_scaled, wst_split = sem("wst_scaled"), sem("wst_split")

        passed = sem("passed")

        def settled(eng):
            eng.sem_inc(passed, 1)

        def tiled(b, c):
            return b * TB + c

        def transposes(eng, dst, src_hi_lo, n):
            for h in range(2):
                for k in range(n):
                    last = eng.transpose(dst[:, h, k, :], src_hi_lo[:, h, k * P:(k + 1) * P], ident)
            return last

        def split_products(eng, dst, lhs, rhs):
            n = 0
            for k in range(KB):
                for a, c in PRODUCTS:
                    last = eng.matmul(dst, lhs(a, k), rhs(c, k), start=(n == 0), stop=(n == 3 * KB - 1))
                    n += 1
            return last

        def bcast_rows(ap, n):
            return ap.rearrange("(o n) -> o n", o=1).to_broadcast([n, ap.shape[0]])

        with nc.Block() as block:

            @block.sync
            def _(sp):
                sp.dma_start(xin[:, 0, :], x[0]).then_inc(xin_loaded[0], 16)
                sp.dma_start(xin[:, 1, :], x[1]).then_inc(xin_loaded[1], 16)
                sp.dma_start(wq_f, wqT.rearrange("(k p) n -> p k n", p=P)).then_inc(q_loaded, 16)
                sp.dma_start(ctx_f, ctxT.rearrange("(k p) (b n) -> p k b n", p=P, b=B)).then_inc(kv_loaded, 16)
                sp.dma_start(wk_f, wkT.rearrange("(k p) n -> p k n", p=P)).then_inc(kv_loaded, 16)
                sp.dma_start(wv_f, wvT.rearrange("(k p) n -> p k n", p=P)).then_inc(kv_loaded, 16)
                sp.dma_start(wo_f, woT.rearrange("(k p) n -> p k n", p=P)).then_inc(o_loaded, 16)
                for m in range(2, TB):
                    sp.wait_ge(ln1_done, m - 1)
                    sp.dma_start(xin[:, m % 2, :], x[m]).then_inc(xin_loaded[m % 2], 16)
                sp.dma_start(xres[:, 0, :], x[0]).then_inc(xres_loaded[0], 16)
                sp.dma_start(wstage[:, 0, :], ffn_w[0, 0, 0:P, :]).then_inc(wstage_loaded[0], 16)
                def store_row(b, t):
                    sp.wait_ge(nlo_done, tiled(b, t + 1))
                    sp.dma_start(xrows[bass.ds(tiled(b, t), 1)].rearrange("o p n -> p (o n)"),
                                 xrow[:, t % 2, :]).then_inc(xrow_stored[t % 2], 16)

                def batch(b, last):
                    for t in range(TB):
                        if not last:
                            sp.wait_ge(ln1_done, tiled(b, TB + t - 1))
                            sp.dma_start(xin[:, t % 2, :],
                                         x[bass.ds(tiled(b, TB + t), 1)].rearrange("o p n -> p (o n)")
                                         ).then_inc(xin_loaded[t % 2], 16)
                        if not (last and t == TB - 1):
                            sp.wait_ge(x1_done, tiled(b, t))
                            sp.dma_start(xres[:, (t + 1) % 2, :],
                                         x[bass.ds(tiled(b, t + 1), 1)].rearrange("o p n -> p (o n)")
                                         ).then_inc(xres_loaded[(t + 1) % 2], 16)
                            sp.wait_ge(wst_split, tiled(b, t))
                            c = (t + 1) % TB
                            sp.dma_start(wstage[:, (t + 1) % 2, :],
                                         ffn_w[bass.ds(b + (t + 1) // TB, 1), c // KB,
                                               (c % KB) * P:(c % KB + 1) * P, :].rearrange("o p n -> p (o n)")
                                         ).then_inc(wstage_loaded[(t + 1) % 2], 16)
                        if t > 0:
                            store_row(b, t - 1)
                    store_row(b, TB - 1)

                with sp.Fori(0, B - 1) as b:
                    batch(b, last=False)
                batch(B - 1, last=True)
                sp.wait_ge(xrow_stored[0], 16 * TILES // 2)
                sp.wait_ge(xrow_stored[1], 16 * TILES // 2)
                sp.wait_ge(prefilled, 32)
                sp.wait_ge(trash_zeroed, 16)

            @block.scalar
            def _(act):
                def guess(i, count, mv, root, mv_done, log_done, done):
                    act.wait_ge(mv_done, count)
                    y = root[:, i, 0:1]
                    act.activation(y, mv, ACT.Ln, bias=eps_c).then_inc(log_done, 1)
                    act.wait_ge(log_done, count)
                    act.activation(y, y, ACT.Exp, scale=-0.5).then_inc(done, 1)

                def guess_1(i, count):
                    guess(i, count, mv1[:, i, 1:2], root1, ln1_mv, ln1_log, ln1_guess)

                def guess_2(count):
                    guess(0, count, mv2[:, 1:2], root2, ln2_mv, ln2_log, ln2_guess)

                act.dma_start(tau_b, bcast_rows(tau, P)).then_inc(small_loaded, 16)
                act.dma_start(delta_f[0:3, :], bcast_rows(delta, 3)).then_inc(small_loaded, 16)
                act.dma_start(bq_c, bq).then_inc(small_loaded, 16)
                act.dma_start(bk_c, bk).then_inc(small_loaded, 16)
                act.dma_start(upb_raw, up_b).then_inc(small_loaded, 16)
                act.dma_start(gate_f, gateT.rearrange("(k p) e -> p k e", p=P)).then_inc(small_loaded, 16)
                act.dma_start(bv_b, bcast_rows(bv, P)).then_inc(small_loaded, 16)
                act.dma_start(bo_b, bcast_rows(bo, P)).then_inc(small_loaded, 16)
                act.wait_ge(consts_ready, 5)
                for i in range(2):
                    n = SLOTS // 2
                    act.dma_start(sorted_rows[i * n * P:(i + 1) * n * P, :].rearrange("(s p) n -> p s n", p=P),
                                  zero_row.rearrange("p (s n) -> p s n", s=1).to_broadcast([P, n, ROW])
                                  ).then_inc(prefilled, 16)
                act.dma_start(out[TOKENS:TOKENS + P, :], zero_row[:, 0:D]).then_inc(trash_zeroed, 16)

                guess_1(0, 1)
                guess_1(1, 2)
                act.wait_ge(small_loaded, 128)
                act.wait_ge(q_loaded, 16)
                act.activation(wq[:, HI], wq_f, ACT.Copy, scale=WSCALE)
                act.activation(wq_f, wq_f, ACT.Copy, scale=WSCALE).then_inc(w_scaled, 1)

                def x_hi(m, count):
                    act.wait_ge(ln1_done, count(1))
                    if m >= 2:
                        act.wait_ge(xturn_done, count(-1))
                    act.activation(xhl[:, m % 2, HI, :], xn1[:, m % 2, :], ACT.Copy).then_inc(xhi_done, 1)

                def x_turned(m, count, q_count=None):
                    act.wait_ge(xturn_done, count(1))
                    if q_count is not None:
                        act.wait_ge(q_mm, q_count)
                    c = m % TB
                    act.activation(xT[:, :, :, c * P:(c + 1) * P], turn16_ps, ACT.Copy).then_inc(xT_ready, 1)

                def q_out(q, count, s_count=None):
                    act.wait_ge(q_mm, count)
                    if s_count is not None:
                        act.wait_ge(scores_done, s_count)
                    act.activation(qT[:, (q // KB) % 2, q % KB, :], proj_ps, ACT.Identity,
                                   bias=bq_c[:, q % KB:q % KB + 1], scale=1.0 / WSCALE).then_inc(q_ready, 1)

                def exps(i, count, pt_count=None):
                    act.wait_ge(sub_done, count)
                    if pt_count is not None:
                        act.wait_ge(pturn_done, pt_count)
                    act.activation(phl[:, i, HI, :], prob[:, i, :], ACT.Exp)
                    act.activation(prob[:, i, :], prob[:, i, :], ACT.Exp).then_inc(exp_done, 1)

                x_hi(0, lambda c: 0 + c)
                x_hi(1, lambda c: 1 + c)
                act.activation(gate[:, HI], gate_f, ACT.Copy, scale=WSCALE)
                act.activation(gate_f, gate_f, ACT.Copy, scale=WSCALE).then_inc(w_scaled, 1)
                act.activation(upb, upb_raw, ACT.Copy, scale=WSCALE)
                for g in range(KB):
                    act.wait_ge(k_mm, g + 1)
                    act.activation(k_f[:, g], psum[:, g % 2, 0:B * SK].rearrange("p (b n) -> p b n", b=B),
                                   ACT.Identity, bias=bk_c[:, g:g + 1]).then_inc(k_read, 1)
                for m in range(TB):
                    x_turned(m, lambda c, m=m: m + c)
                    if m + 2 < TB:
                        guess_1(m % 2, m + 3)
                        x_hi(m + 2, lambda c, m=m: m + 2 + c)
                act.wait_ge(o_loaded, 16)
                act.activation(wo[:, HI], wo_f, ACT.Copy, scale=WSCALE)
                act.activation(wo_f, wo_f, ACT.Copy, scale=WSCALE).then_inc(w_scaled, 1)
                for q in range(KB + 1):
                    q_out(q, q + 1)
                exps(0, 1)
                act.wait_ge(vblk_ready, B)
                act.wait_ge(kblk_ready, KB)
                act.wait_ge(w_split, 3)

                def norm2_out(b, t):
                    act.wait_ge(ln2_done, tiled(b, t + 1))
                    act.activation(xrow[:, t % 2, D:].bitcast(F16)[:, 0:D], xn2, ACT.Copy).then_inc(nhi_done, 1)
                    act.wait_ge(nturn_done, tiled(b, t + 1))
                    act.activation(nT, turn16_ps, ACT.Copy).then_inc(nT_ready, 1)
                    act.wait_ge(gate_done, tiled(b, t + 1))
                    act.activation(logits[:, bass.ds(tiled(b, t), 1), :].rearrange("p o e -> p (o e)"), gate_ps,
                                   ACT.Copy, scale=1.0 / WSCALE).then_inc(logits_ready, 1)

                def batch(b, last):
                    for t in range(TB):
                        if not last:
                            guess_1(t % 2, tiled(b, TB + t + 1))
                        act.wait_ge(pturn_done, tiled(b, t + 1))
                        act.activation(pT, probT_ps[t % 2], ACT.Copy).then_inc(pT_ready, 1)
                        if t > 0:
                            norm2_out(b, t - 1)
                        if not (last and t == TB - 1):
                            exps((t + 1) % 2, tiled(b, t + 2), tiled(b, t))
                        if not last:
                            x_hi(t + TB, lambda c, t=t: tiled(b, TB + t + c))
                            x_turned(t, lambda c, t=t: tiled(b, TB + t + c), tiled(b, 4 * (t // 4) + 4))
                        q = t + KB + 1
                        if not last or q < TB:
                            q_out(q, tiled(b, q + 1), tiled(b, 4 * (q // KB) - 4))
                        act.wait_ge(oturn_done, tiled(b, t + 1))
                        act.activation(oT, turn16_ps, ACT.Copy).then_inc(oT_ready, 1)
                        act.wait_ge(wstage_loaded[t % 2], b * 64 + 16 * (t // 2 + 1))
                        w = weights[:, bass.ds(b, 1), t // KB, HI, t % KB, :].rearrange("p o n -> p (o n)")
                        act.activation(w, wstage[:, t % 2, :], ACT.Copy, scale=WSCALE)
                        act.activation(wstage[:, t % 2, :], wstage[:, t % 2, :], ACT.Copy,
                                       scale=WSCALE).then_inc(wst_scaled, 1)
                        guess_2(tiled(b, t + 1))
                    norm2_out(b, TB - 1)

                with act.Fori(0, B - 1) as b:
                    batch(b, last=False)
                batch(B - 1, last=True)

            @block.gpsimd
            def _(pool):
                pool.memset(ident, 0.0).then_inc(id0, 1)
                pool.wait_ge(id0, 1)
                pool.affine_select(out=ident, in_=ident, compare_op=ALU.not_equal, fill=1.0, base=0,
                                   pattern=[[-1, P]], channel_multiplier=1).then_inc(id_ready, 1)
                pool.iota(zero_row[:, D:D + 1].bitcast(I32), pattern=[[0, 1]], base=TOKENS,
                          channel_multiplier=1).then_inc(consts_ready, 1)

                def rstd(i, count, mv, ve, root, dst, mv_done, guess_done, steps_done, done):
                    pool.wait_ge(mv_done, count)
                    settled(pool)
                    pool.tensor_scalar(ve[:, i:i + 1], mv, EPS, None, ALU.add)
                    pool.wait_ge(guess_done, count)
                    y, u = root[:, i, 0:1], root[:, i, 1:2]
                    pool.tensor_tensor(u, y, y, ALU.mult).then_inc(steps_done, 1)
                    pool.wait_ge(steps_done, count * 3 - 2)
                    pool.tensor_tensor(u, u, ve[:, i:i + 1], ALU.mult).then_inc(steps_done, 1)
                    pool.wait_ge(steps_done, count * 3 - 1)
                    settled(pool)
                    pool.tensor_scalar(u, u, -0.5, 1.5, ALU.mult, ALU.add).then_inc(steps_done, 1)
                    pool.wait_ge(steps_done, count * 3)
                    pool.tensor_tensor(dst, u, y, ALU.mult).then_inc(done, 1)

                def rstd_1(i, count):
                    rstd(i, count, mv1[:, i, 1:2], var1, root1, rstd1[:, i:i + 1], ln1_mv, ln1_guess, ln1_steps, ln1_rstd)

                def rstd_2(count):
                    rstd(0, count, mv2[:, 1:2], var2, root2, rstd2, ln2_mv, ln2_guess, ln2_steps, ln2_rstd)

                def x_lo(m, count):
                    pool.wait_ge(xhi_done, count(1))
                    pool.tensor_tensor(xhl[:, m % 2, LO, :], xn1[:, m % 2, :], xhl[:, m % 2, HI, :],
                                       ALU.subtract).then_inc(xlo_done, 1)

                def p_lo(i, count):
                    pool.wait_ge(exp_done, count)
                    pool.tensor_tensor(phl[:, i, LO, :], prob[:, i, :], phl[:, i, HI, :],
                                       ALU.subtract).then_inc(plo_done, 1)

                def w_lo(dst, src, hi, n):
                    pool.wait_ge(w_scaled, n)
                    pool.tensor_tensor(dst, src, hi, ALU.subtract).then_inc(w_split, 1)

                for m in range(2):
                    rstd_1(m, m + 1)
                w_lo(wq[:, LO], wq_f, wq[:, HI], 1)
                x_lo(0, lambda c: 0 + c)
                x_lo(1, lambda c: 1 + c)
                w_lo(gate[:, LO], gate_f, gate[:, HI], 2)
                for m in range(2, TB):
                    rstd_1(m % 2, m + 1)
                    x_lo(m, lambda c, m=m: m + c)
                w_lo(wo[:, LO], wo_f, wo[:, HI], 3)
                p_lo(0, 1)

                def n_lo(b, t):
                    pool.wait_ge(nhi_done, tiled(b, t + 1))
                    hl = xrow[:, t % 2, D:].bitcast(F16)
                    pool.tensor_tensor(hl[:, D:], xn2, hl[:, 0:D], ALU.subtract).then_inc(nlo_done, 1)

                def batch(b, last):
                    for t in range(TB):
                        if not last:
                            rstd_1(t % 2, tiled(b, TB + t + 1))
                        if t > 0:
                            n_lo(b, t - 1)
                        if not (last and t == TB - 1):
                            p_lo((t + 1) % 2, tiled(b, t + 2))
                        if not last:
                            x_lo(t, lambda c, t=t: tiled(b, TB + t + c))
                        pool.wait_ge(xres_loaded[t % 2], b * 64 + 16 * (t // 2 + 1))
                        pool.tensor_tensor(xres[:, t % 2, :], xres[:, t % 2, :], bo_b, ALU.add).then_inc(xres_biased, 1)
                        pool.wait_ge(wst_scaled, tiled(b, t + 1))
                        w = [weights[:, bass.ds(b, 1), t // KB, h, t % KB, :].rearrange("p o n -> p (o n)")
                             for h in range(2)]
                        pool.tensor_tensor(w[LO], wstage[:, t % 2, :], w[HI], ALU.subtract).then_inc(wst_split, 1)
                        rstd_2(tiled(b, t + 1))
                    n_lo(b, TB - 1)

                with pool.Fori(0, B - 1) as b:
                    batch(b, last=False)
                batch(B - 1, last=True)

            @block.vector
            def _(dve):
                dve.memset(zero_row[:, 0:D], 0.0).then_inc(consts_ready, 1)
                dve.memset(zero_row[:, D + 1:], 0.0).then_inc(consts_ready, 1)
                dve.memset(ones3, 1.0).then_inc(consts_ready, 1)
                dve.memset(eps_c, EPS).then_inc(consts_ready, 1)

                def stats1(m, count, loaded):
                    dve.wait_ge(xin_loaded[m % 2], loaded)
                    dve.bn_stats(stat1[:, m % 2, :], xin[:, m % 2, :]).then_inc(ln1_stats, 1)
                    dve.wait_ge(ln1_stats, count(1))
                    settled(dve)
                    dve.bn_aggr(mv1[:, m % 2, :], stat1[:, m % 2, :]).then_inc(ln1_mv, 1)

                def norm1(m, count):
                    dve.wait_ge(ln1_rstd, count(1))
                    if m >= 2:
                        dve.wait_ge(xlo_done, count(-1))
                    dve.tensor_scalar(xn1[:, m % 2, :], xin[:, m % 2, :], mv1[:, m % 2, 0:1],
                                      rstd1[:, m % 2:m % 2 + 1], ALU.subtract, ALU.mult).then_inc(ln1_done, 1)

                def max_sub(i, count, lo_count=None):
                    s3 = scores_ps[i].rearrange("p (h k) -> p h k", h=H)
                    dve.wait_ge(scores_done, count)
                    dve.tensor_reduce(rowmax[:, i, :], s3, AX.X, ALU.max).then_inc(max_done, 1)
                    dve.wait_ge(max_done, count)
                    if lo_count is not None:
                        dve.wait_ge(plo_done, lo_count)
                    dve.tensor_tensor(prob[:, i, :].rearrange("p (h k) -> p h k", h=H), s3,
                                      rowmax[:, i, :].unsqueeze(2).to_broadcast([P, H, SK]),
                                      ALU.subtract).then_inc(sub_done, 1)

                for m in range(2):
                    stats1(m, lambda c, m=m: m + c, 16)
                for m in range(2):
                    norm1(m, lambda c, m=m: m + c)

                steps = 0

                def step(instruction):
                    nonlocal steps
                    steps += 1
                    instruction.then_inc(pro_dve, 1)
                    dve.wait_ge(pro_dve, steps)

                step(dve.memset(kblk, 0.0))
                step(dve.memset(v_f, 0.0))
                step(dve.memset(vblk[:, :, :, :, 2 * DK:], 0.0))
                step(dve.memset(vblk[0:SK, 0, :, :, 2 * DK], 1.0))
                step(dve.memset(vblk[SK:P, 0, :, :, 2 * DK + 1], 1.0))
                dve.wait_ge(small_loaded, 128)
                step(dve.tensor_scalar(tau_k, tau_b, float(DK) ** -0.5, None, ALU.mult))
                dve.wait_ge(id_ready, 1)
                step(dve.tensor_scalar(delta_f[0:3], delta_f[0:3], float(DK) ** -0.5, None, ALU.mult))
                for i in range(3):
                    step(dve.tensor_copy(delta_p[0:3], delta_f[0:3]))
                    step(dve.tensor_tensor(delta_f[0:3], delta_f[0:3], delta_p[0:3], ALU.subtract))
                    if i == 0:
                        step(dve.tensor_scalar(delta_s[0:3], delta_p[0:3], ident[0:3, 0:1], None, ALU.mult))
                    else:
                        step(dve.scalar_tensor_tensor(out=delta_s[0:3], in0=delta_p[0:3],
                                                      scalar=ident[0:3, i:i + 1], in1=delta_s[0:3],
                                                      op0=ALU.mult, op1=ALU.add))
                dve.tensor_copy(delta3.rearrange("p b n -> p (b n)"), delta_s[0:3]).then_inc(delta_ready, 1)
                dve.wait_ge(kv_loaded, 48)
                for d in range(2):
                    dve.tensor_copy(ctx_2[:, :, :, d, :], ctx_f).then_inc(ctx2_ready, 1)
                for g in range(QUADS):
                    dve.wait_ge(k_read, g + 1)
                    for j in range(4):
                        r = slice(j * DK, (j + 1) * DK)
                        last = dve.tensor_tensor(kblk[r, :, g, j * SK:(j + 1) * SK], k_f[r, g],
                                                 tau_k[r, :].unsqueeze(2).to_broadcast([DK, B, SK]), ALU.mult)
                    last.then_inc(kblk_ready, 1)
                for b in range(B):
                    dve.wait_ge(v_mm, b + 1)
                    for j in range(2):
                        r, c = slice(j * SK, (j + 1) * SK), slice(j * DK, (j + 1) * DK)
                        ins = dve.tensor_tensor(
                            v_f[r, b, :, c], psum[r, 2 + b % 2, :].rearrange("p (r n) -> p r n", r=PAIRS)[:, :, c],
                            bv_b[r].rearrange("p (r n) -> p r n", r=PAIRS)[:, :, c], ALU.add)
                        if j == 1:
                            ins.then_inc(v_read, 1)
                    dve.wait_ge(v_read, b + 1)
                    for i in range(3):
                        ins = dve.tensor_copy(vblk[:, i, b, :, 0:2 * DK], v_f[:, b])
                        if i < 2:
                            step(ins)
                            step(dve.tensor_tensor(v_f[:, b], v_f[:, b], vblk[:, i, b, :, 0:2 * DK], ALU.subtract))
                    ins.then_inc(vblk_ready, 1)
                for m in range(2, TB):
                    stats1(m, lambda c, m=m: m + c, 16 * (m // 2 + 1))
                    norm1(m, lambda c, m=m: m + c)
                max_sub(0, 1)

                def batch(b, last):
                    for t in range(TB):
                        if not last:
                            stats1(t + TB, lambda c, t=t: tiled(b, TB + t + c), b * 64 + 64 + 16 * (t // 2 + 1))
                        if not (last and t == TB - 1):
                            max_sub((t + 1) % 2, tiled(b, t + 2), tiled(b, t))
                        if not last:
                            norm1(t + TB, lambda c, t=t: tiled(b, TB + t + c))
                        dve.wait_ge(att_done, tiled(b, t + 1))
                        dve.reciprocal(rden.rearrange("p (r j) -> p r j", r=PAIRS),
                                       att_ps[:, :, 2 * DK:VW]).then_inc(rden_done, 1)
                        dve.wait_ge(rden_done, tiled(b, t + 1))
                        dve.tensor_tensor(att_o.rearrange("p (r j n) -> p r j n", r=PAIRS, j=2),
                                          att_ps[:, :, 0:2 * DK].rearrange("p r (j n) -> p r j n", j=2),
                                          rden.rearrange("p (r j) -> p r j", r=PAIRS).unsqueeze(3)
                                          .to_broadcast([P, PAIRS, 2, DK]), ALU.mult).then_inc(norm_done, 1)
                        dve.wait_ge(norm_done, tiled(b, t + 1))
                        dve.wait_ge(oturn_done, tiled(b, t))
                        dve.tensor_copy(ohl[:, HI, :], att_o).then_inc(ohi_done, 1)
                        dve.wait_ge(ohi_done, tiled(b, t + 1))
                        dve.tensor_tensor(ohl[:, LO, :], att_o, ohl[:, HI, :], ALU.subtract).then_inc(olo_done, 1)
                        dve.wait_ge(proj_done, tiled(b, t + 1))
                        dve.wait_ge(xres_biased, tiled(b, t + 1))
                        dve.wait_ge(xrow_stored[t % 2], b * 64 + 16 * (t // 2))
                        x1 = xrow[:, t % 2, 0:D]
                        dve.scalar_tensor_tensor(out=x1, in0=proj_ps, scalar=1.0 / WSCALE, in1=xres[:, t % 2, :],
                                                 op0=ALU.mult, op1=ALU.add).then_inc(x1_done, 1)
                        dve.wait_ge(x1_done, tiled(b, t + 1))
                        dve.bn_stats(stat2, x1).then_inc(ln2_stats, 1)
                        dve.wait_ge(ln2_stats, tiled(b, t + 1))
                        settled(dve)
                        dve.bn_aggr(mv2, stat2).then_inc(ln2_mv, 1)
                        dve.wait_ge(ln2_rstd, tiled(b, t + 1))
                        dve.wait_ge(nlo_done, tiled(b, t))
                        dve.tensor_scalar(xn2, x1, mv2[:, 0:1], rstd2, ALU.subtract, ALU.mult).then_inc(ln2_done, 1)

                with dve.Fori(0, B - 1) as b:
                    batch(b, last=False)
                batch(B - 1, last=True)

            @block.tensor
            def _(pe):
                def scores(i, b, col, qi):
                    for a in range(2):
                        bank = scores_ps[i][:, a * 512:(a + 1) * 512]
                        for j in range(2):
                            g = 2 * a + j
                            pe.matmul(bank[:, j * 256:(j + 1) * 256], qT[:, qi, g, col:col + P],
                                      kblk[:, bass.ds(b, 1), g, :].rearrange("p o n -> p (o n)"),
                                      start=(j == 0), stop=False, skip_group_check=True)
                        last = pe.matmul(bank, ones3, delta3[:, bass.ds(b, 1), :].to_broadcast([3, PAIRS, SK]),
                                         start=False, stop=True, skip_group_check=True)
                    last.then_inc(scores_done, 1)

                def x_turn(m, count):
                    pe.wait_ge(xlo_done, count(1))
                    transposes(pe, turn16_ps, xhl[:, m % 2], KB).then_inc(xturn_done, 1)

                def project_q(q):
                    half = (q // KB) % 2
                    split_products(pe, proj_ps,
                                   lambda part, k: wq[:, part, k, (q % KB) * P:(q % KB + 1) * P],
                                   lambda part, k: xT[:, part, k, half * 512:(half + 1) * 512]).then_inc(q_mm, 1)

                def norm2_turn(b, t):
                    pe.wait_ge(nlo_done, tiled(b, t + 1))
                    pe.wait_ge(oT_ready, tiled(b, t + 1))
                    hl = xrow[:, t % 2, D:].bitcast(F16).rearrange("p (h n) -> p h n", h=2)
                    transposes(pe, turn16_ps, hl, KB).then_inc(nturn_done, 1)
                    pe.wait_ge(nT_ready, tiled(b, t + 1))
                    split_products(pe, gate_ps, lambda part, k: nT[:, part, k, :],
                                   lambda part, k: gate[:, part, k, :]).then_inc(gate_done, 1)

                pe.wait_ge(id_ready, 1)
                pe.wait_ge(consts_ready, 5)
                pe.wait_ge(kv_loaded, 48)
                for g in range(QUADS):
                    if g >= 2:
                        pe.wait_ge(k_read, g - 1)
                    for k in range(KB):
                        last = pe.matmul(psum[:, g % 2, 0:B * SK], wk_f[:, k, g * P:(g + 1) * P],
                                         ctx_f[:, k].rearrange("p b n -> p (b n)"), start=(k == 0), stop=(k == KB - 1))
                    last.then_inc(k_mm, 1)
                pe.wait_ge(ctx2_ready, 2)
                for b in range(B):
                    if b >= 2:
                        pe.wait_ge(v_read, b - 1)
                    for k in range(KB):
                        last = pe.matmul(psum[:, 2 + b % 2, :], ctx_2[:, k, b].rearrange("p d n -> p (d n)"),
                                         wv_f[:, k, :], start=(k == 0), stop=(k == KB - 1))
                    last.then_inc(v_mm, 1)
                for m in range(TB):
                    if m >= 1:
                        pe.wait_ge(xT_ready, m)
                    x_turn(m, lambda c, m=m: m + c)
                pe.wait_ge(w_split, 3)
                for q in range(KB + 1):
                    pe.wait_ge(xT_ready, 4 if q < KB else TB)
                    if q >= 1:
                        pe.wait_ge(q_ready, q)
                    project_q(q)
                pe.wait_ge(q_ready, KB)
                pe.wait_ge(kblk_ready, QUADS)
                pe.wait_ge(delta_ready, 1)
                pe.wait_ge(k_read, QUADS)
                scores(0, 0, 0, 0)
                pe.wait_ge(vblk_ready, B)

                def batch(b, last):
                    for t in range(TB):
                        c = t + 1
                        if not (last and c == TB):
                            pe.wait_ge(q_ready, tiled(b, 4 * (c // 4) + 4))
                            pe.wait_ge(pT_ready, tiled(b, t))
                            scores(c % 2, b + c // TB, (c % 4) * P, (c // 4) % 2)
                        pe.wait_ge(plo_done, tiled(b, t + 1))
                        transposes(pe, probT_ps[t % 2], phl[:, t % 2], PAIRS).then_inc(pturn_done, 1)
                        if t > 0:
                            norm2_turn(b, t - 1)
                        pe.wait_ge(pT_ready, tiled(b, t + 1))
                        pe.wait_ge(norm_done, tiled(b, t))
                        pe.wait_ge(logits_ready, tiled(b, t))
                        for r in range(PAIRS):
                            n = 0
                            for h, i in ((HI, 0), (HI, 1), (HI, 2), (LO, 0), (LO, 1), (LO, 2)):
                                mm = pe.matmul(att_ps[:, r, 0:VW], pT[:, h, r, :],
                                               vblk[:, i, bass.ds(b, 1), r, :].rearrange("p o n -> p (o n)"),
                                               start=(n == 0), stop=(n == 5))
                                n += 1
                        mm.then_inc(att_done, 1)
                        if not last:
                            pe.wait_ge(nT_ready, tiled(b, t))
                            x_turn(t, lambda c, t=t: tiled(b, TB + t + c))
                        q = t + KB + 1
                        pe.wait_ge(x1_done, tiled(b, t))
                        if not last or q < TB:
                            pe.wait_ge(xT_ready, tiled(b, 4 * (q // KB) + 4))
                            project_q(q)
                        pe.wait_ge(olo_done, tiled(b, t + 1))
                        pe.wait_ge(nT_ready, tiled(b, t))
                        if not last:
                            pe.wait_ge(xT_ready, tiled(b, TB + t + 1))
                        transposes(pe, turn16_ps, ohl, KB).then_inc(oturn_done, 1)
                        pe.wait_ge(oT_ready, tiled(b, t + 1))
                        if not last or q < TB:
                            pe.wait_ge(q_ready, tiled(b, q + 1))
                        split_products(pe, proj_ps, lambda part, k: oT[:, part, k, :],
                                       lambda part, k: wo[:, part, k, :]).then_inc(proj_done, 1)
                    norm2_turn(b, TB - 1)

                with pe.Fori(0, B - 1) as b:
                    batch(b, last=False)
                batch(B - 1, last=True)


        if stop_after == "attention":
            return

        consts2, iotas_ready, picked, prefix_done, softmax_sub, softmax_exp, routed = (
            sem("consts2"), sem("iotas_ready"), sem("picked"), sem("prefix_done"), sem("softmax_sub"),
            sem("softmax_exp"), sem("routed"))
        route_step, downb_loaded = sem("route_step"), sem("downb_loaded")
        U32 = mybir.dt.uint32
        iota_i = rt(1, SLOTS + TILES + E).rearrange("p a c -> p (a c)").bitcast(I32)
        iota_f = rt(1, SLOTS + TILES + E).rearrange("p a c -> p (a c)")
        slot_f, thresholds, ranks_f = (iota_f[:, 0:SLOTS], iota_f[:, SLOTS:SLOTS + TILES],
                                       iota_f[:, SLOTS + TILES:])
        before = rt(1, P, F16).rearrange("p a c -> p (a c)")
        ones_m = rt(1, P, F16).rearrange("p a c -> p (a c)")
        picks16 = rt(dt=F16)
        shifted, prob8, masked, scratch8 = rt(), rt(), rt(), rt()
        first, second, places_f = rt(), rt(), rt()
        sums = [rt(), rt()]
        totals = rt()
        top, w_first, w_second, best, found = rt(c=1), rt(c=1), rt(c=1), rt(c=1), rt(c=1)
        pos_f = rt(c=1)
        counts = rt(E, TILES)
        used, base = rt(E, 1), rt(E, 1)
        ends = [rt(E, 1), rt(E, 1)]
        slot_ge = rt(SLOTS, E)
        slot_sum = rt(SLOTS, 1)
        assert cuts["rt"] <= FFN0
        prefix_ps = psum[:, 6, 0:TILES * E].rearrange("p (t e) -> p t e", e=E)
        totals_ps = psum[:, 7, 0:TILES * E].rearrange("p (t e) -> p t e", e=E)

        XH = XROW

        def stage_sems(tag):
            names = ("turned", "eT_ready", "up_done", "biased", "silu_done", "hhi_done", "hidden_split",
                     "down_done", "bias_ready", "y_done")
            return [sem(f"{tag}_{n}") for n in names]

        def up_product(pe, dst, place, j):
            for m in range(KB):
                n = 0
                for k in range(KB):
                    for a, c in PRODUCTS:
                        w = weights[:, place, 0, a, k, m * P:(m + 1) * P] if isinstance(place, int) else \
                            weights[:, bass.ds(place, 1), 0, a, k, m * P:(m + 1) * P].rearrange("p o n -> p (o n)")
                        last = pe.matmul(dst[:, m * P:(m + 1) * P], w, eT[:, j, c, k, :],
                                         start=(n == 0), stop=(n == 3 * KB - 1))
                        n += 1
            return last

        def down_product(pe, dst, place, j):
            n = 0
            for k in range(KB):
                for a, c in PRODUCTS:
                    w = weights[:, place, 1, c, k, :] if isinstance(place, int) else \
                        weights[:, bass.ds(place, 1), 1, c, k, :].rearrange("p o n -> p (o n)")
                    last = pe.matmul(dst, hhl[:, j, a, k * P:(k + 1) * P], w, start=(n == 0), stop=(n == 3 * KB - 1))
                    n += 1
            return last

        def split_hidden(dve, j, silu_done, hhi_done, hidden_split, count):
            dve.wait_ge(silu_done, count)
            dve.tensor_copy(hhl[:, j, HI, :], hid).then_inc(hhi_done, 1)
            dve.wait_ge(hhi_done, count)
            dve.tensor_tensor(hhl[:, j, LO, :], hid, hhl[:, j, HI, :], ALU.subtract).then_inc(hidden_split, 1)

        TI = 6
        row_loaded = [sem(f"row_loaded{i}") for i in range(NROW)]
        scattered = [sem(f"scattered{i}") for i in range(NROW)]
        (turned, eT_ready, up_done, biased, silu_done, hhi_done, hidden_split, down_done, x1_biased,
         y_done) = stage_sems("shared")
        meta_copied = sem("meta_copied")
        y_stored = s2("y_stored")
        estage_loaded = s2("estage_loaded")
        est_scaled, est_split = sem("est_scaled"), sem("est_split")
        CHUNKS = [[0, 1], [2], [3], [4, 5], [6], [7], [], []]
        NLOOP2 = PLACES - EARLY - 1

        with nc.Block() as block:

            @block.sync
            def _(sp):
                for i in range(2):
                    sp.dma_start(rows[:, i, 0:XROW], xrows[i]).then_inc(row_loaded[i], 16)
                for j in range(2):
                    sp.dma_start(estage[:, j, :], ffn_w[EARLY, 0, j * P:(j + 1) * P, :]).then_inc(estage_loaded[j], 16)
                sp.dma_start(downb, down_b.rearrange("(o e) n -> o e n", o=1).to_broadcast([P, PLACES, D])
                             ).then_inc(downb_loaded, 16)

                def body(b, last):
                    for t in range(TI + 2 * last):
                        if t + 2 < TI + 2 or not last:
                            if not (last and t >= TI):
                                sp.wait_ge(y_done, b * TI + t)
                                settled(sp)
                                sp.wait_ge(scattered[(t + 2) % NROW], b * 64 + 32 * ((t + 2) // NROW))
                                sp.dma_start(rows[:, (t + 2) % NROW, 0:XROW],
                                             xrows[bass.ds(b * TI + t + 2, 1)].rearrange("o p n -> p (o n)")
                                             ).then_inc(row_loaded[(t + 2) % NROW], 16)
                        for j in CHUNKS[t]:
                            if not (last and j >= 6):
                                sp.wait_ge(est_split, b * 8 + j + 1)
                                c = (j + 2) % 8
                                sp.dma_start(estage[:, j % 2, :],
                                             ffn_w[bass.ds(b + EARLY + (j + 2) // 8, 1), c // KB,
                                                   (c % KB) * P:(c % KB + 1) * P, :].rearrange("o p n -> p (o n)")
                                             ).then_inc(estage_loaded[j % 2], 16)
                        sp.wait_ge(y_done, b * TI + t + 1)
                        sp.dma_start(out[bass.ds((b * TI + t) * P, P), :], yout[:, t % 2, :]
                                     ).then_inc(y_stored[t % 2], 16)

                with sp.Fori(0, NLOOP2) as b:
                    body(b, last=False)
                body(NLOOP2, last=True)
                for i in range(2):
                    sp.wait_ge(y_stored[i], 16 * TILES // 2)

            @block.scalar
            def _(act):
                def turned_out(i, count, up_count=None):
                    act.wait_ge(turned, count)
                    if up_count is not None:
                        act.wait_ge(up_done, up_count)
                    act.activation(eT[:, i % 2], eturn16_ps[i % 2], ACT.Copy).then_inc(eT_ready, 1)

                def silu(i, count, split_count=None):
                    act.wait_ge(biased, count)
                    if split_count is not None:
                        act.wait_ge(hidden_split, split_count)
                    act.activation(hid, pre[:, i % 2, :], ACT.Silu, scale=1.0 / WSCALE).then_inc(silu_done, 1)

                turned_out(0, 1)
                turned_out(1, 2)
                act.wait_ge(softmax_sub, 1)
                act.activation(shifted, shifted, ACT.Exp).then_inc(softmax_exp, 1)
                silu(0, 1)

                def body(b, last):
                    for t in range(TI + 2 * last):
                        if not (last and t >= TI):
                            turned_out(t, b * TI + t + 3, b * TI + t + 1)
                        if not (last and t == TI + 1):
                            silu(t + 1, b * TI + t + 2, b * TI + t + 1)
                        for j in CHUNKS[t]:
                            act.wait_ge(estage_loaded[j % 2], b * 64 + 16 * (j // 2 + 1))
                            w = weights[:, bass.ds(b + EARLY, 1), j // KB, HI, j % KB, :].rearrange("p o n -> p (o n)")
                            act.activation(w, estage[:, j % 2, :], ACT.Copy, scale=WSCALE)
                            act.activation(estage[:, j % 2, :], estage[:, j % 2, :], ACT.Copy,
                                           scale=WSCALE).then_inc(est_scaled, 1)

                with act.Fori(0, NLOOP2) as b:
                    body(b, last=False)
                body(NLOOP2, last=True)

            @block.gpsimd
            def _(pool):
                pool.iota(iota_i[:, 0:SLOTS], pattern=[[1, SLOTS]], base=0, channel_multiplier=0)
                pool.iota(iota_i[:, SLOTS:SLOTS + TILES], pattern=[[P, TILES]], base=0, channel_multiplier=0)
                pool.iota(iota_i[:, SLOTS + TILES:], pattern=[[-1, E]], base=E, channel_multiplier=0
                          ).then_inc(iotas_ready, 1)
                pool.iota(meta[:, :, 0].bitcast(I32), pattern=[[P, TILES]], base=0, channel_multiplier=1
                          ).then_inc(iotas_ready, 1)
                pool.memset(ones_m, 1.0)
                pool.memset(before, 1.0).then_inc(consts2, 1)
                pool.wait_ge(consts2, 1)
                pool.affine_select(out=before, in_=before, compare_op=ALU.is_gt, fill=0.0, base=0,
                                   pattern=[[1, P]], channel_multiplier=-1).then_inc(consts2, 1)
                pool.wait_ge(downb_loaded, 16)

                def body(b, last):
                    for t in range(TI + 2 * last):
                        i = t % NROW
                        pool.wait_ge(row_loaded[i], b * 32 + 16 * (t // NROW + 1))
                        pool.tensor_tensor(rows[:, i, 0:D], rows[:, i, 0:D], downb[:, 0, :], ALU.add
                                           ).then_inc(x1_biased, 1)
                        if t == 0:
                            pool.wait_ge(routed, 1)
                        pool.wait_ge(scattered[i], b * 64 + 32 * (t // NROW))
                        pool.tensor_copy(rows[:, i, XH:XH + META + 2].bitcast(I32),
                                         meta[:, bass.ds(b * TI + t, 1), :].rearrange("p o n -> p (o n)").bitcast(I32)
                                         ).then_inc(meta_copied, 1)
                        pool.wait_ge(meta_copied, b * TI + t + 1)
                        settled(pool)
                        for k in range(TOPK):
                            pool.indirect_dma_start(
                                out=sorted_rows[:, :],
                                out_offset=bass.IndirectOffsetOnAxis(
                                    ap=rows[:, i, XH + META + k:XH + META + k + 1].bitcast(U32), axis=0),
                                in_=rows[:, i, D:D + ROW], in_offset=None).then_inc(scattered[i], 16)
                        for j in CHUNKS[t]:
                            pool.wait_ge(est_scaled, b * 8 + j + 1)
                            w = [weights[:, bass.ds(b + EARLY, 1), j // KB, h, j % KB, :].rearrange("p o n -> p (o n)")
                                 for h in range(2)]
                            pool.tensor_tensor(w[LO], estage[:, j % 2, :], w[HI], ALU.subtract).then_inc(est_split, 1)

                with pool.Fori(0, NLOOP2) as b:
                    body(b, last=False)
                body(NLOOP2, last=True)
                for i in range(NROW):
                    pool.wait_ge(scattered[i], 32 * ((TILES - 1 - i) // NROW + 1))

            @block.vector
            def _(dve):
                def bias(i, count, silu_count=None):
                    dve.wait_ge(up_done, count)
                    if silu_count is not None:
                        dve.wait_ge(silu_done, silu_count)
                    dve.tensor_tensor(pre[:, i % 2, :].rearrange("p (m t) -> p m t", m=KB),
                                      up_ps[i % 2].rearrange("p (m t) -> p m t", m=KB),
                                      upb[:, 0:KB].unsqueeze(2).to_broadcast([P, KB, P]), ALU.add
                                      ).then_inc(biased, 1)

                steps = 0

                def step(instruction):
                    nonlocal steps
                    steps += 1
                    instruction.then_inc(route_step, 1)
                    dve.wait_ge(route_step, steps)

                def over_experts(v):
                    return v.unsqueeze(2).to_broadcast([P, TILES, E])

                ranks = ranks_f.unsqueeze(1).to_broadcast([P, TILES, E])
                dve.wait_ge(iotas_ready, 2)
                step(dve.tensor_copy(iota_f, iota_i))
                step(dve.memset(meta[:, :, 2 * E + 1:META], 0.0))
                step(dve.tensor_reduce(top, logits, AX.X, ALU.max))
                dve.tensor_tensor(shifted, logits, over_experts(top), ALU.subtract).then_inc(softmax_sub, 1)
                dve.wait_ge(softmax_exp, 1)
                step(dve.tensor_reduce(best, shifted, AX.X, ALU.add))
                step(dve.reciprocal(best, best))
                step(dve.tensor_tensor(prob8, shifted, over_experts(best), ALU.mult))

                def pick(scores, weight, one_hot):
                    step(dve.tensor_reduce(weight, scores, AX.X, ALU.max))
                    step(dve.tensor_tensor(scratch8, scores, over_experts(weight), ALU.is_equal))
                    step(dve.tensor_tensor(scratch8, scratch8, ranks, ALU.mult))
                    step(dve.tensor_reduce(found, scratch8, AX.X, ALU.max))
                    step(dve.tensor_tensor(one_hot, ranks, over_experts(found), ALU.is_equal))

                pick(prob8, w_first, first)
                step(dve.scalar_tensor_tensor(out=masked, in0=first, scalar=-2.0, in1=prob8,
                                              op0=ALU.mult, op1=ALU.add))
                pick(masked, w_second, second)
                dve.tensor_tensor(picks16, first, second, ALU.add).then_inc(picked, 1)
                step(dve.tensor_tensor(best, w_first, w_second, ALU.add))
                step(dve.tensor_scalar(best, best, 1e-20, None, ALU.add))
                step(dve.reciprocal(best, best))
                step(dve.tensor_tensor(w_first, w_first, best, ALU.mult))
                step(dve.tensor_tensor(w_second, w_second, best, ALU.mult))
                step(dve.tensor_tensor(scratch8, first, over_experts(w_first), ALU.mult))
                step(dve.tensor_tensor(masked, second, over_experts(w_second), ALU.mult))
                step(dve.tensor_tensor(meta[:, :, 1:E + 1], scratch8, masked, ALU.add))
                step(dve.tensor_scalar(meta[:, :, E + 1:2 * E + 1], meta[:, :, 1:E + 1], 1.0 / WSCALE, None, ALU.mult))
                dve.wait_ge(prefix_done, 1)
                step(dve.tensor_copy(totals, totals_ps))
                src = totals
                for n, shift in enumerate((1, 2, 4, 8, 16)):
                    dst = sums[n % 2]
                    step(dve.tensor_tensor(dst[:, shift:], src[:, shift:], src[:, :-shift], ALU.add))
                    step(dve.tensor_copy(dst[:, :shift], src[:, :shift]))
                    src = dst
                step(dve.tensor_tensor(counts, src[:, TILES - 1, :].unsqueeze(2).to_broadcast([P, E, TILES]),
                                       thresholds.unsqueeze(1).to_broadcast([P, E, TILES]), ALU.is_gt))
                step(dve.tensor_reduce(used, counts, AX.X, ALU.add))
                end = used
                for n, shift in enumerate((1, 2, 4)):
                    dst = ends[n % 2]
                    step(dve.tensor_tensor(dst[:, shift:], end[:, shift:], end[:, :-shift], ALU.add))
                    step(dve.tensor_copy(dst[:, :shift], end[:, :shift]))
                    end = dst
                step(dve.tensor_tensor(base, end, used, ALU.subtract))
                step(dve.tensor_scalar(base, base, float(P), None, ALU.mult))
                step(dve.tensor_tensor(places_f, src, totals, ALU.subtract))
                step(dve.tensor_tensor(places_f, prefix_ps, places_f, ALU.add))
                step(dve.tensor_tensor(places_f, places_f, base.unsqueeze(1).to_broadcast([P, TILES, E]), ALU.add))
                for k, one_hot in enumerate((first, second)):
                    step(dve.tensor_tensor(scratch8, places_f, one_hot, ALU.mult))
                    step(dve.tensor_reduce(pos_f, scratch8, AX.X, ALU.add))
                    step(dve.tensor_copy(meta[:, :, META + k].bitcast(I32), pos_f))
                step(dve.tensor_tensor(slot_ge, slot_f.unsqueeze(2).to_broadcast([P, SLOTS, E]),
                                       end.unsqueeze(1).to_broadcast([P, SLOTS, E]), ALU.is_ge))
                step(dve.tensor_reduce(slot_sum, slot_ge, AX.X, ALU.add))
                dve.tensor_scalar(slot_place, slot_sum, 1.0, float(E), ALU.add, ALU.min).then_inc(routed, 1)
                bias(0, 1)
                split_hidden(dve, 0, silu_done, hhi_done, hidden_split, 1)

                def body(b, last):
                    for t in range(TI + 2 * last):
                        n = b * TI + t
                        if not (last and t == TI + 1):
                            bias(t + 1, n + 2, n)
                            dve.wait_ge(down_done, n)
                            split_hidden(dve, (t + 1) % 2, silu_done, hhi_done, hidden_split, n + 2)
                        dve.wait_ge(down_done, n + 1)
                        dve.wait_ge(x1_biased, n + 1)
                        dve.wait_ge(y_stored[t % 2], b * 48 + 16 * (t // 2))
                        dve.scalar_tensor_tensor(out=yout[:, t % 2, :], in0=down_ps[t % 2], scalar=1.0 / WSCALE,
                                                 in1=rows[:, t % NROW, 0:D], op0=ALU.mult, op1=ALU.add
                                                 ).then_inc(y_done, 1)

                with dve.Fori(0, NLOOP2) as b:
                    body(b, last=False)
                body(NLOOP2, last=True)

            @block.tensor
            def _(pe):
                def turn(i, loaded):
                    pe.wait_ge(row_loaded[i % NROW], loaded)
                    transposes(pe, eturn16_ps[i % 2], row_hl[i % NROW], KB).then_inc(turned, 1)

                turn(0, 16)
                turn(1, 16)
                pe.wait_ge(eT_ready, 1)
                up_product(pe, up_ps[0], 0, 0).then_inc(up_done, 1)
                pe.wait_ge(picked, 1)
                pe.wait_ge(consts2, 2)
                flat = picks16.rearrange("p t e -> p (t e)")
                pe.matmul(psum[:, 6, 0:TILES * E], before, flat, start=True, stop=True)
                pe.matmul(psum[:, 7, 0:TILES * E], ones_m, flat, start=True, stop=True).then_inc(prefix_done, 1)

                def body(b, last):
                    for t in range(TI + 2 * last):
                        n = b * TI + t
                        if not (last and t >= TI):
                            pe.wait_ge(eT_ready, n + 1)
                            turn(t + 2, b * 32 + 16 * ((t + 2) // NROW + 1))
                        if not (last and t == TI + 1):
                            pe.wait_ge(eT_ready, n + 2)
                            pe.wait_ge(biased, n)
                            up_product(pe, up_ps[(t + 1) % 2], 0, (t + 1) % 2).then_inc(up_done, 1)
                        pe.wait_ge(hidden_split, n + 1)
                        pe.wait_ge(y_done, n)
                        down_product(pe, down_ps[t % 2], 0, t % 2).then_inc(down_done, 1)

                with pe.Fori(0, NLOOP2) as b:
                    body(b, last=False)
                body(NLOOP2, last=True)

        if stop_after == "shared":
            return

        slot_loaded = [sem(f"slot_loaded{i}") for i in range(NROW)]
        (turned, eT_ready, up_done, biased, silu_done, hhi_done, hidden_split, down_done, bias_weighted,
         y_done) = stage_sems("slot")
        added = s2("added")
        BODIES = SLOTS // TI
        assert BODIES * TI == SLOTS

        with nc.Block() as block:

            def place_of(eng, n):
                return eng.value_load(slot_place[0:1, bass.ds(n, 1)], min_val=1, max_val=E)

            @block.sync
            def _(sp):
                for i in range(2):
                    sp.dma_start(rows[:, i, D:D + ROW], sorted_rows[i * P:(i + 1) * P, :]).then_inc(slot_loaded[i], 16)

                def body(b, last):
                    for t in range(TI):
                        n = b * TI + t
                        if not (last and t >= TI - 2):
                            sp.wait_ge(y_done, n)
                            settled(sp)
                            sp.wait_ge(added[(t + 1) % 2], b * 48 + 16 * ((t + 1) // 2))
                            sp.dma_start(rows[:, (t + 2) % NROW, D:D + ROW],
                                         sorted_rows[bass.ds((n + 2) * P, P), :]).then_inc(slot_loaded[(t + 2) % NROW], 16)

                with sp.Fori(0, BODIES - 1) as b:
                    body(b, last=False)
                body(BODIES - 1, last=True)

            @block.scalar
            def _(act):
                def turned_out(i, count, up_count=None):
                    act.wait_ge(turned, count)
                    if up_count is not None:
                        act.wait_ge(up_done, up_count)
                    act.activation(eT[:, i % 2], eturn16_ps[i % 2], ACT.Copy).then_inc(eT_ready, 1)

                def silu(i, count, split_count=None):
                    act.wait_ge(biased, count)
                    if split_count is not None:
                        act.wait_ge(hidden_split, split_count)
                    act.activation(hid, pre[:, i % 2, :], ACT.Silu, scale=1.0 / WSCALE).then_inc(silu_done, 1)

                turned_out(0, 1)
                turned_out(1, 2)
                silu(0, 1)

                def body(b, last):
                    for t in range(TI):
                        n = b * TI + t
                        if not (last and t >= TI - 2):
                            turned_out(t, n + 3, n + 1)
                        if not (last and t == TI - 1):
                            silu(t + 1, n + 2, n + 1)
                        place = place_of(act, n)
                        act.wait_ge(slot_loaded[t % NROW], b * 32 + 16 * (t // NROW + 1))
                        act.wait_ge(y_done, n)
                        act.activation(wbias, downb[:, bass.ds(place, 1), :].rearrange("p o n -> p (o n)"), ACT.Copy,
                                       scale=rows[:, t % NROW, bass.ds(XH + place, 1)]).then_inc(bias_weighted, 1)

                with act.Fori(0, BODIES - 1) as b:
                    body(b, last=False)
                body(BODIES - 1, last=True)

            @block.gpsimd
            def _(pool):
                def body(b, last):
                    for t in range(TI):
                        pool.wait_ge(y_done, b * TI + t + 1)
                        pool.wait_ge(added[(t + 1) % 2], b * 48 + 16 * ((t + 1) // 2))
                        settled(pool)
                        pool.indirect_dma_start(
                            out=out[:, :],
                            out_offset=bass.IndirectOffsetOnAxis(
                                ap=rows[:, t % NROW, XH:XH + 1].bitcast(U32), axis=0),
                            in_=yout[:, t % 2, :], in_offset=None, compute_op=ALU.add).then_inc(added[t % 2], 16)

                with pool.Fori(0, BODIES - 1) as b:
                    body(b, last=False)
                body(BODIES - 1, last=True)
                for i in range(2):
                    pool.wait_ge(added[i], 16 * SLOTS // 2)

            @block.vector
            def _(dve):
                def bias(i, n, count, silu_count=None):
                    place = place_of(dve, n)
                    dve.wait_ge(up_done, count)
                    if silu_count is not None:
                        dve.wait_ge(silu_done, silu_count)
                    dve.tensor_tensor(pre[:, i % 2, :].rearrange("p (m t) -> p m t", m=KB),
                                      up_ps[i % 2].rearrange("p (m t) -> p m t", m=KB),
                                      upb[:, bass.ds(place * KB, KB)].unsqueeze(2).to_broadcast([P, KB, P]), ALU.add
                                      ).then_inc(biased, 1)

                bias(0, 0, 1)
                split_hidden(dve, 0, silu_done, hhi_done, hidden_split, 1)

                def body(b, last):
                    for t in range(TI):
                        n = b * TI + t
                        if not (last and t == TI - 1):
                            bias(t + 1, n + 1, n + 2, n)
                            dve.wait_ge(down_done, n)
                            split_hidden(dve, (t + 1) % 2, silu_done, hhi_done, hidden_split, n + 2)
                        place = place_of(dve, n)
                        dve.wait_ge(down_done, n + 1)
                        dve.wait_ge(bias_weighted, n + 1)
                        dve.wait_ge(added[t % 2], b * 48 + 16 * (t // 2))
                        dve.scalar_tensor_tensor(out=yout[:, t % 2, :], in0=down_ps[t % 2],
                                                 scalar=rows[:, t % NROW, bass.ds(XH + E + place, 1)],
                                                 in1=wbias, op0=ALU.mult, op1=ALU.add).then_inc(y_done, 1)

                with dve.Fori(0, BODIES - 1) as b:
                    body(b, last=False)
                body(BODIES - 1, last=True)

            @block.tensor
            def _(pe):
                def turn(i, loaded):
                    pe.wait_ge(slot_loaded[i % NROW], loaded)
                    transposes(pe, eturn16_ps[i % 2], row_hl[i % NROW], KB).then_inc(turned, 1)

                turn(0, 16)
                turn(1, 16)
                pe.wait_ge(eT_ready, 1)
                up_product(pe, up_ps[0], place_of(pe, 0), 0).then_inc(up_done, 1)

                def body(b, last):
                    for t in range(TI):
                        n = b * TI + t
                        if not (last and t >= TI - 2):
                            pe.wait_ge(eT_ready, n + 1)
                            turn(t + 2, b * 32 + 16 * ((t + 2) // NROW + 1))
                        if not (last and t == TI - 1):
                            place = place_of(pe, n + 1)
                            pe.wait_ge(eT_ready, n + 2)
                            pe.wait_ge(biased, n)
                            up_product(pe, up_ps[(t + 1) % 2], place, (t + 1) % 2).then_inc(up_done, 1)
                        place = place_of(pe, n)
                        pe.wait_ge(hidden_split, n + 1)
                        pe.wait_ge(y_done, n)
                        down_product(pe, down_ps[t % 2], place, t % 2).then_inc(down_done, 1)

                with pe.Fori(0, BODIES - 1) as b:
                    body(b, last=False)
                body(BODIES - 1, last=True)


INPUTS = ("x", "ctxT", "tau", "delta", "wqT", "wkT", "wvT", "woT", "bq", "bk", "bv", "bo",
          "gateT", "ffn_w", "up_b", "down_b")


def layout(i):
    a = {k: np.asarray(v) for k, v in i.items()}
    ffn_w = np.empty((PLACES, 2, D, D), np.float32)
    ffn_w[0, 0], ffn_w[0, 1] = a["L0_ffn_sh_up_w"], a["L0_ffn_sh_down_w"]
    ffn_w[1:, 0], ffn_w[1:, 1] = a["L0_ffn_up_w"], a["L0_ffn_down_w"]
    t = np.ascontiguousarray

    def columns(bias):
        return t(bias.reshape(-1, P).T)

    return {
        "x": a["x"].reshape(TILES, P, D),
        "ctxT": t(a["ctx_1024"].reshape(B * SK, D).T),
        "tau": a["condB_tau"],
        "delta": a["fside_BxS2_0"].reshape(B * SK),
        "wqT": t(a["L0_xcond_Wq"].T), "wkT": t(a["L0_xcond_Wk"].T),
        "wvT": t(a["L0_xcond_Wv"].T), "woT": t(a["L0_xcond_Wo"].T),
        "bq": columns(a["L0_xcond_bq"]), "bk": columns(a["L0_xcond_bk"]),
        "bv": a["L0_xcond_bv"], "bo": a["L0_xcond_bo"],
        "gateT": t(a["L0_ffn_gate_w"].T),
        "ffn_w": ffn_w,
        "up_b": columns(np.concatenate([a["L0_ffn_sh_up_b"][None], a["L0_ffn_up_b"]])),
        "down_b": np.concatenate([a["L0_ffn_sh_down_b"][None], a["L0_ffn_down_b"]]),
    }


def kernel(**inputs):
    import concourse.bacc as bacc
    from concourse.bass_utils import run_bass_kernel_spmd

    nc = bacc.Bacc("TRN2", target_bir_lowering=False, num_devices=1)
    arrays = {f"in_{k}": v for k, v in layout(inputs).items()}
    args = [nc.dram_tensor(f"in_{k}", arrays[f"in_{k}"].shape, F32, kind="ExternalInput").ap() for k in INPUTS]
    out = nc.dram_tensor("out", (TOKENS + P, D), F32, kind="ExternalOutput").ap()
    build_program(nc, *args, out)
    r = run_bass_kernel_spmd(nc, [arrays], core_ids=[0])
    return r.results[0]["out"][:TOKENS].reshape(B, S, D)
```

```python
from contextlib import ExitStack

import numpy as np

import concourse.bass as bass
from concourse import mybir

F32 = mybir.dt.float32
F16 = mybir.dt.float16
BF16 = mybir.dt.bfloat16
I32 = mybir.dt.int32
ALU = mybir.AluOpType
ACT = mybir.ActivationFunctionType
AX = mybir.AxisListType

P = 128
B, S, D, H, SK = 4, 1024, 512, 16, 64
DK = D // H
KB = D // P
TOKENS = B * S
TILES = TOKENS // P
TB = S // P
PAIRS = H // 2
QUADS = H // 4
VW = 2 * DK + 2
E = 8
PLACES = E + 1
TOPK = 2
SLOTS = (TOKENS * TOPK + E * (P - 1)) // P
PADS = SLOTS - TOKENS * TOPK // P
WSCALE = 16.0
EPS = 1e-5
EARLY = 4
META = 24
ROW = D + META
XROW = 2 * D
HI, LO = 0, 1
PRODUCTS = ((HI, HI), (HI, LO), (LO, HI))


def build_program(nc, x, ctxT, tau, delta, wqT, wkT, wvT, woT, bq, bk, bv, bo,
                  gateT, ffn_w, up_b, down_b, out, stop_after=None):
    ctx = ExitStack()
    with ctx:
        def sb(name, shape, dt=F32):
            return ctx.enter_context(nc.sbuf_tensor(name, shape, dt))

        def sem(name):
            return ctx.enter_context(nc.semaphore(name))

        xrows = nc.dram_tensor("xrows", [TILES, P, XROW], F32).ap()
        sorted_rows = nc.dram_tensor("sorted_rows", [SLOTS * P, ROW], F32).ap()

        PLACE_W = 4 * KB * D // 2
        ATT0 = EARLY * PLACE_W
        FFN0 = PLACES * PLACE_W
        ARENA = 51620
        arena = sb("arena", [P, ARENA])
        small = sb("small", [P, 1300])
        cuts = {"small": 0}

        def cut(tensor, key, words, dt=F32):
            a = cuts[key]
            cuts[key] = a + words
            v = tensor[:, a:a + words]
            return v if dt == F32 else v.bitcast(dt)

        def keep(words, dt=F32):
            return cut(small, "small", words, dt)

        weights = arena[:, 0:FFN0].bitcast(F16).rearrange(
            "p (e m h k n) -> p e m h k n", e=PLACES, m=2, h=2, k=KB)
        ident = keep(P // 2, F16)
        upb = keep(PLACES * KB)
        zero_row = keep(ROW)
        logits = keep(TILES * E).rearrange("p (t e) -> p t e", e=E)
        slot_place = keep(SLOTS, I32)
        pad_pos = keep(PADS, I32)
        gate = keep(2 * KB * E // 2, F16).rearrange("p (h k e) -> p h k e", h=2, k=KB)
        tau_k = keep(B)
        bq_c = keep(KB)
        bk_c = keep(KB)
        upb_raw = keep(PLACES * KB)
        stat1 = keep(2 * 6).rearrange("p (i c) -> p i c", i=2)
        mv1 = keep(2 * 2).rearrange("p (i c) -> p i c", i=2)
        rstd1 = keep(2)
        root1 = keep(2 * 2).rearrange("p (i c) -> p i c", i=2)
        root2 = keep(2).rearrange("p (i c) -> p i c", i=1)
        eps_c = keep(1)
        stat2 = keep(6)
        mv2 = keep(2)
        rstd2 = keep(1)
        rowmax = keep(2 * H).rearrange("p (i h) -> p i h", i=2)
        rden = keep(H)
        ones3 = keep(P // 2, BF16)[0:3, :]

        cuts["att"] = ATT0

        def att(words, dt=F32):
            return cut(arena, "att", words, dt)

        wq = att(KB * D, F16).rearrange("p (h k n) -> p h k n", h=2, k=KB)
        wo = att(KB * D, F16).rearrange("p (h k n) -> p h k n", h=2, k=KB)
        kblk = att(B * QUADS * 4 * SK).rearrange("p (b g n) -> p b g n", b=B, g=QUADS)
        vblk = att(B * PAIRS * VW, F16).rearrange("p (h b r n) -> p h b r n", h=2, b=B, r=PAIRS)
        delta3 = att(B * SK // 2, BF16)[0:3, :].rearrange("p (b n) -> p b n", b=B)
        bo_b = att(D)
        xT = att(2 * KB * S // 2, F16).rearrange("p (h k t) -> p h k t", h=2, k=KB)
        qT = att(2 * KB * 4 * P).rearrange("p (i k t) -> p i k t", i=2, k=KB)
        xin = att(2 * D).rearrange("p (i n) -> p i n", i=2)
        xn1 = att(2 * D).rearrange("p (i n) -> p i n", i=2)
        xhl = att(2 * D, F16).rearrange("p (i h n) -> p i h n", i=2, h=2)
        x_first = arena[:, cuts["att"]:cuts["att"] + TB * D].rearrange("p (t n) -> p t n", t=TB)
        prob = att(2 * H * SK).rearrange("p (i n) -> p i n", i=2)
        phl = att(2 * H * SK, F16).rearrange("p (i h n) -> p i h n", i=2, h=2)
        assert TB * D <= 4 * H * SK
        pT = att(H * SK, F16).rearrange("p (h r t) -> p h r t", h=2, r=PAIRS)
        xres = att(2 * D).rearrange("p (i n) -> p i n", i=2)
        att_o = att(D)
        ohl = att(D, F16).rearrange("p (h n) -> p h n", h=2)
        oT = att(D, F16).rearrange("p (h k t) -> p h k t", h=2, k=KB)
        xrow = att(2 * XROW).rearrange("p (i n) -> p i n", i=2)
        xn2 = att(D)
        nT = att(D, F16).rearrange("p (h k t) -> p h k t", h=2, k=KB)
        wstage = att(2 * D).rearrange("p (i n) -> p i n", i=2)
        assert cuts["att"] <= ARENA, cuts["att"]

        cuts["pro"] = 0

        def pro(words, dt=F32):
            return cut(arena, "pro", words, dt)

        wk_f = pro(KB * D).rearrange("p (k n) -> p k n", k=KB)
        wv_f = pro(KB * D).rearrange("p (k n) -> p k n", k=KB)
        wq_f = pro(KB * D).rearrange("p (k n) -> p k n", k=KB)
        wo_f = pro(KB * D).rearrange("p (k n) -> p k n", k=KB)
        gate_f = pro(KB * E).rearrange("p (k e) -> p k e", k=KB)
        ctx_f = pro(KB * B * SK).rearrange("p (k b n) -> p k b n", k=KB, b=B)
        ctx_2 = pro(KB * B * 2 * SK).rearrange("p (k b d n) -> p k b d n", k=KB, b=B, d=2)
        k_f = pro(KB * B * SK).rearrange("p (k b n) -> p k b n", k=KB, b=B)
        v_f = pro(B * D).rearrange("p (b r n) -> p b r n", b=B, r=PAIRS)
        bv_b = pro(D)
        tau_b = pro(B)
        delta_f = pro(B * SK)
        delta_p = pro(B * SK // 2, BF16)
        delta_s = pro(B * SK)
        HALF = TB // 2
        FIRST = TB + 1
        stat0 = pro(FIRST * 6).rearrange("p (t c) -> p t c", t=FIRST)
        mv0 = pro(FIRST * 2).rearrange("p (t c) -> p t c", t=FIRST)
        root0 = pro(3 * FIRST).rearrange("p (c t) -> p c t", c=3)
        assert cuts["pro"] <= ATT0

        cuts["ffn"] = FFN0

        def ffn(words, dt=F32):
            return cut(arena, "ffn", words, dt)

        downb = ffn(PLACES * D).rearrange("p (e n) -> p e n", e=PLACES)
        NROW = 3
        RBUF = ROW + TOPK
        NSLOT = 6
        slots0 = cuts["ffn"]
        rows = ffn(NROW * RBUF).rearrange("p (i n) -> p i n", i=NROW)
        x1_rows = ffn(NROW * D).rearrange("p (i n) -> p i n", i=NROW)
        estage = ffn(2 * D).rearrange("p (i n) -> p i n", i=2)
        slots = arena[:, slots0:slots0 + NSLOT * ROW].rearrange("p (i n) -> p i n", i=NSLOT)
        assert slots0 + NSLOT * ROW <= cuts["ffn"]
        eT = ffn(2 * D, F16).rearrange("p (i h k t) -> p i h k t", i=2, h=2, k=KB)
        pre = ffn(2 * D).rearrange("p (i n) -> p i n", i=2)
        hid = ffn(D)
        hhl = ffn(2 * D, F16).rearrange("p (i h n) -> p i h n", i=2, h=2)
        wbias = ffn(D)
        yout = ffn(2 * D).rearrange("p (i n) -> p i n", i=2)
        meta = ffn(TILES * (META + 2)).rearrange("p (t n) -> p t n", t=TILES)
        cuts["rt"] = (PLACES - 2) * PLACE_W

        def rt(a=TILES, c=E, dt=F32):
            v = cut(arena, "rt", a * c // (2 if dt == F16 else 1), dt)
            return v.rearrange("p (a c) -> p a c", a=a) if c > 1 else v

        assert cuts["ffn"] <= ARENA, cuts["ffn"]

        def parts(row):
            return row[:, 0:D].bitcast(F16).rearrange("p (h n) -> p h n", h=2)

        psum = ctx.enter_context(nc.psum_tensor("psum", [P, 8, 512], F32))
        scores_ps = psum[:, 0:2, :].rearrange("p a n -> p (a n)")
        probT_ps = psum[:, 2:4, :].rearrange("p a n -> p (a n)").bitcast(F16).rearrange(
            "p (h r t) -> p h r t", h=2, r=PAIRS)
        att_ps = psum[:, 4:6, :].rearrange("p a n -> p (a n)").rearrange("p (r n) -> p r n", r=PAIRS)
        gate_ps = psum[:, 4, VW:VW + E]
        turn_ps = psum[:, 6, :]
        turn16_ps = turn_ps.bitcast(F16).rearrange("p (h k t) -> p h k t", h=2, k=KB)
        proj_ps = psum[:, 7, :]
        eturn16_ps = [psum[:, 0 + i, :].bitcast(F16).rearrange("p (h k t) -> p h k t", h=2, k=KB) for i in range(2)]
        up_ps = [psum[:, 2 + i, :] for i in range(2)]
        down_ps = [psum[:, 4 + i, :] for i in range(2)]

        def s2(name):
            return [sem(f"{name}0"), sem(f"{name}1")]

        id0, id_ready, consts_ready = sem("id0"), sem("id_ready"), sem("consts_ready")
        v_loaded, wo_split = sem("v_loaded"), sem("wo_split")
        kv_loaded, q_loaded, misc_loaded, small_loaded, o_loaded = (
            sem("kv_loaded"), sem("q_loaded"), sem("misc_loaded"), sem("small_loaded"), sem("o_loaded"))
        ctx2_ready, k_mm, k_read, kblk_ready, v_mm, v_read = (
            sem("ctx2_ready"), sem("k_mm"), sem("k_read"), sem("kblk_ready"), sem("v_mm"), sem("v_read"))
        vblk_ready, pro_dve, w_scaled, w_hi_ready, w_split, tau_ready, delta_ready, cleared = (
            sem("vblk_ready"), sem("pro_dve"), sem("w_scaled"), sem("w_hi_ready"), sem("w_split"),
            sem("tau_ready"), sem("delta_ready"), sem("cleared"))
        first_loaded = s2("first_loaded")
        first_stats, first_mv, first_log, first_guess, first_steps, first_rstd = (
            sem("first_stats"), sem("first_mv"), sem("first_log"), sem("first_guess"), sem("first_steps"),
            sem("first_rstd"))
        trash_zeroed = sem("trash_zeroed")
        xin_loaded = s2("xin_loaded")
        ln1_stats, ln1_mv, ln1_rstd, ln1_done = sem("ln1_stats"), sem("ln1_mv"), sem("ln1_rstd"), sem("ln1_done")
        ln1_guess, ln1_steps, ln2_guess, ln2_steps, ln1_log, ln2_log = (
            sem("ln1_guess"), sem("ln1_steps"), sem("ln2_guess"), sem("ln2_steps"), sem("ln1_log"), sem("ln2_log"))
        xhi_done, xlo_done, xturn_done, xT_ready = sem("xhi_done"), sem("xlo_done"), sem("xturn_done"), sem("xT_ready")
        q_mm, q_ready = sem("q_mm"), sem("q_ready")
        scores_done, max_done, sub_done, exp_done, plo_done = (
            sem("scores_done"), sem("max_done"), sem("sub_done"), sem("exp_done"), sem("plo_done"))
        pturn_done, pT_ready, att_done, rden_done, norm_done = (
            sem("pturn_done"), sem("pT_ready"), sem("att_done"), sem("rden_done"), sem("norm_done"))
        ohi_done, olo_done, oturn_done, oT_ready, proj_done = (
            sem("ohi_done"), sem("olo_done"), sem("oturn_done"), sem("oT_ready"), sem("proj_done"))
        xres_loaded = s2("xres_loaded")
        xres_biased, x1_done, ln2_stats, ln2_mv, ln2_rstd, ln2_done = (
            sem("xres_biased"), sem("x1_done"), sem("ln2_stats"), sem("ln2_mv"), sem("ln2_rstd"), sem("ln2_done"))
        nhi_done, nlo_done, nturn_done, nT_ready, gate_done, logits_ready = (
            sem("nhi_done"), sem("nlo_done"), sem("nturn_done"), sem("nT_ready"), sem("gate_done"), sem("logits_ready"))
        xrow_stored = s2("xrow_stored")
        wstage_loaded = s2("wstage_loaded")
        wst_hi, wst_split = sem("wst_hi"), sem("wst_split")

        passed = sem("passed")

        def settled(eng):
            eng.sem_inc(passed, 1)

        def tiled(b, c):
            return b * TB + c

        def bodies(eng, n, body):
            body(0, False)
            with eng.Fori(1, n - 1) as b:
                body(b, False)
            body(n - 1, True)

        def batches(eng, batch):
            batch(0, True, False)
            with eng.Fori(1, B - 1) as b:
                batch(b, False, False)
            batch(B - 1, False, True)

        def there(first, last, t):
            return not (first and t < 0) and not (last and t >= TB)

        def transposes(eng, dst, src_hi_lo, n):
            for h in range(2):
                for k in range(n):
                    last = eng.transpose(dst[:, h, k, :], src_hi_lo[:, h, k * P:(k + 1) * P], ident)
            return last

        def split_products(eng, dst, lhs, rhs):
            n = 0
            for k in range(KB):
                for a, c in PRODUCTS:
                    last = eng.matmul(dst, lhs(a, k), rhs(c, k), start=(n == 0), stop=(n == 3 * KB - 1))
                    n += 1
            return last

        def bcast_rows(ap, n):
            return ap.rearrange("(o n) -> o n", o=1).to_broadcast([n, ap.shape[0]])

        with nc.Block() as block:

            @block.sync
            def _(sp):
                sp.dma_start(x_first[:, 0:HALF, :], x[0:HALF].rearrange("t p n -> p t n")).then_inc(first_loaded[0], 16)
                sp.dma_start(ctx_f, ctxT.rearrange("(k p) (b n) -> p k b n", p=P, b=B)).then_inc(kv_loaded, 16)
                sp.dma_start(wk_f, wkT.rearrange("(k p) n -> p k n", p=P)).then_inc(kv_loaded, 16)
                sp.dma_start(x_first[:, HALF:, :], x[HALF:TB].rearrange("t p n -> p t n")).then_inc(first_loaded[1], 16)
                sp.dma_start(xin[:, 0, :], x[TB]).then_inc(xin_loaded[0], 16)
                sp.dma_start(wv_f, wvT.rearrange("(k p) n -> p k n", p=P)).then_inc(v_loaded, 16)
                sp.dma_start(wq_f, wqT.rearrange("(k p) n -> p k n", p=P)).then_inc(q_loaded, 16)
                sp.dma_start(wo_f, woT.rearrange("(k p) n -> p k n", p=P)).then_inc(o_loaded, 16)
                sp.dma_start(xin[:, 1, :], x[TB + 1]).then_inc(xin_loaded[1], 16)
                sp.dma_start(xres[:, 0, :], x[0]).then_inc(xres_loaded[0], 16)
                sp.dma_start(wstage[:, 0, :], ffn_w[0, 0, 0:P, :]).then_inc(wstage_loaded[0], 16)

                def load_x(b, c):
                    sp.wait_ge(ln1_done, tiled(b, c - 1))
                    tile = tiled(b, c)
                    if c == 2 * TB:
                        tile = (b + 2) % B * TB
                    sp.dma_start(xin[:, c % 2, :], x[bass.ds(tile, 1)].rearrange("o p n -> p (o n)")
                                 ).then_inc(xin_loaded[c % 2], 16)

                def batch(b, first, last):
                    if not first and not last:
                        load_x(b, TB + 1)
                    for t in range(TB + last):
                        if there(first, last, t + 1):
                            sp.wait_ge(x1_done, tiled(b, t))
                            sp.dma_start(xres[:, (t + 1) % 2, :],
                                         x[bass.ds(tiled(b, t + 1), 1)].rearrange("o p n -> p (o n)")
                                         ).then_inc(xres_loaded[(t + 1) % 2], 16)
                            sp.wait_ge(wst_split, tiled(b, t))
                            c = (t + 1) % TB
                            sp.dma_start(wstage[:, (t + 1) % 2, :],
                                         ffn_w[bass.ds(b + (t + 1) // TB, 1), c // KB,
                                               (c % KB) * P:(c % KB + 1) * P, :].rearrange("o p n -> p (o n)")
                                         ).then_inc(wstage_loaded[(t + 1) % 2], 16)
                        if not last and t + 2 <= TB:
                            load_x(b, TB + t + 2)
                        if there(first, last, t - 1):
                            sp.wait_ge(nlo_done, tiled(b, t))
                            sp.dma_start(xrows[bass.ds(tiled(b, t - 1), 1)].rearrange("o p n -> p (o n)"),
                                         xrow[:, (t - 1) % 2, :]).then_inc(xrow_stored[(t - 1) % 2], 16)

                batches(sp, batch)
                sp.wait_ge(xrow_stored[0], 16 * TILES // 2)
                sp.wait_ge(xrow_stored[1], 16 * TILES // 2)
                sp.wait_ge(trash_zeroed, 16)

            @block.scalar
            def _(act):
                def guess(i, count, mv, root, mv_done, log_done, done):
                    act.wait_ge(mv_done, count)
                    y = root[:, i, 0:1]
                    act.activation(y, mv, ACT.Ln, bias=eps_c).then_inc(log_done, 1)
                    act.wait_ge(log_done, count)
                    act.activation(y, y, ACT.Exp, scale=-0.5).then_inc(done, 1)

                def guess_1(i, count):
                    guess(i, count, mv1[:, i, 1:2], root1, ln1_mv, ln1_log, ln1_guess)

                def guess_2(count):
                    guess(0, count, mv2[:, 1:2], root2, ln2_mv, ln2_log, ln2_guess)

                act.preload_act_table_set("natural_log_exp_and_others")
                act.dma_start(tau_b, bcast_rows(tau, P)).then_inc(small_loaded, 16)
                act.dma_start(delta_f[0:3, :], bcast_rows(delta, 3)).then_inc(small_loaded, 16)
                act.dma_start(bq_c, bq).then_inc(small_loaded, 16)
                act.dma_start(bk_c, bk).then_inc(small_loaded, 16)
                act.dma_start(upb_raw, up_b).then_inc(small_loaded, 16)
                act.dma_start(gate_f, gateT.rearrange("(k p) e -> p k e", p=P)).then_inc(small_loaded, 16)
                act.dma_start(bv_b, bcast_rows(bv, P)).then_inc(small_loaded, 16)
                act.dma_start(bo_b, bcast_rows(bo, P)).then_inc(small_loaded, 16)
                act.wait_ge(consts_ready, 5)
                act.dma_start(out[TOKENS:TOKENS + P, :], zero_row[:, 0:D]).then_inc(trash_zeroed, 16)

                act.wait_ge(first_mv, FIRST)
                act.wait_ge(consts_ready, 5)
                act.activation(root0[:, 0, :], mv0[:, :, 1], ACT.Ln, bias=eps_c).then_inc(first_log, 1)
                act.wait_ge(first_log, 1)
                act.activation(root0[:, 0, :], root0[:, 0, :], ACT.Exp, scale=-0.5).then_inc(first_guess, 1)

                def x_hi(m, count):
                    act.wait_ge(ln1_done, count(1))
                    if m >= 2:
                        act.wait_ge(xturn_done, count(-1))
                    src = x_first[:, m, :] if m < TB else xn1[:, m % 2, :]
                    act.activation(xhl[:, m % 2, HI, :], src, ACT.Copy).then_inc(xhi_done, 1)

                def x_turned(m, count, q_count=None):
                    act.wait_ge(xturn_done, count(1))
                    if q_count is not None:
                        act.wait_ge(q_mm, q_count)
                    c = m % TB
                    act.activation(xT[:, :, :, c * P:(c + 1) * P], turn16_ps, ACT.Copy).then_inc(xT_ready, 1)

                def q_out(q, count, s_count=None):
                    act.wait_ge(q_mm, count)
                    if s_count is not None:
                        act.wait_ge(scores_done, s_count)
                    act.activation(qT[:, (q // KB) % 2, q % KB, :], proj_ps, ACT.Identity,
                                   bias=bq_c[:, q % KB:q % KB + 1], scale=1.0 / WSCALE).then_inc(q_ready, 1)

                def exps(i, count, pt_count=None):
                    act.wait_ge(sub_done, count)
                    if pt_count is not None:
                        act.wait_ge(pturn_done, pt_count)
                    act.activation(phl[:, i, HI, :], prob[:, i, :], ACT.Exp)
                    act.activation(prob[:, i, :], prob[:, i, :], ACT.Exp).then_inc(exp_done, 1)

                def k_out(g):
                    act.wait_ge(k_mm, g + 1)
                    act.activation(k_f[:, g], psum[:, g % 2, 0:B * SK].rearrange("p (b n) -> p b n", b=B),
                                   ACT.Identity, bias=bk_c[:, g:g + 1]).then_inc(k_read, 1)

                x_hi(0, lambda c: 0 + c)
                x_hi(1, lambda c: 1 + c)
                act.wait_ge(small_loaded, 128)
                act.activation(gate[:, HI], gate_f, ACT.Copy, scale=WSCALE).then_inc(w_hi_ready, 1)
                act.activation(upb, upb_raw, ACT.Copy, scale=WSCALE)
                for m in range(TB):
                    if m == KB:
                        act.wait_ge(q_loaded, 16)
                        act.activation(wq[:, HI], wq_f, ACT.Copy, scale=WSCALE).then_inc(w_hi_ready, 1)
                    x_turned(m, lambda c, m=m: m + c)
                    if m + 2 < FIRST:
                        x_hi(m + 2, lambda c, m=m: m + 2 + c)
                    if m < KB:
                        k_out(m)
                act.wait_ge(o_loaded, 16)
                act.activation(wo[:, HI], wo_f, ACT.Copy, scale=WSCALE)
                act.activation(wo_f, wo_f, ACT.Copy, scale=WSCALE).then_inc(w_scaled, 1)
                for q in range(KB + 1):
                    q_out(q, q + 1)
                exps(0, 1)
                act.wait_ge(vblk_ready, B)
                act.wait_ge(kblk_ready, KB)
                act.wait_ge(w_split, 2)
                act.wait_ge(wo_split, 1)

                def batch(b, first, last):
                    for t in range(TB + 2 * last):
                        if there(first, last, t):
                            act.wait_ge(pturn_done, tiled(b, t + 1))
                            act.wait_ge(att_done, tiled(b, t))
                            act.activation(pT, probT_ps, ACT.Copy).then_inc(pT_ready, 1)
                        if there(first, last, t - 2):
                            act.wait_ge(nturn_done, tiled(b, t - 1))
                            act.activation(nT, turn16_ps, ACT.Copy).then_inc(nT_ready, 1)
                        if there(first, last, t + 1):
                            exps((t + 1) % 2, tiled(b, t + 2))
                        if there(first, last, t - 1):
                            guess_2(tiled(b, t))
                        if not last:
                            x_turned(t, lambda c, t=t: tiled(b, TB + t + c), tiled(b, 4 * (t // 4) + 4))
                        if there(first, last, t):
                            act.wait_ge(wstage_loaded[t % 2], b * 64 + 16 * (t // 2 + 1))
                            w = weights[:, bass.ds(b, 1), t // KB, HI, t % KB, :].rearrange("p o n -> p (o n)")
                            act.activation(w, wstage[:, t % 2, :], ACT.Copy, scale=WSCALE).then_inc(wst_hi, 1)
                        q = t + KB + 1
                        if there(first, last, q):
                            q_out(q, tiled(b, q + 1), tiled(b, 4 * (q // KB) - 4))
                        if there(first, last, t - 1):
                            act.wait_ge(ln2_done, tiled(b, t))
                            act.activation(xrow[:, (t - 1) % 2, D:].bitcast(F16)[:, 0:D], xn2, ACT.Copy
                                           ).then_inc(nhi_done, 1)
                        if not last:
                            guess_1((t + 1) % 2, tiled(b, t + 1))
                        if there(first, last, t):
                            act.wait_ge(oturn_done, tiled(b, t + 1))
                            act.activation(oT, turn16_ps, ACT.Copy).then_inc(oT_ready, 1)
                        if there(first, last, t - 2):
                            act.wait_ge(gate_done, tiled(b, t - 1))
                            act.activation(logits[:, bass.ds(tiled(b, t - 2), 1), :].rearrange("p o e -> p (o e)"),
                                           gate_ps, ACT.Copy, scale=1.0 / WSCALE).then_inc(logits_ready, 1)
                        if not last:
                            x_hi(TB + t + 1, lambda c, t=t: tiled(b, TB + t + 1 + c))

                batches(act, batch)

            @block.gpsimd
            def _(pool):
                pool.memset(ident, 0.0).then_inc(id0, 1)
                pool.wait_ge(id0, 1)
                pool.affine_select(out=ident, in_=ident, compare_op=ALU.not_equal, fill=1.0, base=0,
                                   pattern=[[-1, P]], channel_multiplier=1).then_inc(id_ready, 1)
                pool.iota(zero_row[:, D:D + 1].bitcast(I32), pattern=[[0, 1]], base=TOKENS,
                          channel_multiplier=1).then_inc(consts_ready, 1)

                def x_lo(m, count):
                    pool.wait_ge(xhi_done, count(1))
                    src = x_first[:, m, :] if m < TB else xn1[:, m % 2, :]
                    pool.tensor_tensor(xhl[:, m % 2, LO, :], src, xhl[:, m % 2, HI, :],
                                       ALU.subtract).then_inc(xlo_done, 1)

                def p_lo(i, count):
                    pool.wait_ge(exp_done, count)
                    pool.tensor_tensor(phl[:, i, LO, :], prob[:, i, :], phl[:, i, HI, :],
                                       ALU.subtract).then_inc(plo_done, 1)

                pool.memset(v_f, 0.0).then_inc(cleared, 1)
                pool.memset(kblk, 0.0).then_inc(cleared, 1)
                pool.wait_ge(cleared, 2)
                for m in range(FIRST):
                    x_lo(m, lambda c, m=m: m + c)
                pool.wait_ge(w_scaled, 1)
                pool.tensor_tensor(wo[:, LO], wo_f, wo[:, HI], ALU.subtract).then_inc(wo_split, 1)
                p_lo(0, 1)

                def batch(b, first, last):
                    for t in range(TB + last):
                        if there(first, last, t):
                            pool.wait_ge(xres_loaded[t % 2], b * 64 + 16 * (t // 2 + 1))
                            pool.tensor_tensor(xres[:, t % 2, :], xres[:, t % 2, :], bo_b, ALU.add
                                               ).then_inc(xres_biased, 1)
                        if there(first, last, t + 1):
                            p_lo((t + 1) % 2, tiled(b, t + 2))
                        if there(first, last, t - 1):
                            pool.wait_ge(nhi_done, tiled(b, t))
                            hl = xrow[:, (t - 1) % 2, D:].bitcast(F16)
                            pool.tensor_tensor(hl[:, D:], xn2, hl[:, 0:D], ALU.subtract).then_inc(nlo_done, 1)
                        if not last:
                            x_lo(TB + t + 1, lambda c, t=t: tiled(b, TB + t + 1 + c))

                batches(pool, batch)

            @block.vector
            def _(dve):
                dve.memset(zero_row[:, 0:D], 0.0).then_inc(consts_ready, 1)
                dve.memset(zero_row[:, D + 1:], 0.0).then_inc(consts_ready, 1)
                dve.memset(ones3, 1.0).then_inc(consts_ready, 1)
                dve.memset(eps_c, EPS).then_inc(consts_ready, 1)

                def stats1(m, count, loaded):
                    dve.wait_ge(xin_loaded[m % 2], loaded)
                    dve.bn_stats(stat1[:, m % 2, :], xin[:, m % 2, :]).then_inc(ln1_stats, 1)
                    dve.wait_ge(ln1_stats, count)
                    settled(dve)
                    dve.bn_aggr(mv1[:, m % 2, :], stat1[:, m % 2, :]).then_inc(ln1_mv, 1)

                def newton(dst, count, var, root, i, guess_done, steps_done, done):
                    y, u = root[:, i, 0:1], root[:, i, 1:2]
                    dve.wait_ge(guess_done, count)
                    dve.scalar_tensor_tensor(out=u, in0=var, scalar=EPS, in1=y, op0=ALU.add, op1=ALU.mult
                                             ).then_inc(steps_done, 1)
                    dve.wait_ge(steps_done, count * 2 - 1)
                    dve.tensor_scalar(u, u, y, -0.5, ALU.mult, ALU.mult).then_inc(steps_done, 1)
                    dve.wait_ge(steps_done, count * 2)
                    dve.scalar_tensor_tensor(out=dst, in0=u, scalar=1.5, in1=y, op0=ALU.add, op1=ALU.mult
                                             ).then_inc(done, 1)

                def norm1(m, count, tile):
                    i = m % 2
                    newton(rstd1[:, i:i + 1], count, mv1[:, i, 1:2], root1, i, ln1_guess, ln1_steps, ln1_rstd)
                    dve.wait_ge(ln1_rstd, count)
                    dve.wait_ge(xlo_done, tile - 1)
                    dve.tensor_scalar(xn1[:, i, :], xin[:, i, :], mv1[:, i, 0:1],
                                      rstd1[:, i:i + 1], ALU.subtract, ALU.mult).then_inc(ln1_done, 1)

                def max_sub(i, count, lo_count=None):
                    s3 = scores_ps.rearrange("p (h k) -> p h k", h=H)
                    dve.wait_ge(scores_done, count)
                    dve.tensor_reduce(rowmax[:, i, :], s3, AX.X, ALU.max).then_inc(max_done, 1)
                    dve.wait_ge(max_done, count)
                    if lo_count is not None:
                        dve.wait_ge(plo_done, lo_count)
                    dve.tensor_tensor(prob[:, i, :].rearrange("p (h k) -> p h k", h=H), s3,
                                      rowmax[:, i, :].unsqueeze(2).to_broadcast([P, H, SK]),
                                      ALU.subtract).then_inc(sub_done, 1)

                def first_tile(m):
                    return x_first[:, m, :] if m < TB else xin[:, 0, :]

                for m in range(FIRST):
                    if m % HALF == 0 and m < TB:
                        dve.wait_ge(first_loaded[m // HALF], 16)
                    elif m == TB:
                        dve.wait_ge(xin_loaded[0], 16)
                    dve.bn_stats(stat0[:, m, :], first_tile(m)).then_inc(first_stats, 1)
                for m in range(FIRST):
                    dve.wait_ge(first_stats, m + 1)
                    dve.bn_aggr(mv0[:, m, :], stat0[:, m, :]).then_inc(first_mv, 1)
                dve.wait_ge(first_guess, 1)
                guess, term, root = root0[:, 0, :], root0[:, 1, :], root0[:, 2, :]
                dve.scalar_tensor_tensor(out=term, in0=mv0[:, :, 1], scalar=EPS, in1=guess, op0=ALU.add, op1=ALU.mult
                                         ).then_inc(first_steps, 1)
                dve.wait_ge(first_steps, 1)
                dve.tensor_tensor(term, term, guess, ALU.mult).then_inc(first_steps, 1)
                dve.wait_ge(first_steps, 2)
                dve.tensor_scalar(term, term, -0.5, 1.5, ALU.mult, ALU.add).then_inc(first_steps, 1)
                dve.wait_ge(first_steps, 3)
                dve.tensor_tensor(root, term, guess, ALU.mult).then_inc(first_rstd, 1)
                dve.wait_ge(first_rstd, 1)
                for m in range(FIRST):
                    dst = x_first[:, m, :] if m < TB else xn1[:, 0, :]
                    dve.tensor_scalar(dst, first_tile(m), mv0[:, m, 0:1], root[:, m:m + 1], ALU.subtract, ALU.mult
                                      ).then_inc(ln1_done, 1)

                steps = 0

                def step(instruction):
                    nonlocal steps
                    steps += 1
                    instruction.then_inc(pro_dve, 1)
                    dve.wait_ge(pro_dve, steps)

                step(dve.memset(vblk[:, :, :, :, 2 * DK:], 0.0))
                step(dve.memset(vblk[0:SK, HI, :, :, 2 * DK], WSCALE))
                step(dve.memset(vblk[SK:P, HI, :, :, 2 * DK + 1], WSCALE))
                dve.wait_ge(small_loaded, 128)
                dve.tensor_scalar(tau_k, tau_b, float(DK) ** -0.5, None, ALU.mult).then_inc(tau_ready, 1)
                dve.wait_ge(id_ready, 1)
                step(dve.tensor_scalar(delta_f[0:3], delta_f[0:3], float(DK) ** -0.5, None, ALU.mult))
                for i in range(3):
                    step(dve.tensor_copy(delta_p[0:3], delta_f[0:3]))
                    step(dve.tensor_tensor(delta_f[0:3], delta_f[0:3], delta_p[0:3], ALU.subtract))
                    if i == 0:
                        step(dve.tensor_scalar(delta_s[0:3], delta_p[0:3], ident[0:3, 0:1], None, ALU.mult))
                    else:
                        step(dve.scalar_tensor_tensor(out=delta_s[0:3], in0=delta_p[0:3],
                                                      scalar=ident[0:3, i:i + 1], in1=delta_s[0:3],
                                                      op0=ALU.mult, op1=ALU.add))
                dve.tensor_copy(delta3.rearrange("p b n -> p (b n)"), delta_s[0:3]).then_inc(delta_ready, 1)
                dve.wait_ge(kv_loaded, 32)
                for d in range(2):
                    dve.tensor_copy(ctx_2[:, :, :, d, :], ctx_f).then_inc(ctx2_ready, 1)

                def w_lo(dst, src, hi, n):
                    dve.wait_ge(w_hi_ready, n)
                    dve.scalar_tensor_tensor(out=dst, in0=src, scalar=WSCALE, in1=hi, op0=ALU.mult, op1=ALU.subtract
                                             ).then_inc(w_split, 1)

                w_lo(gate[:, LO], gate_f, gate[:, HI], 1)
                dve.wait_ge(cleared, 2)
                dve.wait_ge(tau_ready, 1)
                for g in range(QUADS):
                    dve.wait_ge(k_read, g + 1)
                    for j in range(4):
                        r = slice(j * DK, (j + 1) * DK)
                        ins = dve.tensor_tensor(kblk[r, :, g, j * SK:(j + 1) * SK], k_f[r, g],
                                                tau_k[r, :].unsqueeze(2).to_broadcast([DK, B, SK]), ALU.mult)
                    ins.then_inc(kblk_ready, 1)
                for b in range(B):
                    if b == 2:
                        w_lo(wq[:, LO], wq_f, wq[:, HI], 2)
                    dve.wait_ge(v_mm, b + 1)
                    for j in range(2):
                        r, c = slice(j * SK, (j + 1) * SK), slice(j * DK, (j + 1) * DK)
                        ins = dve.tensor_tensor(
                            v_f[r, b, :, c], psum[r, 2 + b % 2, :].rearrange("p (r n) -> p r n", r=PAIRS)[:, :, c],
                            bv_b[r].rearrange("p (r n) -> p r n", r=PAIRS)[:, :, c], ALU.add)
                        if j == 1:
                            ins.then_inc(v_read, 1)
                    dve.wait_ge(v_read, b + 1)
                    hi, lo = vblk[:, HI, b, :, 0:2 * DK], vblk[:, LO, b, :, 0:2 * DK]
                    step(dve.tensor_scalar(hi, v_f[:, b], WSCALE, None, ALU.mult))
                    ins = dve.scalar_tensor_tensor(out=lo, in0=v_f[:, b], scalar=WSCALE, in1=hi,
                                                   op0=ALU.mult, op1=ALU.subtract)
                    ins.then_inc(vblk_ready, 1)
                dve.wait_ge(xlo_done, TB)
                max_sub(0, 1)

                def batch(b, first, last):
                    for t in range(TB + last):
                        if there(first, last, t + 1):
                            max_sub((t + 1) % 2, tiled(b, t + 2), tiled(b, t))
                        if there(first, last, t - 1):
                            i = (t - 1) % 2
                            dve.wait_ge(proj_done, tiled(b, t))
                            dve.wait_ge(xres_biased, tiled(b, t))
                            dve.wait_ge(xrow_stored[i], b * 64 + 16 * ((t - 1) // 2))
                            x1 = xrow[:, i, 0:D]
                            dve.scalar_tensor_tensor(out=x1, in0=proj_ps, scalar=1.0 / WSCALE, in1=xres[:, i, :],
                                                     op0=ALU.mult, op1=ALU.add).then_inc(x1_done, 1)
                            dve.wait_ge(x1_done, tiled(b, t))
                            dve.bn_stats(stat2, x1).then_inc(ln2_stats, 1)
                            dve.wait_ge(ln2_stats, tiled(b, t))
                            settled(dve)
                            dve.bn_aggr(mv2, stat2).then_inc(ln2_mv, 1)
                        if there(first, last, t):
                            dve.wait_ge(att_done, tiled(b, t + 1))
                            dve.reciprocal(rden.rearrange("p (r j) -> p r j", r=PAIRS),
                                           att_ps[:, :, 2 * DK:VW]).then_inc(rden_done, 1)
                            dve.wait_ge(rden_done, tiled(b, t + 1))
                            dve.tensor_tensor(att_o.rearrange("p (r j n) -> p r j n", r=PAIRS, j=2),
                                              att_ps[:, :, 0:2 * DK].rearrange("p r (j n) -> p r j n", j=2),
                                              rden.rearrange("p (r j) -> p r j", r=PAIRS).unsqueeze(3)
                                              .to_broadcast([P, PAIRS, 2, DK]), ALU.mult).then_inc(norm_done, 1)
                            dve.wait_ge(norm_done, tiled(b, t + 1))
                            dve.wait_ge(oturn_done, tiled(b, t))
                            dve.tensor_copy(ohl[:, HI, :], att_o).then_inc(ohi_done, 1)
                            dve.wait_ge(ohi_done, tiled(b, t + 1))
                            dve.tensor_tensor(ohl[:, LO, :], att_o, ohl[:, HI, :], ALU.subtract).then_inc(olo_done, 1)
                        if there(first, last, t - 1):
                            newton(rstd2, tiled(b, t), mv2[:, 1:2], root2, 0, ln2_guess, ln2_steps, ln2_rstd)
                            dve.wait_ge(ln2_rstd, tiled(b, t))
                            if not (first and t == 1):
                                dve.wait_ge(nlo_done, tiled(b, t - 1))
                            dve.tensor_scalar(xn2, x1, mv2[:, 0:1], rstd2, ALU.subtract, ALU.mult).then_inc(ln2_done, 1)
                        if not last:
                            m = TB + t + 1
                            stats1(m, tiled(b, t + 1), b * 64 + 16 * ((m - TB) // 2 + 1))
                        if there(first, last, t):
                            dve.wait_ge(wst_hi, tiled(b, t + 1))
                            w = [weights[:, bass.ds(b, 1), t // KB, h, t % KB, :].rearrange("p o n -> p (o n)")
                                 for h in range(2)]
                            dve.scalar_tensor_tensor(out=w[LO], in0=wstage[:, t % 2, :], scalar=WSCALE, in1=w[HI],
                                                     op0=ALU.mult, op1=ALU.subtract).then_inc(wst_split, 1)
                        if not last:
                            norm1(TB + t + 1, tiled(b, t + 1), tiled(b, TB + t + 1))

                batches(dve, batch)

            @block.tensor
            def _(pe):
                def scores(b, col, qi):
                    for a in range(2):
                        bank = scores_ps[:, a * 512:(a + 1) * 512]
                        for j in range(2):
                            g = 2 * a + j
                            pe.matmul(bank[:, j * 256:(j + 1) * 256], qT[:, qi, g, col:col + P],
                                      kblk[:, bass.ds(b, 1), g, :].rearrange("p o n -> p (o n)"),
                                      start=(j == 0), stop=False, skip_group_check=True)
                        last = pe.matmul(bank, ones3, delta3[:, bass.ds(b, 1), :].to_broadcast([3, PAIRS, SK]),
                                         start=False, stop=True, skip_group_check=True)
                    last.then_inc(scores_done, 1)

                def x_turn(m, count):
                    pe.wait_ge(xlo_done, count(1))
                    transposes(pe, turn16_ps, xhl[:, m % 2], KB).then_inc(xturn_done, 1)

                def project_q(q):
                    half = (q // KB) % 2
                    split_products(pe, proj_ps,
                                   lambda part, k: wq[:, part, k, (q % KB) * P:(q % KB + 1) * P],
                                   lambda part, k: xT[:, part, k, half * 512:(half + 1) * 512]).then_inc(q_mm, 1)

                pe.wait_ge(id_ready, 1)
                pe.wait_ge(consts_ready, 5)

                def keys(g):
                    if g == 0:
                        pe.wait_ge(kv_loaded, 32)
                    if g >= 2:
                        pe.wait_ge(k_read, g - 1)
                    for k in range(KB):
                        ins = pe.matmul(psum[:, g % 2, 0:B * SK], wk_f[:, k, g * P:(g + 1) * P],
                                        ctx_f[:, k].rearrange("p b n -> p (b n)"), start=(k == 0), stop=(k == KB - 1))
                    ins.then_inc(k_mm, 1)

                def values(b):
                    if b == 0:
                        pe.wait_ge(v_loaded, 16)
                        pe.wait_ge(ctx2_ready, 2)
                    if b >= 2:
                        pe.wait_ge(v_read, b - 1)
                    for k in range(KB):
                        ins = pe.matmul(psum[:, 2 + b % 2, :], ctx_2[:, k, b].rearrange("p d n -> p (d n)"),
                                        wv_f[:, k, :], start=(k == 0), stop=(k == KB - 1))
                    ins.then_inc(v_mm, 1)

                for m in range(TB):
                    if m >= 1:
                        pe.wait_ge(xT_ready, m)
                    x_turn(m, lambda c, m=m: m + c)
                    if m < KB:
                        keys(m)
                    else:
                        values(m - KB)
                pe.wait_ge(w_split, 2)
                for q in range(KB + 1):
                    pe.wait_ge(xT_ready, 4 if q < KB else TB)
                    if q >= 1:
                        pe.wait_ge(q_ready, q)
                    project_q(q)
                pe.wait_ge(q_ready, KB)
                pe.wait_ge(kblk_ready, QUADS)
                pe.wait_ge(delta_ready, 1)
                pe.wait_ge(k_read, QUADS)
                scores(0, 0, 0)
                pe.wait_ge(vblk_ready, B)
                pe.wait_ge(sub_done, 1)
                scores(0, P, 0)
                pe.wait_ge(wo_split, 1)

                def next_scores(b, first, last, c):
                    if there(first, last, c):
                        pe.wait_ge(q_ready, tiled(b, 4 * (c // 4) + 4))
                        pe.wait_ge(sub_done, tiled(b, c))
                        scores(b + c // TB, (c % 4) * P, (c // 4) % 2)

                def batch(b, first, last):
                    for t in range(TB + 2 * last):
                        if there(first, last, t):
                            pe.wait_ge(plo_done, tiled(b, t + 1))
                            pe.wait_ge(pT_ready, tiled(b, t))
                            transposes(pe, probT_ps, phl[:, t % 2], PAIRS).then_inc(pturn_done, 1)
                        if there(first, last, t - 2):
                            pe.wait_ge(nlo_done, tiled(b, t - 1))
                            pe.wait_ge(oT_ready, tiled(b, min(t, TB) if last else t))
                            hl = xrow[:, t % 2, D:].bitcast(F16).rearrange("p (h n) -> p h n", h=2)
                            transposes(pe, turn16_ps, hl, KB).then_inc(nturn_done, 1)
                        if there(first, last, t - 1):
                            pe.wait_ge(oT_ready, tiled(b, t))
                            pe.wait_ge(q_ready, tiled(b, min(t + KB + 1, TB) if last else t + KB + 1))
                            split_products(pe, proj_ps, lambda part, k: oT[:, part, k, :],
                                           lambda part, k: wo[:, part, k, :]).then_inc(proj_done, 1)
                        if there(first, last, t):
                            pe.wait_ge(pT_ready, tiled(b, t + 1))
                            pe.wait_ge(norm_done, tiled(b, t))
                            if there(first, last, t - 3):
                                pe.wait_ge(logits_ready, tiled(b, t - 2))
                            for r in range(PAIRS):
                                for n, (h, i) in enumerate(PRODUCTS):
                                    mm = pe.matmul(att_ps[:, r, 0:VW], pT[:, h, r, :],
                                                   vblk[:, i, bass.ds(b, 1), r, :].rearrange("p o n -> p (o n)"),
                                                   start=(n == 0), stop=(n == 2))
                            mm.then_inc(att_done, 1)
                        if not last:
                            if there(first, last, t - 2):
                                pe.wait_ge(nT_ready, tiled(b, t - 1))
                            elif t > 0:
                                pe.wait_ge(oT_ready, tiled(b, t))
                            x_turn(t, lambda c, t=t: tiled(b, TB + t + c))
                        if t % 4 == 3:
                            next_scores(b, first, last, t + 2)
                        q = t + KB + 1
                        if there(first, last, q):
                            pe.wait_ge(x1_done, tiled(b, t))
                            pe.wait_ge(xT_ready, tiled(b, 4 * (q // KB) + 4))
                            project_q(q)
                        if there(first, last, t):
                            pe.wait_ge(olo_done, tiled(b, t + 1))
                            if not last:
                                pe.wait_ge(xT_ready, tiled(b, TB + t + 1))
                            else:
                                pe.wait_ge(nT_ready, tiled(b, t - 1))
                            transposes(pe, turn16_ps, ohl, KB).then_inc(oturn_done, 1)
                        if there(first, last, t - 2):
                            pe.wait_ge(nT_ready, tiled(b, t - 1))
                            split_products(pe, gate_ps, lambda part, k: nT[:, part, k, :],
                                           lambda part, k: gate[:, part, k, :]).then_inc(gate_done, 1)
                        if t % 4 != 3:
                            next_scores(b, first, last, t + 2)

                batches(pe, batch)

        if stop_after == "attention":
            return

        consts2, iotas_ready, picked, prefix_done, softmax_sub, softmax_exp, routed = (
            sem("consts2"), sem("iotas_ready"), sem("picked"), sem("prefix_done"), sem("softmax_sub"),
            sem("softmax_exp"), sem("routed"))
        pads_placed, pads_scattered = sem("pads_placed"), sem("pads_scattered")
        route_step, downb_loaded = sem("route_step"), sem("downb_loaded")
        U32 = mybir.dt.uint32
        N_IOTA = SLOTS + TILES + E + PADS
        iota_i = rt(1, N_IOTA).rearrange("p a c -> p (a c)").bitcast(I32)
        iota_f = rt(1, N_IOTA).rearrange("p a c -> p (a c)")
        slot_f, thresholds, ranks_f, pad_f = (iota_f[:, 0:SLOTS], iota_f[:, SLOTS:SLOTS + TILES],
                                              iota_f[:, SLOTS + TILES:N_IOTA - PADS], iota_f[:, N_IOTA - PADS:])
        before = rt(1, P, F16).rearrange("p a c -> p (a c)")
        ones_m = rt(1, P, F16).rearrange("p a c -> p (a c)")
        picks16 = rt(dt=F16)
        shifted, prob8, masked, scratch8 = rt(), rt(), rt(), rt()
        first, second, places_f = rt(), rt(), rt()
        sums = [rt(), rt()]
        totals = rt()
        top, w_first, w_second, best, found = rt(c=1), rt(c=1), rt(c=1), rt(c=1), rt(c=1)
        pos_f = rt(c=1)
        counts = rt(E, TILES)
        used_count, starts = rt(2, E), rt(2, E)
        used, count = used_count[:, 0, :], used_count[:, 1, :]
        ends = [rt(2, E), rt(2, E)]
        base, pad_start = rt(E, 1), rt(E, 1)
        pad_ge, pad_sum = rt(PADS, E), rt(PADS, 1)
        slot_ge = rt(SLOTS, E)
        slot_sum = rt(SLOTS, 1)
        assert cuts["rt"] <= FFN0
        prefix_ps = psum[:, 6, 0:TILES * E].rearrange("p (t e) -> p t e", e=E)
        totals_ps = psum[:, 7, 0:TILES * E].rearrange("p (t e) -> p t e", e=E)


        def stage_sems(tag):
            names = ("turned", "eT_ready", "up_done", "biased", "silu_done", "hhi_done", "hidden_split",
                     "down_done", "bias_ready", "y_done")
            return [sem(f"{tag}_{n}") for n in names]

        def up_product(pe, dst, place, j):
            for m in range(KB):
                n = 0
                for k in range(KB):
                    for a, c in PRODUCTS:
                        w = weights[:, place, 0, a, k, m * P:(m + 1) * P] if isinstance(place, int) else \
                            weights[:, bass.ds(place, 1), 0, a, k, m * P:(m + 1) * P].rearrange("p o n -> p (o n)")
                        last = pe.matmul(dst[:, m * P:(m + 1) * P], w, eT[:, j, c, k, :],
                                         start=(n == 0), stop=(n == 3 * KB - 1))
                        n += 1
            return last

        def down_product(pe, dst, place, j):
            n = 0
            for k in range(KB):
                for a, c in PRODUCTS:
                    w = weights[:, place, 1, c, k, :] if isinstance(place, int) else \
                        weights[:, bass.ds(place, 1), 1, c, k, :].rearrange("p o n -> p (o n)")
                    last = pe.matmul(dst, hhl[:, j, a, k * P:(k + 1) * P], w, start=(n == 0), stop=(n == 3 * KB - 1))
                    n += 1
            return last

        def split_hidden(dve, j, silu_done, hhi_done, hidden_split, count):
            dve.wait_ge(silu_done, count)
            dve.tensor_copy(hhl[:, j, HI, :], hid).then_inc(hhi_done, 1)
            dve.wait_ge(hhi_done, count)
            dve.tensor_tensor(hhl[:, j, LO, :], hid, hhl[:, j, HI, :], ALU.subtract).then_inc(hidden_split, 1)

        TI = 6
        row_loaded = [sem(f"row_loaded{i}") for i in range(NROW)]
        x1_loaded = [sem(f"x1_loaded{i}") for i in range(NROW)]
        scattered = [sem(f"scattered{i}") for i in range(NROW)]
        (turned, eT_ready, up_done, biased, silu_done, hhi_done, hidden_split, down_done, x1_biased,
         y_done) = stage_sems("shared")
        meta_copied = sem("meta_copied")
        y_stored = s2("y_stored")
        estage_loaded = s2("estage_loaded")
        est_scaled, est_split = sem("est_scaled"), sem("est_split")
        CHUNKS = [[0, 1], [2], [3], [4, 5], [6], [7], [], []]
        NBODY2 = PLACES - EARLY

        with nc.Block() as block:

            @block.sync
            def _(sp):
                for i in range(NROW):
                    sp.dma_start(rows[:, i, 0:D], xrows[i, :, D:XROW]).then_inc(row_loaded[i], 16)
                    if i < 2:
                        sp.dma_start(x1_rows[:, i, :], xrows[i, :, 0:D]).then_inc(x1_loaded[i], 16)
                for j in range(2):
                    sp.dma_start(estage[:, j, :], ffn_w[EARLY, 0, j * P:(j + 1) * P, :]).then_inc(estage_loaded[j], 16)
                sp.dma_start(downb, down_b.rearrange("(o e) n -> o e n", o=1).to_broadcast([P, PLACES, D])
                             ).then_inc(downb_loaded, 16)

                def body(b, last):
                    tiles = TI + 2 * last
                    for t in range(tiles):
                        if t + 3 < tiles or not last:
                            sp.wait_ge(turned, b * TI + t + 1)
                            settled(sp)
                            sp.wait_ge(scattered[t % NROW], b * 64 + 32 * (t // NROW + 1))
                            sp.dma_start(rows[:, t % NROW, 0:D],
                                         xrows[bass.ds(b * TI + t + 3, 1), :, D:XROW].rearrange("o p n -> p (o n)")
                                         ).then_inc(row_loaded[t % NROW], 16)
                        if t + 2 < tiles or not last:
                            sp.wait_ge(y_done, b * TI + t)
                            settled(sp)
                            sp.dma_start(x1_rows[:, (t + 2) % NROW, :],
                                         xrows[bass.ds(b * TI + t + 2, 1), :, 0:D].rearrange("o p n -> p (o n)")
                                         ).then_inc(x1_loaded[(t + 2) % NROW], 16)
                        for j in CHUNKS[t]:
                            if not (last and j >= 6):
                                sp.wait_ge(est_split, b * 8 + j + 1)
                                c = (j + 2) % 8
                                sp.dma_start(estage[:, j % 2, :],
                                             ffn_w[bass.ds(b + EARLY + (j + 2) // 8, 1), c // KB,
                                                   (c % KB) * P:(c % KB + 1) * P, :].rearrange("o p n -> p (o n)")
                                             ).then_inc(estage_loaded[j % 2], 16)
                        sp.wait_ge(y_done, b * TI + t + 1)
                        sp.dma_start(out[bass.ds((b * TI + t) * P, P), :], yout[:, t % 2, :]
                                     ).then_inc(y_stored[t % 2], 16)

                bodies(sp, NBODY2, body)
                for i in range(2):
                    sp.wait_ge(y_stored[i], 16 * TILES // 2)

            @block.scalar
            def _(act):
                def turned_out(i, count, up_count=None):
                    act.wait_ge(turned, count)
                    if up_count is not None:
                        act.wait_ge(up_done, up_count)
                    act.activation(eT[:, i % 2], eturn16_ps[i % 2], ACT.Copy).then_inc(eT_ready, 1)

                def silu(i, count, split_count=None):
                    act.wait_ge(biased, count)
                    if split_count is not None:
                        act.wait_ge(hidden_split, split_count)
                    act.activation(hid, pre[:, i % 2, :], ACT.Silu, scale=1.0 / WSCALE).then_inc(silu_done, 1)

                turned_out(0, 1)
                turned_out(1, 2)
                act.wait_ge(softmax_sub, 1)
                act.activation(shifted, shifted, ACT.Exp).then_inc(softmax_exp, 1)
                silu(0, 1)

                def body(b, last):
                    for t in range(TI + 2 * last):
                        if not (last and t >= TI):
                            turned_out(t, b * TI + t + 3, b * TI + t + 1)
                        if not (last and t == TI + 1):
                            silu(t + 1, b * TI + t + 2, b * TI + t + 1)
                        for j in CHUNKS[t]:
                            act.wait_ge(estage_loaded[j % 2], b * 64 + 16 * (j // 2 + 1))
                            w = weights[:, bass.ds(b + EARLY, 1), j // KB, HI, j % KB, :].rearrange("p o n -> p (o n)")
                            act.activation(w, estage[:, j % 2, :], ACT.Copy, scale=WSCALE)
                            act.activation(estage[:, j % 2, :], estage[:, j % 2, :], ACT.Copy,
                                           scale=WSCALE).then_inc(est_scaled, 1)

                bodies(act, NBODY2, body)

            @block.gpsimd
            def _(pool):
                pool.iota(iota_i[:, 0:SLOTS], pattern=[[1, SLOTS]], base=0, channel_multiplier=0)
                pool.iota(iota_i[:, SLOTS:SLOTS + TILES], pattern=[[P, TILES]], base=0, channel_multiplier=0)
                pool.iota(iota_i[:, SLOTS + TILES:N_IOTA - PADS], pattern=[[-1, E]], base=E, channel_multiplier=0)
                pool.iota(iota_i[:, N_IOTA - PADS:], pattern=[[P, PADS]], base=0, channel_multiplier=1
                          ).then_inc(iotas_ready, 1)
                pool.iota(meta[:, :, 0].bitcast(I32), pattern=[[P, TILES]], base=0, channel_multiplier=1
                          ).then_inc(iotas_ready, 1)
                pool.memset(ones_m, 1.0)
                pool.memset(before, 1.0).then_inc(consts2, 1)
                pool.wait_ge(consts2, 1)
                pool.affine_select(out=before, in_=before, compare_op=ALU.is_gt, fill=0.0, base=0,
                                   pattern=[[1, P]], channel_multiplier=-1).then_inc(consts2, 1)
                def scatter(b, t):
                    i = t % NROW
                    pool.wait_ge(row_loaded[i], b * 32 + 16 * (t // NROW + 1))
                    pool.tensor_copy(rows[:, i, D:D + META + TOPK].bitcast(I32),
                                     meta[:, bass.ds(b * TI + t, 1), :].rearrange("p o n -> p (o n)").bitcast(I32)
                                     ).then_inc(meta_copied, 1)
                    pool.wait_ge(meta_copied, b * TI + t + 1)
                    settled(pool)
                    for k in range(TOPK):
                        pool.indirect_dma_start(
                            out=sorted_rows[:, :],
                            out_offset=bass.IndirectOffsetOnAxis(
                                ap=rows[:, i, D + META + k:D + META + k + 1].bitcast(U32), axis=0),
                            in_=rows[:, i, 0:ROW], in_offset=None).then_inc(scattered[i], 16)

                pool.wait_ge(downb_loaded, 16)
                pool.wait_ge(routed, 1)
                scatter(0, 0)
                scatter(0, 1)

                def body(b, last):
                    tiles = TI + 2 * last
                    for t in range(tiles):
                        pool.wait_ge(x1_loaded[t % NROW], b * 32 + 16 * (t // NROW + 1))
                        pool.tensor_tensor(x1_rows[:, t % NROW, :], x1_rows[:, t % NROW, :], downb[:, 0, :], ALU.add
                                           ).then_inc(x1_biased, 1)
                        if t + 2 < tiles or not last:
                            scatter(b, t + 2)
                        if last and t < PADS:
                            pool.wait_ge(pads_placed, 1)
                            pool.indirect_dma_start(
                                out=sorted_rows[:, :],
                                out_offset=bass.IndirectOffsetOnAxis(ap=pad_pos[:, t:t + 1].bitcast(U32), axis=0),
                                in_=zero_row, in_offset=None).then_inc(pads_scattered, 16)
                        for j in CHUNKS[t]:
                            pool.wait_ge(est_scaled, b * 8 + j + 1)
                            w = [weights[:, bass.ds(b + EARLY, 1), j // KB, h, j % KB, :].rearrange("p o n -> p (o n)")
                                 for h in range(2)]
                            pool.tensor_tensor(w[LO], estage[:, j % 2, :], w[HI], ALU.subtract).then_inc(est_split, 1)

                bodies(pool, NBODY2, body)
                pool.wait_ge(pads_scattered, 16 * PADS)
                for i in range(NROW):
                    pool.wait_ge(scattered[i], 32 * ((TILES - 1 - i) // NROW + 1))

            @block.vector
            def _(dve):
                def bias(i, count, silu_count=None):
                    dve.wait_ge(up_done, count)
                    if silu_count is not None:
                        dve.wait_ge(silu_done, silu_count)
                    dve.tensor_tensor(pre[:, i % 2, :].rearrange("p (m t) -> p m t", m=KB),
                                      up_ps[i % 2].rearrange("p (m t) -> p m t", m=KB),
                                      upb[:, 0:KB].unsqueeze(2).to_broadcast([P, KB, P]), ALU.add
                                      ).then_inc(biased, 1)

                steps = 0

                def step(instruction):
                    nonlocal steps
                    steps += 1
                    instruction.then_inc(route_step, 1)
                    dve.wait_ge(route_step, steps)

                def over_experts(v):
                    return v.unsqueeze(2).to_broadcast([P, TILES, E])

                ranks = ranks_f.unsqueeze(1).to_broadcast([P, TILES, E])
                dve.wait_ge(iotas_ready, 2)
                step(dve.tensor_copy(iota_f, iota_i))
                step(dve.memset(meta[:, :, 2 * E + 1:META], 0.0))
                step(dve.tensor_reduce(top, logits, AX.X, ALU.max))
                dve.tensor_tensor(shifted, logits, over_experts(top), ALU.subtract).then_inc(softmax_sub, 1)
                dve.wait_ge(softmax_exp, 1)
                step(dve.tensor_reduce(best, shifted, AX.X, ALU.add))
                step(dve.reciprocal(best, best))
                step(dve.tensor_tensor(prob8, shifted, over_experts(best), ALU.mult))

                def pick(scores, weight, one_hot):
                    step(dve.tensor_reduce(weight, scores, AX.X, ALU.max))
                    step(dve.tensor_tensor(scratch8, scores, over_experts(weight), ALU.is_equal))
                    step(dve.tensor_tensor(scratch8, scratch8, ranks, ALU.mult))
                    step(dve.tensor_reduce(found, scratch8, AX.X, ALU.max))
                    step(dve.tensor_tensor(one_hot, ranks, over_experts(found), ALU.is_equal))

                pick(prob8, w_first, first)
                step(dve.scalar_tensor_tensor(out=masked, in0=first, scalar=-2.0, in1=prob8,
                                              op0=ALU.mult, op1=ALU.add))
                pick(masked, w_second, second)
                dve.tensor_tensor(picks16, first, second, ALU.add).then_inc(picked, 1)
                step(dve.tensor_tensor(best, w_first, w_second, ALU.add))
                step(dve.tensor_scalar(best, best, 1e-20, None, ALU.add))
                step(dve.reciprocal(best, best))
                step(dve.tensor_tensor(w_first, w_first, best, ALU.mult))
                step(dve.tensor_tensor(w_second, w_second, best, ALU.mult))
                step(dve.tensor_tensor(scratch8, first, over_experts(w_first), ALU.mult))
                step(dve.tensor_tensor(masked, second, over_experts(w_second), ALU.mult))
                step(dve.tensor_tensor(meta[:, :, 1:E + 1], scratch8, masked, ALU.add))
                step(dve.tensor_scalar(meta[:, :, E + 1:2 * E + 1], meta[:, :, 1:E + 1], 1.0 / WSCALE, None, ALU.mult))
                dve.wait_ge(prefix_done, 1)
                step(dve.tensor_copy(totals, totals_ps))
                src = totals
                for n, shift in enumerate((1, 2, 4, 8, 16)):
                    dst = sums[n % 2]
                    step(dve.tensor_tensor(dst[:, shift:], src[:, shift:], src[:, :-shift], ALU.add))
                    step(dve.tensor_copy(dst[:, :shift], src[:, :shift]))
                    src = dst
                step(dve.tensor_tensor(counts, src[:, TILES - 1, :].unsqueeze(2).to_broadcast([P, E, TILES]),
                                       thresholds.unsqueeze(1).to_broadcast([P, E, TILES]), ALU.is_gt))
                step(dve.tensor_reduce(used, counts, AX.X, ALU.add))
                step(dve.tensor_copy(count, src[:, TILES - 1, :]))
                end = used_count
                for n, shift in enumerate((1, 2, 4)):
                    dst = ends[n % 2]
                    step(dve.tensor_tensor(dst[:, :, shift:], end[:, :, shift:], end[:, :, :-shift], ALU.add))
                    step(dve.tensor_copy(dst[:, :, :shift], end[:, :, :shift]))
                    end = dst
                step(dve.tensor_tensor(starts, end, used_count, ALU.subtract))
                end = end[:, 0, :]
                step(dve.tensor_scalar(base, starts[:, 0, :], float(P), None, ALU.mult))
                step(dve.tensor_tensor(places_f, src, totals, ALU.subtract))
                step(dve.tensor_tensor(places_f, prefix_ps, places_f, ALU.add))
                step(dve.tensor_tensor(places_f, places_f, base.unsqueeze(1).to_broadcast([P, TILES, E]), ALU.add))
                for k, one_hot in enumerate((first, second)):
                    step(dve.tensor_tensor(scratch8, places_f, one_hot, ALU.mult))
                    step(dve.tensor_reduce(pos_f, scratch8, AX.X, ALU.add))
                    step(dve.tensor_copy(meta[:, :, META + k].bitcast(I32), pos_f))
                step(dve.tensor_tensor(slot_ge, slot_f.unsqueeze(2).to_broadcast([P, SLOTS, E]),
                                       end.unsqueeze(1).to_broadcast([P, SLOTS, E]), ALU.is_ge))
                step(dve.tensor_reduce(slot_sum, slot_ge, AX.X, ALU.add))
                dve.tensor_scalar(slot_place, slot_sum, 1.0, float(E), ALU.add, ALU.min).then_inc(routed, 1)
                step(dve.tensor_tensor(pad_start, base, starts[:, 1, :], ALU.subtract))
                step(dve.tensor_tensor(pad_ge, pad_f.unsqueeze(2).to_broadcast([P, PADS, E]),
                                       pad_start.unsqueeze(1).to_broadcast([P, PADS, E]), ALU.is_ge))
                step(dve.tensor_tensor(pad_ge, pad_ge, count.unsqueeze(1).to_broadcast([P, PADS, E]), ALU.mult))
                step(dve.tensor_reduce(pad_sum, pad_ge, AX.X, ALU.add))
                dve.tensor_tensor(pad_pos, pad_sum, pad_f, ALU.add).then_inc(pads_placed, 1)
                bias(0, 1)
                split_hidden(dve, 0, silu_done, hhi_done, hidden_split, 1)

                def body(b, last):
                    for t in range(TI + 2 * last):
                        n = b * TI + t
                        if not (last and t == TI + 1):
                            bias(t + 1, n + 2, n)
                            dve.wait_ge(down_done, n)
                            split_hidden(dve, (t + 1) % 2, silu_done, hhi_done, hidden_split, n + 2)
                        dve.wait_ge(down_done, n + 1)
                        dve.wait_ge(x1_biased, n + 1)
                        dve.wait_ge(y_stored[t % 2], b * 48 + 16 * (t // 2))
                        dve.scalar_tensor_tensor(out=yout[:, t % 2, :], in0=down_ps[t % 2], scalar=1.0 / WSCALE,
                                                 in1=x1_rows[:, t % NROW, :], op0=ALU.mult, op1=ALU.add
                                                 ).then_inc(y_done, 1)

                bodies(dve, NBODY2, body)

            @block.tensor
            def _(pe):
                def turn(i, loaded):
                    pe.wait_ge(row_loaded[i % NROW], loaded)
                    transposes(pe, eturn16_ps[i % 2], parts(rows[:, i % NROW, :]), KB).then_inc(turned, 1)

                turn(0, 16)
                turn(1, 16)
                pe.wait_ge(eT_ready, 1)
                up_product(pe, up_ps[0], 0, 0).then_inc(up_done, 1)
                pe.wait_ge(picked, 1)
                pe.wait_ge(consts2, 2)
                flat = picks16.rearrange("p t e -> p (t e)")
                pe.matmul(psum[:, 6, 0:TILES * E], before, flat, start=True, stop=True)
                pe.matmul(psum[:, 7, 0:TILES * E], ones_m, flat, start=True, stop=True).then_inc(prefix_done, 1)

                def body(b, last):
                    for t in range(TI + 2 * last):
                        n = b * TI + t
                        if not (last and t == TI + 1):
                            pe.wait_ge(eT_ready, n + 2)
                            pe.wait_ge(biased, n)
                            up_product(pe, up_ps[(t + 1) % 2], 0, (t + 1) % 2).then_inc(up_done, 1)
                        if not (last and t >= TI):
                            turn(t + 2, b * 32 + 16 * ((t + 2) // NROW + 1))
                        pe.wait_ge(hidden_split, n + 1)
                        pe.wait_ge(y_done, n)
                        down_product(pe, down_ps[t % 2], 0, t % 2).then_inc(down_done, 1)

                bodies(pe, NBODY2, body)

        if stop_after == "shared":
            return

        slot_loaded = [sem(f"slot_loaded{i}") for i in range(NSLOT)]
        (turned, eT_ready, up_done, biased, silu_done, hhi_done, hidden_split, down_done, bias_weighted,
         y_done) = stage_sems("slot")
        added = s2("added")
        BODIES = -(-SLOTS // TI)
        assert TI == NSLOT

        def slots_of(last):
            return SLOTS - (BODIES - 1) * TI if last else TI

        AHEAD = 4

        with nc.Block() as block:

            def place_of(eng, n):
                return eng.value_load(slot_place[0:1, bass.ds(n, 1)], min_val=1, max_val=E)

            @block.sync
            def _(sp):
                for i in range(AHEAD):
                    sp.dma_start(slots[:, i, :], sorted_rows[i * P:(i + 1) * P, :]).then_inc(slot_loaded[i], 16)

                def body(b, last):
                    for t in range(slots_of(last)):
                        if not (last and t + AHEAD >= slots_of(last)):
                            sp.wait_ge(added[t % 2], b * 48 + 16 * (t // 2))
                            settled(sp)
                            i = (t + AHEAD) % NSLOT
                            sp.dma_start(slots[:, i, :], sorted_rows[bass.ds((b * TI + t + AHEAD) * P, P), :]
                                         ).then_inc(slot_loaded[i], 16)

                bodies(sp, BODIES, body)

            @block.scalar
            def _(act):
                def turned_out(i, count, up_count=None):
                    act.wait_ge(turned, count)
                    if up_count is not None:
                        act.wait_ge(up_done, up_count)
                    act.activation(eT[:, i % 2], eturn16_ps[i % 2], ACT.Copy).then_inc(eT_ready, 1)

                def silu(i, count, split_count=None):
                    act.wait_ge(biased, count)
                    if split_count is not None:
                        act.wait_ge(hidden_split, split_count)
                    act.activation(hid, pre[:, i % 2, :], ACT.Silu, scale=1.0 / WSCALE).then_inc(silu_done, 1)

                turned_out(0, 1)
                turned_out(1, 2)
                silu(0, 1)

                def body(b, last):
                    for t in range(slots_of(last)):
                        n = b * TI + t
                        if not (last and t >= slots_of(last) - 2):
                            turned_out(t, n + 3, n + 1)
                        if not (last and t == slots_of(last) - 1):
                            silu(t + 1, n + 2, n + 1)
                        place = place_of(act, n)
                        act.wait_ge(slot_loaded[t], b * 16 + 16)
                        act.wait_ge(y_done, n)
                        act.activation(wbias, downb[:, bass.ds(place, 1), :].rearrange("p o n -> p (o n)"), ACT.Copy,
                                       scale=slots[:, t, bass.ds(D + place, 1)]).then_inc(bias_weighted, 1)

                bodies(act, BODIES, body)

            @block.gpsimd
            def _(pool):
                def body(b, last):
                    for t in range(slots_of(last)):
                        pool.wait_ge(y_done, b * TI + t + 1)
                        pool.wait_ge(added[(t + 1) % 2], b * 48 + 16 * ((t + 1) // 2))
                        settled(pool)
                        pool.indirect_dma_start(
                            out=out[:, :],
                            out_offset=bass.IndirectOffsetOnAxis(
                                ap=slots[:, t, D:D + 1].bitcast(U32), axis=0),
                            in_=yout[:, t % 2, :], in_offset=None, compute_op=ALU.add).then_inc(added[t % 2], 16)

                bodies(pool, BODIES, body)
                for i in range(2):
                    pool.wait_ge(added[i], 16 * ((SLOTS + 1 - i) // 2))

            @block.vector
            def _(dve):
                def bias(i, n, count, silu_count=None):
                    place = place_of(dve, n)
                    dve.wait_ge(up_done, count)
                    if silu_count is not None:
                        dve.wait_ge(silu_done, silu_count)
                    dve.tensor_tensor(pre[:, i % 2, :].rearrange("p (m t) -> p m t", m=KB),
                                      up_ps[i % 2].rearrange("p (m t) -> p m t", m=KB),
                                      upb[:, bass.ds(place * KB, KB)].unsqueeze(2).to_broadcast([P, KB, P]), ALU.add
                                      ).then_inc(biased, 1)

                bias(0, 0, 1)
                split_hidden(dve, 0, silu_done, hhi_done, hidden_split, 1)

                def body(b, last):
                    for t in range(slots_of(last)):
                        n = b * TI + t
                        if not (last and t == slots_of(last) - 1):
                            bias(t + 1, n + 1, n + 2, n)
                            dve.wait_ge(down_done, n)
                            split_hidden(dve, (t + 1) % 2, silu_done, hhi_done, hidden_split, n + 2)
                        place = place_of(dve, n)
                        dve.wait_ge(down_done, n + 1)
                        dve.wait_ge(bias_weighted, n + 1)
                        dve.wait_ge(added[t % 2], b * 48 + 16 * (t // 2))
                        dve.scalar_tensor_tensor(out=yout[:, t % 2, :], in0=down_ps[t % 2],
                                                 scalar=slots[:, t, bass.ds(D + E + place, 1)],
                                                 in1=wbias, op0=ALU.mult, op1=ALU.add).then_inc(y_done, 1)

                bodies(dve, BODIES, body)

            @block.tensor
            def _(pe):
                def turn(i, loaded):
                    pe.wait_ge(slot_loaded[i % NSLOT], loaded)
                    transposes(pe, eturn16_ps[i % 2], parts(slots[:, i % NSLOT, :]), KB).then_inc(turned, 1)

                turn(0, 16)
                turn(1, 16)
                pe.wait_ge(eT_ready, 1)
                up_product(pe, up_ps[0], place_of(pe, 0), 0).then_inc(up_done, 1)

                def body(b, last):
                    place = place_of(pe, b * TI)
                    for t in range(slots_of(last)):
                        n = b * TI + t
                        if not (last and t == slots_of(last) - 1):
                            next_place = place_of(pe, n + 1)
                            pe.wait_ge(eT_ready, n + 2)
                            pe.wait_ge(biased, n)
                            up_product(pe, up_ps[(t + 1) % 2], next_place, (t + 1) % 2).then_inc(up_done, 1)
                        if not (last and t >= slots_of(last) - 2):
                            turn(t + 2, b * 16 + 16 * ((t + 2) // NSLOT + 1))
                        pe.wait_ge(hidden_split, n + 1)
                        pe.wait_ge(y_done, n)
                        down_product(pe, down_ps[t % 2], place, t % 2).then_inc(down_done, 1)
                        place = next_place

                bodies(pe, BODIES, body)


INPUTS = ("x", "ctxT", "tau", "delta", "wqT", "wkT", "wvT", "woT", "bq", "bk", "bv", "bo",
          "gateT", "ffn_w", "up_b", "down_b")


def layout(i):
    a = {k: np.asarray(v) for k, v in i.items()}
    ffn_w = np.empty((PLACES, 2, D, D), np.float32)
    ffn_w[0, 0], ffn_w[0, 1] = a["L0_ffn_sh_up_w"], a["L0_ffn_sh_down_w"]
    ffn_w[1:, 0], ffn_w[1:, 1] = a["L0_ffn_up_w"], a["L0_ffn_down_w"]
    t = np.ascontiguousarray

    def columns(bias):
        return t(bias.reshape(-1, P).T)

    return {
        "x": a["x"].reshape(TILES, P, D),
        "ctxT": t(a["ctx_1024"].reshape(B * SK, D).T),
        "tau": a["condB_tau"],
        "delta": a["fside_BxS2_0"].reshape(B * SK),
        "wqT": t(a["L0_xcond_Wq"].T), "wkT": t(a["L0_xcond_Wk"].T),
        "wvT": t(a["L0_xcond_Wv"].T), "woT": t(a["L0_xcond_Wo"].T),
        "bq": columns(a["L0_xcond_bq"]), "bk": columns(a["L0_xcond_bk"]),
        "bv": a["L0_xcond_bv"], "bo": a["L0_xcond_bo"],
        "gateT": t(a["L0_ffn_gate_w"].T),
        "ffn_w": ffn_w,
        "up_b": columns(np.concatenate([a["L0_ffn_sh_up_b"][None], a["L0_ffn_up_b"]])),
        "down_b": np.concatenate([a["L0_ffn_sh_down_b"][None], a["L0_ffn_down_b"]]),
    }


def kernel(**inputs):
    import concourse.bacc as bacc
    from concourse.bass_utils import run_bass_kernel_spmd

    nc = bacc.Bacc("TRN2", target_bir_lowering=False, num_devices=1)
    arrays = {f"in_{k}": v for k, v in layout(inputs).items()}
    args = [nc.dram_tensor(f"in_{k}", arrays[f"in_{k}"].shape, F32, kind="ExternalInput").ap() for k in INPUTS]
    out = nc.dram_tensor("out", (TOKENS + P, D), F32, kind="ExternalOutput").ap()
    build_program(nc, *args, out)
    r = run_bass_kernel_spmd(nc, [arrays], core_ids=[0])
    return r.results[0]["out"][:TOKENS].reshape(B, S, D)
```

```python
from contextlib import ExitStack

import numpy as np

import concourse.bass as bass
from concourse import mybir

F32 = mybir.dt.float32
F16 = mybir.dt.float16
BF16 = mybir.dt.bfloat16
I32 = mybir.dt.int32
ALU = mybir.AluOpType
ACT = mybir.ActivationFunctionType
AX = mybir.AxisListType

P = 128
B, S, D, H, SK = 4, 1024, 512, 16, 64
DK = D // H
KB = D // P
TOKENS = B * S
TILES = TOKENS // P
TB = S // P
PAIRS = H // 2
QUADS = H // 4
VW = 2 * DK + 2
E = 8
PLACES = E + 1
TOPK = 2
SLOTS = (TOKENS * TOPK + E * (P - 1)) // P
PADS = SLOTS - TOKENS * TOPK // P
WSCALE = 16.0
EPS = 1e-5
EARLY = 4
META = 24
ROW = D + META
XROW = 2 * D
HI, LO = 0, 1
PRODUCTS = ((HI, HI), (HI, LO), (LO, HI))


def build_program(nc, x, ctxT, tau, delta, wqT, wkT, wvT, woT, bq, bk, bv, bo,
                  gateT, ffn_w, up_b, down_b, out):
    ctx = ExitStack()
    with ctx:
        def sb(name, shape, dt=F32):
            return ctx.enter_context(nc.sbuf_tensor(name, shape, dt))

        def sem(name):
            return ctx.enter_context(nc.semaphore(name))

        xrows = nc.dram_tensor("xrows", [TILES, P, XROW], F32).ap()
        sorted_rows = nc.dram_tensor("sorted_rows", [SLOTS * P, ROW], F32).ap()

        PLACE_W = 4 * KB * D // 2
        ATT0 = EARLY * PLACE_W
        FFN0 = PLACES * PLACE_W
        ARENA = 51620
        arena = sb("arena", [P, ARENA])
        small = sb("small", [P, 1300])
        cuts = {"small": 0}

        def cut(tensor, key, words, dt=F32):
            a = cuts[key]
            cuts[key] = a + words
            v = tensor[:, a:a + words]
            return v if dt == F32 else v.bitcast(dt)

        def keep(words, dt=F32):
            return cut(small, "small", words, dt)

        weights = arena[:, 0:FFN0].bitcast(F16).rearrange(
            "p (e m h k n) -> p e m h k n", e=PLACES, m=2, h=2, k=KB)
        ident = keep(P // 2, F16)
        zero_row = keep(ROW)
        logits = keep(TILES * E).rearrange("p (t e) -> p t e", e=E)
        slot_place = keep(SLOTS, I32)
        pad_pos = keep(PADS, I32)
        gate = keep(2 * KB * E // 2, F16).rearrange("p (h k e) -> p h k e", h=2, k=KB)
        tau_k = keep(B)
        bq_c = keep(KB)
        bk_c = keep(KB)
        upb = keep(PLACES * KB)
        stat1 = keep(2 * 6).rearrange("p (i c) -> p i c", i=2)
        mv1 = keep(2 * 2).rearrange("p (i c) -> p i c", i=2)
        rstd1 = keep(2)
        root1 = keep(2 * 2).rearrange("p (i c) -> p i c", i=2)
        root2 = keep(2).rearrange("p (i c) -> p i c", i=1)
        eps_c = keep(1)
        stat2 = keep(6)
        mv2 = keep(2)
        rstd2 = keep(1)
        rowmax = keep(2 * H).rearrange("p (i h) -> p i h", i=2)
        rden = keep(H)
        ones3 = keep(P // 2, BF16)[0:3, :]

        cuts["att"] = ATT0

        def att(words, dt=F32):
            return cut(arena, "att", words, dt)

        wq = att(KB * D, F16).rearrange("p (h k n) -> p h k n", h=2, k=KB)
        wo = att(KB * D, F16).rearrange("p (h k n) -> p h k n", h=2, k=KB)
        kblk = att(B * QUADS * 4 * SK).rearrange("p (b g n) -> p b g n", b=B, g=QUADS)
        vblk = att(B * PAIRS * VW, F16).rearrange("p (h b r n) -> p h b r n", h=2, b=B, r=PAIRS)
        delta3 = att(B * SK // 2, BF16)[0:3, :].rearrange("p (b n) -> p b n", b=B)
        bo_b = att(D)
        shb_b = att(D)
        xT = att(2 * KB * S // 2, F16).rearrange("p (h k t) -> p h k t", h=2, k=KB)
        qT = att(2 * KB * 4 * P).rearrange("p (i k t) -> p i k t", i=2, k=KB)
        xin = att(2 * D).rearrange("p (i n) -> p i n", i=2)
        xn1 = att(2 * D).rearrange("p (i n) -> p i n", i=2)
        xhl = att(2 * D, F16).rearrange("p (i h n) -> p i h n", i=2, h=2)
        x_first = arena[:, cuts["att"]:cuts["att"] + TB * D].rearrange("p (t n) -> p t n", t=TB)
        prob = att(2 * H * SK).rearrange("p (i n) -> p i n", i=2)
        phl = att(2 * H * SK, F16).rearrange("p (i h n) -> p i h n", i=2, h=2)
        assert TB * D <= 4 * H * SK
        pT = att(H * SK, F16).rearrange("p (h r t) -> p h r t", h=2, r=PAIRS)
        xres = att(2 * D).rearrange("p (i n) -> p i n", i=2)
        att_o = att(D)
        ohl = att(D, F16).rearrange("p (h n) -> p h n", h=2)
        oT = att(D, F16).rearrange("p (h k t) -> p h k t", h=2, k=KB)
        xrow = att(2 * XROW).rearrange("p (i n) -> p i n", i=2)
        xn2 = att(D)
        nT = att(D, F16).rearrange("p (h k t) -> p h k t", h=2, k=KB)
        wstage = att(2 * D).rearrange("p (i n) -> p i n", i=2)
        assert cuts["att"] <= ARENA, cuts["att"]

        cuts["pro"] = 0

        def pro(words, dt=F32):
            return cut(arena, "pro", words, dt)

        wk_f = pro(KB * D).rearrange("p (k n) -> p k n", k=KB)
        wv_f = pro(KB * D).rearrange("p (k n) -> p k n", k=KB)
        wq_f = pro(KB * D).rearrange("p (k n) -> p k n", k=KB)
        wo_f = pro(KB * D).rearrange("p (k n) -> p k n", k=KB)
        gate_f = pro(KB * E).rearrange("p (k e) -> p k e", k=KB)
        ctx_f = pro(KB * B * SK).rearrange("p (k b n) -> p k b n", k=KB, b=B)
        ctx_2 = pro(KB * B * 2 * SK).rearrange("p (k b d n) -> p k b d n", k=KB, b=B, d=2)
        k_f = pro(KB * B * SK).rearrange("p (k b n) -> p k b n", k=KB, b=B)
        v_f = pro(B * D).rearrange("p (b r n) -> p b r n", b=B, r=PAIRS)
        bv_b = pro(D)
        tau_b = pro(B)
        delta_f = pro(B * SK)
        delta_p = pro(B * SK // 2, BF16)
        delta_s = pro(B * SK)
        HALF = TB // 2
        FIRST = TB + 1
        stat0 = pro(FIRST * 6).rearrange("p (t c) -> p t c", t=FIRST)
        mv0 = pro(FIRST * 2).rearrange("p (t c) -> p t c", t=FIRST)
        root0 = pro(3 * FIRST).rearrange("p (c t) -> p c t", c=3)
        assert cuts["pro"] <= ATT0

        cuts["ffn"] = FFN0

        def ffn(words, dt=F32):
            return cut(arena, "ffn", words, dt)

        downb = ffn(PLACES * D).rearrange("p (e n) -> p e n", e=PLACES)
        NROW, NSLOT = 3, 6
        RBUF = ROW + TOPK
        cuts["shared"] = cuts["ffn"]
        slots = ffn(NSLOT * ROW).rearrange("p (i n) -> p i n", i=NSLOT)
        wbias = ffn(D)
        def shared(words):
            return cut(arena, "shared", words)

        x1_rows = shared(NROW * D).rearrange("p (i n) -> p i n", i=NROW)
        rows = shared(NROW * D).rearrange("p (i n) -> p i n", i=NROW)
        estage = shared(2 * D).rearrange("p (i n) -> p i n", i=2)
        cuts["ffn"] = max(cuts["ffn"], cuts["shared"])
        sc_rows = ffn(NROW * RBUF).rearrange("p (i n) -> p i n", i=NROW)
        eT = ffn(2 * D, F16).rearrange("p (i h k t) -> p i h k t", i=2, h=2, k=KB)
        hid = ffn(D)
        hhl = ffn(2 * D, F16).rearrange("p (i h n) -> p i h n", i=2, h=2)
        yout = ffn(2 * D).rearrange("p (i n) -> p i n", i=2)
        meta = ffn(TILES * (META + 2)).rearrange("p (t n) -> p t n", t=TILES)
        cuts["rt"] = (PLACES - 2) * PLACE_W

        def rt(a=TILES, c=E, dt=F32):
            v = cut(arena, "rt", a * c // (2 if dt == F16 else 1), dt)
            return v.rearrange("p (a c) -> p a c", a=a) if c > 1 else v

        assert cuts["ffn"] <= ARENA, cuts["ffn"]

        def parts(row):
            return row[:, 0:D].bitcast(F16).rearrange("p (h n) -> p h n", h=2)

        psum = ctx.enter_context(nc.psum_tensor("psum", [P, 8, 512], F32))
        scores_ps = psum[:, 0:2, :].rearrange("p a n -> p (a n)")
        probT_ps = psum[:, 2:4, :].rearrange("p a n -> p (a n)").bitcast(F16).rearrange(
            "p (h r t) -> p h r t", h=2, r=PAIRS)
        att_ps = psum[:, 4:6, :].rearrange("p a n -> p (a n)").rearrange("p (r n) -> p r n", r=PAIRS)
        gate_ps = psum[:, 4, VW:VW + E]
        turn_ps = psum[:, 6, :]
        turn16_ps = turn_ps.bitcast(F16).rearrange("p (h k t) -> p h k t", h=2, k=KB)
        proj_ps = psum[:, 7, :]
        first_q_ps = (proj_ps, psum[:, 5, :])
        eturn16_ps = [psum[:, 0 + i, :].bitcast(F16).rearrange("p (h k t) -> p h k t", h=2, k=KB) for i in range(2)]
        up_ps = [psum[:, 2 + i, :] for i in range(2)]
        down_ps = [psum[:, 4 + i, :] for i in range(2)]

        def s2(name):
            return [sem(f"{name}0"), sem(f"{name}1")]

        ident_cleared, id_ready, consts_ready = sem("ident_cleared"), sem("id_ready"), sem("consts_ready")
        tau_loaded = sem("tau_loaded")
        v_loaded, wo_split = sem("v_loaded"), sem("wo_split")
        kv_loaded, q_loaded, small_loaded, o_loaded = (
            sem("kv_loaded"), sem("q_loaded"), sem("small_loaded"), sem("o_loaded"))
        ctx2_ready, k_mm, k_read, kblk_ready, v_mm, v_read = (
            sem("ctx2_ready"), sem("k_mm"), sem("k_read"), sem("kblk_ready"), sem("v_mm"), sem("v_read"))
        vblk_ready, pro_dve, w_scaled, w_hi_ready, w_split, tau_ready, delta_ready, cleared = (
            sem("vblk_ready"), sem("pro_dve"), sem("w_scaled"), sem("w_hi_ready"), sem("w_split"),
            sem("tau_ready"), sem("delta_ready"), sem("cleared"))
        first_loaded = s2("first_loaded")
        first_stats, first_mv, first_log, first_guess, first_steps, first_rstd = (
            sem("first_stats"), sem("first_mv"), sem("first_log"), sem("first_guess"), sem("first_steps"),
            sem("first_rstd"))
        trash_zeroed = sem("trash_zeroed")
        xin_loaded = s2("xin_loaded")
        ln1_stats, ln1_mv, ln1_rstd, ln1_done = sem("ln1_stats"), sem("ln1_mv"), sem("ln1_rstd"), sem("ln1_done")
        ln1_guess, ln1_steps, ln2_guess, ln2_steps, ln1_log, ln2_log = (
            sem("ln1_guess"), sem("ln1_steps"), sem("ln2_guess"), sem("ln2_steps"), sem("ln1_log"), sem("ln2_log"))
        xhi_done, xlo_done, xturn_done, xT_ready = sem("xhi_done"), sem("xlo_done"), sem("xturn_done"), sem("xT_ready")
        q_mm, q_ready = sem("q_mm"), sem("q_ready")
        scores_done, max_done, sub_done, exp_done, plo_done = (
            sem("scores_done"), sem("max_done"), sem("sub_done"), sem("exp_done"), sem("plo_done"))
        pturn_done, pT_ready, att_done, rden_done, norm_done = (
            sem("pturn_done"), sem("pT_ready"), sem("att_done"), sem("rden_done"), sem("norm_done"))
        ohi_done, olo_done, oturn_done, oT_ready, proj_done = (
            sem("ohi_done"), sem("olo_done"), sem("oturn_done"), sem("oT_ready"), sem("proj_done"))
        xres_loaded = s2("xres_loaded")
        xres_biased, x1_done, ln2_stats, ln2_mv, ln2_rstd, ln2_done = (
            sem("xres_biased"), sem("x1_done"), sem("ln2_stats"), sem("ln2_mv"), sem("ln2_rstd"), sem("ln2_done"))
        nhi_done, nlo_done, nturn_done, nT_ready, gate_done, logits_ready = (
            sem("nhi_done"), sem("nlo_done"), sem("nturn_done"), sem("nT_ready"), sem("gate_done"), sem("logits_ready"))
        xrow_stored, xrow_ready = s2("xrow_stored"), sem("xrow_ready")
        wstage_loaded = s2("wstage_loaded")
        wst_hi, wst_split = sem("wst_hi"), sem("wst_split")

        passed = sem("passed")

        def settled(eng):
            eng.sem_inc(passed, 1)

        def tiled(b, c):
            return b * TB + c

        def bodies(eng, n, body):
            body(0, True, False)
            with eng.Fori(1, n - 1) as b:
                body(b, False, False)
            body(n - 1, False, True)

        def batches(eng, batch):
            batch(0, True, False)
            with eng.Fori(1, B - 1) as b:
                batch(b, False, False)
            batch(B - 1, False, True)

        def there(first, last, t):
            return not (first and t < 0) and not (last and t >= TB)

        def transposes(eng, dst, src_hi_lo, n):
            for h in range(2):
                for k in range(n):
                    last = eng.transpose(dst[:, h, k, :], src_hi_lo[:, h, k * P:(k + 1) * P], ident)
            return last

        def split_products(eng, dst, lhs, rhs):
            n = 0
            for k in range(KB):
                for a, c in PRODUCTS:
                    last = eng.matmul(dst, lhs(a, k), rhs(c, k), start=(n == 0), stop=(n == 3 * KB - 1))
                    n += 1
            return last

        def bcast_rows(ap, n):
            return ap.rearrange("(o n) -> o n", o=1).to_broadcast([n, ap.shape[0]])

        with nc.Block() as block:

            @block.sync
            def _(sp):
                sp.dma_start(x_first[:, 0:HALF, :], x[0:HALF].rearrange("t p n -> p t n")).then_inc(first_loaded[0], 16)
                sp.dma_start(x_first[:, HALF:, :], x[HALF:TB].rearrange("t p n -> p t n")).then_inc(first_loaded[1], 16)
                sp.dma_start(xin[:, 0, :], x[TB]).then_inc(xin_loaded[0], 16)
                sp.dma_start(ctx_f, ctxT.rearrange("(k p) (b n) -> p k b n", p=P, b=B)).then_inc(kv_loaded, 16)
                sp.dma_start(wk_f, wkT.rearrange("(k p) n -> p k n", p=P)).then_inc(kv_loaded, 16)
                sp.dma_start(wv_f, wvT.rearrange("(k p) n -> p k n", p=P)).then_inc(v_loaded, 16)
                sp.dma_start(wq_f, wqT.rearrange("(k p) n -> p k n", p=P)).then_inc(q_loaded, 16)
                sp.dma_start(wo_f, woT.rearrange("(k p) n -> p k n", p=P)).then_inc(o_loaded, 16)
                sp.dma_start(xin[:, 1, :], x[TB + 1]).then_inc(xin_loaded[1], 16)
                sp.dma_start(xres[:, 0, :], x[0]).then_inc(xres_loaded[0], 16)
                sp.dma_start(wstage[:, 0, :], ffn_w[0, 0, 0:P, :]).then_inc(wstage_loaded[0], 16)

                def load_x(b, c):
                    sp.wait_ge(ln1_done, tiled(b, c - 1))
                    tile = tiled(b, c)
                    if c == 2 * TB:
                        tile = (b + 2) % B * TB
                    sp.dma_start(xin[:, c % 2, :], x[bass.ds(tile, 1)].rearrange("o p n -> p (o n)")
                                 ).then_inc(xin_loaded[c % 2], 16)

                def batch(b, first, last):
                    if not first and not last:
                        load_x(b, TB + 1)
                    for t in range(TB + last):
                        if there(first, last, t + 1):
                            sp.wait_ge(x1_done, tiled(b, t))
                            sp.dma_start(xres[:, (t + 1) % 2, :],
                                         x[bass.ds(tiled(b, t + 1), 1)].rearrange("o p n -> p (o n)")
                                         ).then_inc(xres_loaded[(t + 1) % 2], 16)
                            sp.wait_ge(wst_split, tiled(b, t))
                            c = (t + 1) % TB
                            sp.dma_start(wstage[:, (t + 1) % 2, :],
                                         ffn_w[bass.ds(b + (t + 1) // TB, 1), c // KB,
                                               (c % KB) * P:(c % KB + 1) * P, :].rearrange("o p n -> p (o n)")
                                         ).then_inc(wstage_loaded[(t + 1) % 2], 16)
                        if not last and t + 2 <= TB:
                            load_x(b, TB + t + 2)
                        if there(first, last, t - 1):
                            sp.wait_ge(xrow_ready, tiled(b, t))
                            sp.dma_start(xrows[bass.ds(tiled(b, t - 1), 1)].rearrange("o p n -> p (o n)"),
                                         xrow[:, (t - 1) % 2, :]).then_inc(xrow_stored[(t - 1) % 2], 16)

                batches(sp, batch)
                sp.wait_ge(xrow_stored[0], 16 * TILES // 2)
                sp.wait_ge(xrow_stored[1], 16 * TILES // 2)
                sp.wait_ge(trash_zeroed, 16)

            @block.scalar
            def _(act):
                def guess(i, count, mv, root, mv_done, log_done, done):
                    act.wait_ge(mv_done, count)
                    y = root[:, i, 0:1]
                    act.activation(y, mv, ACT.Ln, bias=eps_c).then_inc(log_done, 1)
                    act.wait_ge(log_done, count)
                    act.activation(y, y, ACT.Exp, scale=-0.5).then_inc(done, 1)

                def guess_1(i, count):
                    guess(i, count, mv1[:, i, 1:2], root1, ln1_mv, ln1_log, ln1_guess)

                def guess_2(count):
                    guess(0, count, mv2[:, 1:2], root2, ln2_mv, ln2_log, ln2_guess)

                act.preload_act_table_set("natural_log_exp_and_others")
                act.dma_start(tau_b, bcast_rows(tau, P)).then_inc(tau_loaded, 16)
                act.dma_start(delta_f[0:3, :], bcast_rows(delta, 3)).then_inc(tau_loaded, 16)
                act.dma_start(bq_c, bq).then_inc(tau_loaded, 16)
                act.dma_start(bk_c, bk).then_inc(tau_loaded, 16)
                act.dma_start(upb, up_b).then_inc(small_loaded, 16)
                act.dma_start(gate_f, gateT.rearrange("(k p) e -> p k e", p=P)).then_inc(small_loaded, 16)
                act.dma_start(bv_b, bcast_rows(bv, P)).then_inc(small_loaded, 16)
                act.dma_start(bo_b, bcast_rows(bo, P)).then_inc(small_loaded, 16)
                act.dma_start(shb_b, bcast_rows(down_b[0], P)).then_inc(small_loaded, 16)
                act.wait_ge(consts_ready, 5)
                act.dma_start(out[TOKENS:TOKENS + P, :], zero_row[:, 0:D]).then_inc(trash_zeroed, 16)

                act.wait_ge(first_mv, FIRST)
                act.wait_ge(consts_ready, 5)
                act.activation(root0[:, 0, :], mv0[:, :, 1], ACT.Ln, bias=eps_c).then_inc(first_log, 1)
                act.wait_ge(first_log, 1)
                act.activation(root0[:, 0, :], root0[:, 0, :], ACT.Exp, scale=-0.5).then_inc(first_guess, 1)

                def x_hi(m, count):
                    act.wait_ge(ln1_done, count(1))
                    if m >= 2:
                        act.wait_ge(xturn_done, count(-1))
                    src = x_first[:, m, :] if m < TB else xn1[:, m % 2, :]
                    act.activation(xhl[:, m % 2, HI, :], src, ACT.Copy).then_inc(xhi_done, 1)

                def x_turned(m, count, q_count=None):
                    act.wait_ge(xturn_done, count(1))
                    if q_count is not None:
                        act.wait_ge(q_mm, q_count)
                    c = m % TB
                    act.activation(xT[:, :, :, c * P:(c + 1) * P], turn16_ps, ACT.Copy).then_inc(xT_ready, 1)

                def q_out(q, count, s_count=None, src=proj_ps):
                    act.wait_ge(q_mm, count)
                    if s_count is not None:
                        act.wait_ge(scores_done, s_count)
                    act.activation(qT[:, (q // KB) % 2, q % KB, :], src, ACT.Identity,
                                   bias=bq_c[:, q % KB:q % KB + 1], scale=1.0 / WSCALE).then_inc(q_ready, 1)

                def exps(i, count, pt_count=None):
                    act.wait_ge(sub_done, count)
                    if pt_count is not None:
                        act.wait_ge(pturn_done, pt_count)
                    act.activation(phl[:, i, HI, :], prob[:, i, :], ACT.Exp)
                    act.activation(prob[:, i, :], prob[:, i, :], ACT.Exp).then_inc(exp_done, 1)

                def k_out(g):
                    act.wait_ge(tau_loaded, 64)
                    act.wait_ge(k_mm, g + 1)
                    act.activation(k_f[:, g], psum[:, g % 2, 0:B * SK].rearrange("p (b n) -> p b n", b=B),
                                   ACT.Identity, bias=bk_c[:, g:g + 1]).then_inc(k_read, 1)

                x_hi(0, lambda c: 0 + c)
                x_hi(1, lambda c: 1 + c)
                for m in range(TB):
                    if m == KB:
                        act.wait_ge(small_loaded, 80)
                        act.activation(gate[:, HI], gate_f, ACT.Copy, scale=WSCALE).then_inc(w_hi_ready, 1)
                        act.wait_ge(q_loaded, 16)
                        act.activation(wq[:, HI], wq_f, ACT.Copy, scale=WSCALE).then_inc(w_hi_ready, 1)
                    x_turned(m, lambda c, m=m: m + c)
                    if m + 2 < FIRST:
                        x_hi(m + 2, lambda c, m=m: m + 2 + c)
                    if m < KB:
                        k_out(m)
                for q in range(KB + 1):
                    q_out(q, q + 1, src=first_q_ps[q % 2])
                exps(0, 1)
                act.wait_ge(o_loaded, 16)
                act.activation(wo[:, HI], wo_f, ACT.Copy, scale=WSCALE)
                act.activation(wo_f, wo_f, ACT.Copy, scale=WSCALE).then_inc(w_scaled, 1)
                act.wait_ge(vblk_ready, B)
                act.wait_ge(kblk_ready, KB)
                act.wait_ge(w_split, 2)

                def batch(b, first, last):
                    for t in range(TB + 2 * last):
                        if there(first, last, t):
                            act.wait_ge(pturn_done, tiled(b, t + 1))
                            act.wait_ge(att_done, tiled(b, t))
                            act.activation(pT, probT_ps, ACT.Copy).then_inc(pT_ready, 1)
                        if there(first, last, t - 2):
                            act.wait_ge(nturn_done, tiled(b, t - 1))
                            act.activation(nT, turn16_ps, ACT.Copy).then_inc(nT_ready, 1)
                        if there(first, last, t + 1):
                            exps((t + 1) % 2, tiled(b, t + 2))
                        if there(first, last, t - 1):
                            guess_2(tiled(b, t))
                        if not last:
                            x_turned(t, lambda c, t=t: tiled(b, TB + t + c), tiled(b, 4 * (t // 4) + 4))
                        if there(first, last, t):
                            if first and t == 1:
                                act.wait_ge(wo_split, 1)
                            act.wait_ge(wstage_loaded[t % 2], b * 64 + 16 * (t // 2 + 1))
                            w = weights[:, bass.ds(b, 1), t // KB, HI, t % KB, :].rearrange("p o n -> p (o n)")
                            act.activation(w, wstage[:, t % 2, :], ACT.Copy, scale=WSCALE).then_inc(wst_hi, 1)
                        q = t + KB + 1
                        if there(first, last, q) and t % 4 != 3:
                            q_out(q, tiled(b, q + 1), tiled(b, 4 * (q // KB) - 4))
                        if there(first, last, t - 1):
                            act.wait_ge(ln2_done, tiled(b, t))
                            act.activation(xrow[:, (t - 1) % 2, D:].bitcast(F16)[:, 0:D], xn2, ACT.Copy
                                           ).then_inc(nhi_done, 1)
                        if there(first, last, q) and t % 4 == 3:
                            q_out(q, tiled(b, q + 1), tiled(b, 4 * (q // KB) - 4))
                        if not last:
                            guess_1((t + 1) % 2, tiled(b, t + 1))
                        if there(first, last, t):
                            act.wait_ge(oturn_done, tiled(b, t + 1))
                            act.activation(oT, turn16_ps, ACT.Copy).then_inc(oT_ready, 1)
                        if there(first, last, t - 2):
                            act.wait_ge(gate_done, tiled(b, t - 1))
                            act.activation(logits[:, bass.ds(tiled(b, t - 2), 1), :].rearrange("p o e -> p (o e)"),
                                           gate_ps, ACT.Copy, scale=1.0 / WSCALE).then_inc(logits_ready, 1)
                        if not last:
                            x_hi(TB + t + 1, lambda c, t=t: tiled(b, TB + t + 1 + c))

                batches(act, batch)

            @block.gpsimd
            def _(pool):
                pool.memset(ident, 0.0).then_inc(ident_cleared, 1)
                pool.wait_ge(ident_cleared, 1)
                pool.affine_select(out=ident, in_=ident, compare_op=ALU.not_equal, fill=1.0, base=0,
                                   pattern=[[-1, P]], channel_multiplier=1).then_inc(id_ready, 1)
                pool.iota(zero_row[:, D:D + 1].bitcast(I32), pattern=[[0, 1]], base=TOKENS,
                          channel_multiplier=1).then_inc(consts_ready, 1)

                def x_lo(m, count):
                    pool.wait_ge(xhi_done, count(1))
                    src = x_first[:, m, :] if m < TB else xn1[:, m % 2, :]
                    pool.tensor_tensor(xhl[:, m % 2, LO, :], src, xhl[:, m % 2, HI, :],
                                       ALU.subtract).then_inc(xlo_done, 1)

                def p_lo(i, count):
                    pool.wait_ge(exp_done, count)
                    pool.tensor_tensor(phl[:, i, LO, :], prob[:, i, :], phl[:, i, HI, :],
                                       ALU.subtract).then_inc(plo_done, 1)

                pool.memset(v_f, 0.0).then_inc(cleared, 1)
                pool.memset(kblk, 0.0).then_inc(cleared, 1)
                pool.wait_ge(cleared, 2)
                for m in range(FIRST):
                    x_lo(m, lambda c, m=m: m + c)
                p_lo(0, 1)
                pool.wait_ge(w_scaled, 1)
                pool.tensor_tensor(wo[:, LO], wo_f, wo[:, HI], ALU.subtract).then_inc(wo_split, 1)

                def batch(b, first, last):
                    for t in range(TB + last):
                        if there(first, last, t):
                            pool.wait_ge(xres_loaded[t % 2], b * 64 + 16 * (t // 2 + 1))
                            pool.tensor_tensor(xres[:, t % 2, :], xres[:, t % 2, :], bo_b, ALU.add
                                               ).then_inc(xres_biased, 1)
                        if there(first, last, t + 1):
                            p_lo((t + 1) % 2, tiled(b, t + 2))
                        if there(first, last, t - 1):
                            pool.wait_ge(nhi_done, tiled(b, t))
                            hl = xrow[:, (t - 1) % 2, D:].bitcast(F16)
                            pool.tensor_tensor(hl[:, D:], xn2, hl[:, 0:D], ALU.subtract).then_inc(nlo_done, 1)
                            x1 = xrow[:, (t - 1) % 2, 0:D]
                            pool.tensor_tensor(x1, x1, shb_b, ALU.add).then_inc(xrow_ready, 1)
                        if not last:
                            x_lo(TB + t + 1, lambda c, t=t: tiled(b, TB + t + 1 + c))

                batches(pool, batch)

            @block.vector
            def _(dve):
                dve.memset(zero_row[:, 0:D], 0.0).then_inc(consts_ready, 1)
                dve.memset(zero_row[:, D + 1:], 0.0).then_inc(consts_ready, 1)
                dve.memset(ones3, 1.0).then_inc(consts_ready, 1)
                dve.memset(eps_c, EPS).then_inc(consts_ready, 1)

                def stats1(m, count, loaded):
                    dve.wait_ge(xin_loaded[m % 2], loaded)
                    dve.bn_stats(stat1[:, m % 2, :], xin[:, m % 2, :]).then_inc(ln1_stats, 1)
                    dve.wait_ge(ln1_stats, count)
                    settled(dve)
                    dve.bn_aggr(mv1[:, m % 2, :], stat1[:, m % 2, :]).then_inc(ln1_mv, 1)

                def newton(dst, count, var, root, i, guess_done, steps_done, done):
                    y, u = root[:, i, 0:1], root[:, i, 1:2]
                    dve.wait_ge(guess_done, count)
                    dve.scalar_tensor_tensor(out=u, in0=var, scalar=EPS, in1=y, op0=ALU.add, op1=ALU.mult
                                             ).then_inc(steps_done, 1)
                    dve.wait_ge(steps_done, count * 2 - 1)
                    dve.tensor_scalar(u, u, y, -0.5, ALU.mult, ALU.mult).then_inc(steps_done, 1)
                    dve.wait_ge(steps_done, count * 2)
                    dve.scalar_tensor_tensor(out=dst, in0=u, scalar=1.5, in1=y, op0=ALU.add, op1=ALU.mult
                                             ).then_inc(done, 1)

                def norm1(m, count, tile):
                    i = m % 2
                    newton(rstd1[:, i:i + 1], count, mv1[:, i, 1:2], root1, i, ln1_guess, ln1_steps, ln1_rstd)
                    dve.wait_ge(ln1_rstd, count)
                    dve.wait_ge(xlo_done, tile - 1)
                    dve.tensor_scalar(xn1[:, i, :], xin[:, i, :], mv1[:, i, 0:1],
                                      rstd1[:, i:i + 1], ALU.subtract, ALU.mult).then_inc(ln1_done, 1)

                def max_sub(i, count, lo_count=None):
                    s3 = scores_ps.rearrange("p (h k) -> p h k", h=H)
                    dve.wait_ge(scores_done, count)
                    dve.tensor_reduce(rowmax[:, i, :], s3, AX.X, ALU.max).then_inc(max_done, 1)
                    dve.wait_ge(max_done, count)
                    if lo_count is not None:
                        dve.wait_ge(plo_done, lo_count)
                    dve.tensor_tensor(prob[:, i, :].rearrange("p (h k) -> p h k", h=H), s3,
                                      rowmax[:, i, :].unsqueeze(2).to_broadcast([P, H, SK]),
                                      ALU.subtract).then_inc(sub_done, 1)

                def first_tile(m):
                    return x_first[:, m, :] if m < TB else xin[:, 0, :]

                for m in range(FIRST):
                    if m % HALF == 0 and m < TB:
                        dve.wait_ge(first_loaded[m // HALF], 16)
                    elif m == TB:
                        dve.wait_ge(xin_loaded[0], 16)
                    dve.bn_stats(stat0[:, m, :], first_tile(m)).then_inc(first_stats, 1)
                for m in range(FIRST):
                    dve.wait_ge(first_stats, m + 1)
                    dve.bn_aggr(mv0[:, m, :], stat0[:, m, :]).then_inc(first_mv, 1)
                dve.wait_ge(first_guess, 1)
                guess, term, root = root0[:, 0, :], root0[:, 1, :], root0[:, 2, :]
                dve.scalar_tensor_tensor(out=term, in0=mv0[:, :, 1], scalar=EPS, in1=guess, op0=ALU.add, op1=ALU.mult
                                         ).then_inc(first_steps, 1)
                dve.wait_ge(first_steps, 1)
                dve.tensor_tensor(term, term, guess, ALU.mult).then_inc(first_steps, 1)
                dve.wait_ge(first_steps, 2)
                dve.tensor_scalar(term, term, -0.5, 1.5, ALU.mult, ALU.add).then_inc(first_steps, 1)
                dve.wait_ge(first_steps, 3)
                dve.tensor_tensor(root, term, guess, ALU.mult).then_inc(first_rstd, 1)
                dve.wait_ge(first_rstd, 1)
                for m in range(FIRST):
                    dst = x_first[:, m, :] if m < TB else xn1[:, 0, :]
                    dve.tensor_scalar(dst, first_tile(m), mv0[:, m, 0:1], root[:, m:m + 1], ALU.subtract, ALU.mult
                                      ).then_inc(ln1_done, 1)

                steps = 0

                def step(instruction):
                    nonlocal steps
                    steps += 1
                    instruction.then_inc(pro_dve, 1)
                    dve.wait_ge(pro_dve, steps)

                step(dve.memset(vblk[:, :, :, :, 2 * DK:], 0.0))
                step(dve.memset(vblk[0:SK, HI, :, :, 2 * DK], WSCALE))
                step(dve.memset(vblk[SK:P, HI, :, :, 2 * DK + 1], WSCALE))
                dve.wait_ge(tau_loaded, 64)
                dve.tensor_scalar(tau_k, tau_b, float(DK) ** -0.5, None, ALU.mult).then_inc(tau_ready, 1)
                dve.wait_ge(id_ready, 1)
                step(dve.tensor_scalar(delta_f[0:3], delta_f[0:3], float(DK) ** -0.5, None, ALU.mult))
                for i in range(3):
                    step(dve.tensor_copy(delta_p[0:3], delta_f[0:3]))
                    step(dve.tensor_tensor(delta_f[0:3], delta_f[0:3], delta_p[0:3], ALU.subtract))
                    if i == 0:
                        step(dve.tensor_scalar(delta_s[0:3], delta_p[0:3], ident[0:3, 0:1], None, ALU.mult))
                    else:
                        step(dve.scalar_tensor_tensor(out=delta_s[0:3], in0=delta_p[0:3],
                                                      scalar=ident[0:3, i:i + 1], in1=delta_s[0:3],
                                                      op0=ALU.mult, op1=ALU.add))
                dve.tensor_copy(delta3.rearrange("p b n -> p (b n)"), delta_s[0:3]).then_inc(delta_ready, 1)
                dve.wait_ge(kv_loaded, 32)
                for d in range(2):
                    dve.tensor_copy(ctx_2[:, :, :, d, :], ctx_f).then_inc(ctx2_ready, 1)

                def w_lo(dst, src, hi, n):
                    dve.wait_ge(w_hi_ready, n)
                    dve.scalar_tensor_tensor(out=dst, in0=src, scalar=WSCALE, in1=hi, op0=ALU.mult, op1=ALU.subtract
                                             ).then_inc(w_split, 1)

                dve.wait_ge(cleared, 2)
                dve.wait_ge(tau_ready, 1)
                for g in range(QUADS):
                    dve.wait_ge(k_read, g + 1)
                    for j in range(4):
                        r = slice(j * DK, (j + 1) * DK)
                        ins = dve.tensor_tensor(kblk[r, :, g, j * SK:(j + 1) * SK], k_f[r, g],
                                                tau_k[r, :].unsqueeze(2).to_broadcast([DK, B, SK]), ALU.mult)
                    ins.then_inc(kblk_ready, 1)
                for b in range(B):
                    if b == 0:
                        dve.wait_ge(small_loaded, 80)
                    if b == 2:
                        w_lo(gate[:, LO], gate_f, gate[:, HI], 1)
                        w_lo(wq[:, LO], wq_f, wq[:, HI], 2)
                    dve.wait_ge(v_mm, b + 1)
                    for j in range(2):
                        r, c = slice(j * SK, (j + 1) * SK), slice(j * DK, (j + 1) * DK)
                        ins = dve.tensor_tensor(
                            v_f[r, b, :, c], psum[r, 2 + b % 2, :].rearrange("p (r n) -> p r n", r=PAIRS)[:, :, c],
                            bv_b[r].rearrange("p (r n) -> p r n", r=PAIRS)[:, :, c], ALU.add)
                        if j == 1:
                            ins.then_inc(v_read, 1)
                    dve.wait_ge(v_read, b + 1)
                    hi, lo = vblk[:, HI, b, :, 0:2 * DK], vblk[:, LO, b, :, 0:2 * DK]
                    step(dve.tensor_scalar(hi, v_f[:, b], WSCALE, None, ALU.mult))
                    ins = dve.scalar_tensor_tensor(out=lo, in0=v_f[:, b], scalar=WSCALE, in1=hi,
                                                   op0=ALU.mult, op1=ALU.subtract)
                    ins.then_inc(vblk_ready, 1)
                dve.wait_ge(xlo_done, TB)
                max_sub(0, 1)

                def batch(b, first, last):
                    for t in range(TB + last):
                        if there(first, last, t + 1):
                            max_sub((t + 1) % 2, tiled(b, t + 2), tiled(b, t))
                        if there(first, last, t - 1):
                            i = (t - 1) % 2
                            dve.wait_ge(proj_done, tiled(b, t))
                            dve.wait_ge(xres_biased, tiled(b, t))
                            dve.wait_ge(xrow_stored[i], b * 64 + 16 * ((t - 1) // 2))
                            x1 = xrow[:, i, 0:D]
                            dve.scalar_tensor_tensor(out=x1, in0=proj_ps, scalar=1.0 / WSCALE, in1=xres[:, i, :],
                                                     op0=ALU.mult, op1=ALU.add).then_inc(x1_done, 1)
                            dve.wait_ge(x1_done, tiled(b, t))
                            dve.bn_stats(stat2, x1).then_inc(ln2_stats, 1)
                            dve.wait_ge(ln2_stats, tiled(b, t))
                            settled(dve)
                            dve.bn_aggr(mv2, stat2).then_inc(ln2_mv, 1)
                        if there(first, last, t):
                            dve.wait_ge(att_done, tiled(b, t + 1))
                            dve.reciprocal(rden.rearrange("p (r j) -> p r j", r=PAIRS),
                                           att_ps[:, :, 2 * DK:VW]).then_inc(rden_done, 1)
                            dve.wait_ge(rden_done, tiled(b, t + 1))
                            dve.tensor_tensor(att_o.rearrange("p (r j n) -> p r j n", r=PAIRS, j=2),
                                              att_ps[:, :, 0:2 * DK].rearrange("p r (j n) -> p r j n", j=2),
                                              rden.rearrange("p (r j) -> p r j", r=PAIRS).unsqueeze(3)
                                              .to_broadcast([P, PAIRS, 2, DK]), ALU.mult).then_inc(norm_done, 1)
                            dve.wait_ge(norm_done, tiled(b, t + 1))
                            dve.wait_ge(oturn_done, tiled(b, t))
                            dve.tensor_copy(ohl[:, HI, :], att_o).then_inc(ohi_done, 1)
                            dve.wait_ge(ohi_done, tiled(b, t + 1))
                            dve.tensor_tensor(ohl[:, LO, :], att_o, ohl[:, HI, :], ALU.subtract).then_inc(olo_done, 1)
                        if there(first, last, t - 1):
                            newton(rstd2, tiled(b, t), mv2[:, 1:2], root2, 0, ln2_guess, ln2_steps, ln2_rstd)
                            dve.wait_ge(ln2_rstd, tiled(b, t))
                            if not (first and t == 1):
                                dve.wait_ge(nlo_done, tiled(b, t - 1))
                            dve.tensor_scalar(xn2, x1, mv2[:, 0:1], rstd2, ALU.subtract, ALU.mult).then_inc(ln2_done, 1)
                        if not last:
                            m = TB + t + 1
                            stats1(m, tiled(b, t + 1), b * 64 + 16 * ((m - TB) // 2 + 1))
                        if there(first, last, t):
                            dve.wait_ge(wst_hi, tiled(b, t + 1))
                            w = [weights[:, bass.ds(b, 1), t // KB, h, t % KB, :].rearrange("p o n -> p (o n)")
                                 for h in range(2)]
                            dve.scalar_tensor_tensor(out=w[LO], in0=wstage[:, t % 2, :], scalar=WSCALE, in1=w[HI],
                                                     op0=ALU.mult, op1=ALU.subtract).then_inc(wst_split, 1)
                        if not last:
                            norm1(TB + t + 1, tiled(b, t + 1), tiled(b, TB + t + 1))

                batches(dve, batch)

            @block.tensor
            def _(pe):
                def scores(b, col, qi):
                    for a in range(2):
                        bank = scores_ps[:, a * 512:(a + 1) * 512]
                        for j in range(2):
                            g = 2 * a + j
                            pe.matmul(bank[:, j * 256:(j + 1) * 256], qT[:, qi, g, col:col + P],
                                      kblk[:, bass.ds(b, 1), g, :].rearrange("p o n -> p (o n)"),
                                      start=(j == 0), stop=False, skip_group_check=True)
                        last = pe.matmul(bank, ones3, delta3[:, bass.ds(b, 1), :].to_broadcast([3, PAIRS, SK]),
                                         start=False, stop=True, skip_group_check=True)
                    last.then_inc(scores_done, 1)

                def x_turn(m, count):
                    pe.wait_ge(xlo_done, count(1))
                    transposes(pe, turn16_ps, xhl[:, m % 2], KB).then_inc(xturn_done, 1)

                def project_q(q, dst=proj_ps):
                    half = (q // KB) % 2
                    split_products(pe, dst,
                                   lambda part, k: wq[:, part, k, (q % KB) * P:(q % KB + 1) * P],
                                   lambda part, k: xT[:, part, k, half * 512:(half + 1) * 512]).then_inc(q_mm, 1)

                pe.wait_ge(id_ready, 1)
                pe.wait_ge(consts_ready, 5)

                def keys(g):
                    if g == 0:
                        pe.wait_ge(kv_loaded, 32)
                    if g >= 2:
                        pe.wait_ge(k_read, g - 1)
                    for k in range(KB):
                        ins = pe.matmul(psum[:, g % 2, 0:B * SK], wk_f[:, k, g * P:(g + 1) * P],
                                        ctx_f[:, k].rearrange("p b n -> p (b n)"), start=(k == 0), stop=(k == KB - 1))
                    ins.then_inc(k_mm, 1)

                def values(b):
                    if b == 0:
                        pe.wait_ge(v_loaded, 16)
                        pe.wait_ge(ctx2_ready, 2)
                    if b >= 2:
                        pe.wait_ge(v_read, b - 1)
                    for k in range(KB):
                        ins = pe.matmul(psum[:, 2 + b % 2, :], ctx_2[:, k, b].rearrange("p d n -> p (d n)"),
                                        wv_f[:, k, :], start=(k == 0), stop=(k == KB - 1))
                    ins.then_inc(v_mm, 1)

                for m in range(TB):
                    if m >= 1:
                        pe.wait_ge(xT_ready, m)
                    x_turn(m, lambda c, m=m: m + c)
                    if m < KB:
                        keys(m)
                    else:
                        values(m - KB)
                pe.wait_ge(w_split, 2)
                for q in range(KB + 1):
                    pe.wait_ge(xT_ready, 4 if q < KB else TB)
                    if q >= 2:
                        pe.wait_ge(q_ready, q - 1)
                    if q == KB:
                        pe.wait_ge(q_ready, KB)
                        pe.wait_ge(kblk_ready, QUADS)
                        pe.wait_ge(delta_ready, 1)
                        pe.wait_ge(k_read, QUADS)
                        scores(0, 0, 0)
                    project_q(q, first_q_ps[q % 2])
                pe.wait_ge(vblk_ready, B)
                pe.wait_ge(sub_done, 1)
                scores(0, P, 0)

                def next_scores(b, first, last, c):
                    if there(first, last, c):
                        pe.wait_ge(q_ready, tiled(b, 4 * (c // 4) + 4))
                        pe.wait_ge(sub_done, tiled(b, c))
                        scores(b + c // TB, (c % 4) * P, (c // 4) % 2)

                def batch(b, first, last):
                    for t in range(TB + 2 * last):
                        if there(first, last, t):
                            pe.wait_ge(plo_done, tiled(b, t + 1))
                            pe.wait_ge(pT_ready, tiled(b, t))
                            transposes(pe, probT_ps, phl[:, t % 2], PAIRS).then_inc(pturn_done, 1)
                        if there(first, last, t - 2):
                            pe.wait_ge(nlo_done, tiled(b, t - 1))
                            pe.wait_ge(oT_ready, tiled(b, min(t, TB) if last else t))
                            hl = xrow[:, t % 2, D:].bitcast(F16).rearrange("p (h n) -> p h n", h=2)
                            transposes(pe, turn16_ps, hl, KB).then_inc(nturn_done, 1)
                        if there(first, last, t - 1):
                            if first and t == 1:
                                pe.wait_ge(wo_split, 1)
                            pe.wait_ge(oT_ready, tiled(b, t))
                            pe.wait_ge(q_ready, tiled(b, min(t + KB + 1, TB) if last else t + KB + 1))
                            split_products(pe, proj_ps, lambda part, k: oT[:, part, k, :],
                                           lambda part, k: wo[:, part, k, :]).then_inc(proj_done, 1)
                        if there(first, last, t):
                            pe.wait_ge(pT_ready, tiled(b, t + 1))
                            pe.wait_ge(norm_done, tiled(b, t))
                            if there(first, last, t - 3):
                                pe.wait_ge(logits_ready, tiled(b, t - 2))
                            for r in range(PAIRS):
                                for n, (h, i) in enumerate(PRODUCTS):
                                    mm = pe.matmul(att_ps[:, r, 0:VW], pT[:, h, r, :],
                                                   vblk[:, i, bass.ds(b, 1), r, :].rearrange("p o n -> p (o n)"),
                                                   start=(n == 0), stop=(n == 2))
                            mm.then_inc(att_done, 1)
                        if not last:
                            if there(first, last, t - 2):
                                pe.wait_ge(nT_ready, tiled(b, t - 1))
                            elif t > 0:
                                pe.wait_ge(oT_ready, tiled(b, t))
                            x_turn(t, lambda c, t=t: tiled(b, TB + t + c))
                        scores_early = t % 4 == 3 or (last and t > 3)
                        if scores_early:
                            next_scores(b, first, last, t + 2)
                        q = t + KB + 1
                        if there(first, last, q):
                            pe.wait_ge(x1_done, tiled(b, t))
                            pe.wait_ge(xT_ready, tiled(b, 4 * (q // KB) + 4))
                            project_q(q)
                        if there(first, last, t):
                            pe.wait_ge(olo_done, tiled(b, t + 1))
                            if not last:
                                pe.wait_ge(xT_ready, tiled(b, TB + t + 1))
                            else:
                                pe.wait_ge(nT_ready, tiled(b, t - 1))
                            transposes(pe, turn16_ps, ohl, KB).then_inc(oturn_done, 1)
                        if there(first, last, t - 2):
                            pe.wait_ge(nT_ready, tiled(b, t - 1))
                            split_products(pe, gate_ps, lambda part, k: nT[:, part, k, :],
                                           lambda part, k: gate[:, part, k, :]).then_inc(gate_done, 1)
                        if not scores_early:
                            next_scores(b, first, last, t + 2)

                batches(pe, batch)

        consts2, iotas_ready, picked, prefix_done, softmax_sub, softmax_exp, routed = (
            sem("consts2"), sem("iotas_ready"), sem("picked"), sem("prefix_done"), sem("softmax_sub"),
            sem("softmax_exp"), sem("routed"))
        pads_placed, pads_scattered = sem("pads_placed"), sem("pads_scattered")
        route_step, downb_loaded = sem("route_step"), sem("downb_loaded")
        U32 = mybir.dt.uint32
        N_IOTA = SLOTS + TILES + E + PADS
        iota_i = rt(1, N_IOTA).rearrange("p a c -> p (a c)").bitcast(I32)
        iota_f = rt(1, N_IOTA).rearrange("p a c -> p (a c)")
        slot_f, thresholds, ranks_f, pad_f = (iota_f[:, 0:SLOTS], iota_f[:, SLOTS:SLOTS + TILES],
                                              iota_f[:, SLOTS + TILES:N_IOTA - PADS], iota_f[:, N_IOTA - PADS:])
        before = rt(1, P, F16).rearrange("p a c -> p (a c)")
        ones_m = rt(1, P, F16).rearrange("p a c -> p (a c)")
        picks16 = rt(dt=F16)
        shifted, prob8, masked, scratch8 = rt(), rt(), rt(), rt()
        first_hot, second_hot, places_f = rt(), rt(), rt()
        PAD_T, PAD_E = TILES // 2, E // 2
        sums = [rt(PAD_T + TILES), rt(PAD_T + TILES)]
        totals_pad = rt(PAD_T + TILES)
        totals = totals_pad[:, PAD_T:, :]
        top, w_first, w_second, best, found = rt(c=1), rt(c=1), rt(c=1), rt(c=1), rt(c=1)
        pos_f = rt(c=1)
        counts = rt(E, TILES)
        used_count_pad, starts = rt(2, PAD_E + E), rt(2, E)
        used_count = used_count_pad[:, :, PAD_E:]
        used, count = used_count[:, 0, :], used_count[:, 1, :]
        ends = [rt(2, PAD_E + E), rt(2, PAD_E + E)]
        base, pad_start = rt(E, 1), rt(E, 1)
        pad_ge, pad_sum = rt(PADS, E), rt(PADS, 1)
        slot_ge = rt(SLOTS, E)
        slot_sum = rt(SLOTS, 1)
        assert cuts["rt"] <= FFN0
        prefix_ps = psum[:, 6, 0:TILES * E].rearrange("p (t e) -> p t e", e=E)
        totals_ps = psum[:, 7, 0:TILES * E].rearrange("p (t e) -> p t e", e=E)


        def stage_sems(tag):
            names = ("turned", "eT_ready", "up_done", "silu_done", "hhi_done", "hidden_split", "down_done", "y_done")
            return [sem(f"{tag}_{n}") for n in names]

        def up_product(pe, dst, place, j):
            for m in range(KB):
                n = 0
                for k in range(KB):
                    for a, c in PRODUCTS:
                        w = weights[:, place, 0, a, k, m * P:(m + 1) * P] if isinstance(place, int) else \
                            weights[:, bass.ds(place, 1), 0, a, k, m * P:(m + 1) * P].rearrange("p o n -> p (o n)")
                        last = pe.matmul(dst[:, m * P:(m + 1) * P], w, eT[:, j, c, k, :],
                                         start=(n == 0), stop=(n == 3 * KB - 1))
                        n += 1
            return last

        def down_product(pe, dst, place, j):
            n = 0
            for k in range(KB):
                for a, c in PRODUCTS:
                    w = weights[:, place, 1, c, k, :] if isinstance(place, int) else \
                        weights[:, bass.ds(place, 1), 1, c, k, :].rearrange("p o n -> p (o n)")
                    last = pe.matmul(dst, hhl[:, j, a, k * P:(k + 1) * P], w, start=(n == 0), stop=(n == 3 * KB - 1))
                    n += 1
            return last

        def silu_blocks(act, i, bias):
            for m in range(KB):
                cols = slice(m * P, (m + 1) * P)
                ins = act.activation(hid[:, cols], up_ps[i % 2][:, cols], ACT.Silu, bias=bias(m), scale=1.0 / WSCALE)
            return ins

        def split_hidden(dve, j, silu_done, hhi_done, hidden_split, count):
            dve.wait_ge(silu_done, count)
            dve.tensor_copy(hhl[:, j, HI, :], hid).then_inc(hhi_done, 1)
            dve.wait_ge(hhi_done, count)
            dve.tensor_tensor(hhl[:, j, LO, :], hid, hhl[:, j, HI, :], ALU.subtract).then_inc(hidden_split, 1)

        TI = 6
        row_loaded = [sem(f"row_loaded{i}") for i in range(NROW)]
        x1_loaded = [sem(f"x1_loaded{i}") for i in range(NROW)]
        sc_loaded = [sem(f"sc_loaded{i}") for i in range(NROW)]
        scattered = [sem(f"scattered{i}") for i in range(NROW)]
        turned, eT_ready, up_done, silu_done, hhi_done, hidden_split, down_done, y_done = stage_sems("shared")
        meta_copied = sem("meta_copied")
        y_stored = s2("y_stored")
        estage_loaded = s2("estage_loaded")
        est_hi, est_split = sem("est_hi"), sem("est_split")
        POOL_CHUNKS = 6
        est_scaled, est_split_first = sem("est_scaled"), sem("est_split_first")
        CHUNKS = [[0, 1], [2], [3], [4, 5], [6], [7], [], []]
        NBODY2 = PLACES - EARLY

        with nc.Block() as block:

            @block.sync
            def _(sp):
                for i in range(NROW):
                    sp.dma_start(rows[:, i, :], xrows[i, :, D:XROW]).then_inc(row_loaded[i], 16)
                    if i < 2:
                        sp.dma_start(x1_rows[:, i, :], xrows[i, :, 0:D]).then_inc(x1_loaded[i], 16)
                for j in range(2):
                    sp.dma_start(estage[:, j, :], ffn_w[EARLY, 0, j * P:(j + 1) * P, :]).then_inc(estage_loaded[j], 16)

                sp.wait_ge(turned, 1)
                sp.dma_start(rows[:, 0, :], xrows[NROW, :, D:XROW]).then_inc(row_loaded[0], 16)
                sp.dma_start(downb, down_b.rearrange("(o e) n -> o e n", o=1).to_broadcast([P, PLACES, D])
                             ).then_inc(downb_loaded, 16)

                def body(b, first, last):
                    tiles = TI + 2 * last
                    for t in range(tiles):
                        if t + NROW + 1 < tiles or not last:
                            i = (t + 1) % NROW
                            sp.wait_ge(turned, b * TI + t + 2)
                            settled(sp)
                            sp.dma_start(rows[:, i, :], xrows[bass.ds(b * TI + t + NROW + 1, 1), :, D:XROW]
                                         .rearrange("o p n -> p (o n)")).then_inc(row_loaded[i], 16)
                        if t + 2 < tiles or not last:
                            sp.wait_ge(y_done, b * TI + t)
                            settled(sp)
                            sp.dma_start(x1_rows[:, (t + 2) % NROW, :],
                                         xrows[bass.ds(b * TI + t + 2, 1), :, 0:D].rearrange("o p n -> p (o n)")
                                         ).then_inc(x1_loaded[(t + 2) % NROW], 16)
                        for j in CHUNKS[t]:
                            if not (last and j >= 6):
                                if first and j < POOL_CHUNKS:
                                    sp.wait_ge(est_split_first, j + 1)
                                else:
                                    sp.wait_ge(est_split, b * 8 + j + 1 - POOL_CHUNKS)
                                c = (j + 2) % 8
                                sp.dma_start(estage[:, j % 2, :],
                                             ffn_w[bass.ds(b + EARLY + (j + 2) // 8, 1), c // KB,
                                                   (c % KB) * P:(c % KB + 1) * P, :].rearrange("o p n -> p (o n)")
                                             ).then_inc(estage_loaded[j % 2], 16)
                        sp.wait_ge(y_done, b * TI + t + 1)
                        sp.dma_start(out[bass.ds((b * TI + t) * P, P), :], yout[:, t % 2, :]
                                     ).then_inc(y_stored[t % 2], 16)

                bodies(sp, NBODY2, body)
                for i in range(2):
                    sp.wait_ge(y_stored[i], 16 * TILES // 2)
                sp.wait_ge(downb_loaded, 16)

            @block.scalar
            def _(act):
                def turned_out(i, count, up_count=None):
                    act.wait_ge(turned, count)
                    if up_count is not None:
                        act.wait_ge(up_done, up_count)
                    act.activation(eT[:, i % 2], eturn16_ps[i % 2], ACT.Copy).then_inc(eT_ready, 1)

                def silu(i, count, split_count=None):
                    act.wait_ge(up_done, count)
                    if split_count is not None:
                        act.wait_ge(hidden_split, split_count)
                    silu_blocks(act, i, lambda m: upb[:, m:m + 1]).then_inc(silu_done, 1)

                turned_out(0, 1)
                turned_out(1, 2)
                act.wait_ge(softmax_sub, 1)
                act.activation(shifted, shifted, ACT.Exp).then_inc(softmax_exp, 1)
                silu(0, 1)

                def body(b, first, last):
                    for t in range(TI + 2 * last):
                        if not (last and t >= TI):
                            turned_out(t, b * TI + t + 3, b * TI + t + 1)
                        if not (last and t == TI + 1):
                            silu(t + 1, b * TI + t + 2, b * TI + t + 1)
                        for j in CHUNKS[t]:
                            act.wait_ge(estage_loaded[j % 2], b * 64 + 16 * (j // 2 + 1))
                            w = weights[:, bass.ds(b + EARLY, 1), j // KB, HI, j % KB, :].rearrange("p o n -> p (o n)")
                            if first and j < POOL_CHUNKS:
                                act.activation(w, estage[:, j % 2, :], ACT.Copy, scale=WSCALE)
                                act.activation(estage[:, j % 2, :], estage[:, j % 2, :], ACT.Copy, scale=WSCALE
                                               ).then_inc(est_scaled, 1)
                            else:
                                act.activation(w, estage[:, j % 2, :], ACT.Copy, scale=WSCALE).then_inc(est_hi, 1)

                bodies(act, NBODY2, body)

            @block.gpsimd
            def _(pool):
                pool.iota(iota_i[:, 0:SLOTS], pattern=[[1, SLOTS]], base=0, channel_multiplier=0)
                pool.iota(iota_i[:, SLOTS:SLOTS + TILES], pattern=[[P, TILES]], base=0, channel_multiplier=0)
                pool.iota(iota_i[:, SLOTS + TILES:N_IOTA - PADS], pattern=[[-1, E]], base=E, channel_multiplier=0)
                pool.iota(iota_i[:, N_IOTA - PADS:], pattern=[[P, PADS]], base=0, channel_multiplier=1
                          ).then_inc(iotas_ready, 1)
                pool.iota(meta[:, :, 0].bitcast(I32), pattern=[[P, TILES]], base=0, channel_multiplier=1
                          ).then_inc(iotas_ready, 1)
                for padded in sums + [totals_pad]:
                    pool.memset(padded[:, 0:PAD_T, :], 0.0)
                for padded in ends + [used_count_pad]:
                    pool.memset(padded[:, :, 0:PAD_E], 0.0)
                pool.memset(ones_m, 1.0)
                pool.memset(before, 1.0).then_inc(consts2, 1)
                pool.wait_ge(consts2, 1)
                pool.affine_select(out=before, in_=before, compare_op=ALU.is_gt, fill=0.0, base=0,
                                   pattern=[[1, P]], channel_multiplier=-1).then_inc(consts2, 1)
                def load(i, tile):
                    pool.dma_start(sc_rows[:, i, 0:D], tile).then_inc(sc_loaded[i], 16)

                load(0, xrows[0, :, D:XROW])
                load(1, xrows[1, :, D:XROW])
                for j in range(POOL_CHUNKS):
                    pool.wait_ge(est_scaled, j + 1)
                    pool.tensor_tensor(weights[:, EARLY, j // KB, LO, j % KB, :], estage[:, j % 2, :],
                                       weights[:, EARLY, j // KB, HI, j % KB, :], ALU.subtract
                                       ).then_inc(est_split_first, 1)
                pool.wait_ge(routed, 1)

                def body(b, first, last):
                    tiles = TI + 2 * last
                    for t in range(tiles):
                        if (t + 1 < tiles or not last) and not (first and t == 0):
                            i = (t + 1) % NROW
                            if not (first and t == 1):
                                pool.wait_ge(scattered[i], b * 64 + 32 * ((t + 1) // NROW))
                                settled(pool)
                            load(i, xrows[bass.ds(b * TI + t + 1, 1), :, D:XROW].rearrange("o p n -> p (o n)"))
                        i = t % NROW
                        pool.wait_ge(sc_loaded[i], b * 32 + 16 * (t // NROW + 1))
                        pool.tensor_copy(sc_rows[:, i, D:D + META + TOPK].bitcast(I32),
                                         meta[:, bass.ds(b * TI + t, 1), :].rearrange("p o n -> p (o n)").bitcast(I32)
                                         ).then_inc(meta_copied, 1)
                        pool.wait_ge(meta_copied, b * TI + t + 1)
                        settled(pool)
                        for k in range(TOPK):
                            pool.indirect_dma_start(
                                out=sorted_rows[:, :],
                                out_offset=bass.IndirectOffsetOnAxis(
                                    ap=sc_rows[:, i, D + META + k:D + META + k + 1].bitcast(U32), axis=0),
                                in_=sc_rows[:, i, 0:ROW], in_offset=None).then_inc(scattered[i], 16)
                        if last and t < PADS:
                            pool.wait_ge(pads_placed, 1)
                            pool.indirect_dma_start(
                                out=sorted_rows[:, :],
                                out_offset=bass.IndirectOffsetOnAxis(ap=pad_pos[:, t:t + 1].bitcast(U32), axis=0),
                                in_=zero_row, in_offset=None).then_inc(pads_scattered, 16)
                bodies(pool, NBODY2, body)
                pool.wait_ge(pads_scattered, 16 * PADS)
                for i in range(NROW):
                    pool.wait_ge(scattered[i], 32 * ((TILES - 1 - i) // NROW + 1))

            @block.vector
            def _(dve):
                steps = 0

                def step(instruction):
                    nonlocal steps
                    steps += 1
                    instruction.then_inc(route_step, 1)
                    dve.wait_ge(route_step, steps)

                def over_experts(v):
                    return v.unsqueeze(2).to_broadcast([P, TILES, E])

                ranks = ranks_f.unsqueeze(1).to_broadcast([P, TILES, E])

                def pick(scores, weight, one_hot):
                    step(dve.tensor_reduce(weight, scores, AX.X, ALU.max))
                    step(dve.tensor_tensor(scratch8, scores, over_experts(weight), ALU.is_equal))
                    step(dve.tensor_tensor(scratch8, scratch8, ranks, ALU.mult))
                    step(dve.tensor_reduce(found, scratch8, AX.X, ALU.max))
                    step(dve.tensor_tensor(one_hot, ranks, over_experts(found), ALU.is_equal))

                def pick_first():
                    step(dve.tensor_reduce(top, logits, AX.X, ALU.max))
                    dve.tensor_tensor(shifted, logits, over_experts(top), ALU.subtract).then_inc(softmax_sub, 1)
                    dve.wait_ge(iotas_ready, 2)
                    step(dve.tensor_copy(iota_f, iota_i))
                    step(dve.memset(meta[:, :, 2 * E + 1:META], 0.0))
                    dve.wait_ge(softmax_exp, 1)
                    step(dve.tensor_reduce(best, shifted, AX.X, ALU.add))
                    step(dve.reciprocal(best, best))
                    step(dve.tensor_tensor(prob8, shifted, over_experts(best), ALU.mult))
                    pick(prob8, w_first, first_hot)

                def pick_second():
                    step(dve.scalar_tensor_tensor(out=masked, in0=first_hot, scalar=-2.0, in1=prob8,
                                                  op0=ALU.mult, op1=ALU.add))
                    pick(masked, w_second, second_hot)
                    dve.tensor_tensor(picks16, first_hot, second_hot, ALU.add).then_inc(picked, 1)

                def weigh():
                    step(dve.tensor_tensor(best, w_first, w_second, ALU.add))
                    step(dve.tensor_scalar(best, best, 1e-20, None, ALU.add))
                    step(dve.reciprocal(best, best))
                    step(dve.tensor_tensor(w_first, w_first, best, ALU.mult))
                    step(dve.tensor_tensor(w_second, w_second, best, ALU.mult))
                    step(dve.tensor_tensor(scratch8, first_hot, over_experts(w_first), ALU.mult))
                    step(dve.tensor_tensor(masked, second_hot, over_experts(w_second), ALU.mult))
                    step(dve.tensor_tensor(meta[:, :, 1:E + 1], scratch8, masked, ALU.add))
                    step(dve.tensor_scalar(meta[:, :, E + 1:2 * E + 1], meta[:, :, 1:E + 1], 1.0 / WSCALE, None,
                                           ALU.mult))

                def sum_tiles():
                    dve.wait_ge(consts2, 2)
                    dve.wait_ge(prefix_done, 1)
                    step(dve.tensor_copy(totals, totals_ps))
                    src = totals_pad
                    for n, shift in enumerate((1, 2, 4, 8, 16)):
                        dst = sums[n % 2]
                        step(dve.tensor_tensor(dst[:, PAD_T:, :], src[:, PAD_T:, :],
                                               src[:, PAD_T - shift:PAD_T + TILES - shift, :], ALU.add))
                        src = dst
                    return src[:, PAD_T:, :]

                def start_experts(up_to):
                    step(dve.tensor_tensor(counts, up_to[:, TILES - 1, :].unsqueeze(2).to_broadcast([P, E, TILES]),
                                           thresholds.unsqueeze(1).to_broadcast([P, E, TILES]), ALU.is_gt))
                    step(dve.tensor_reduce(used, counts, AX.X, ALU.add))
                    step(dve.tensor_copy(count, up_to[:, TILES - 1, :]))
                    src = used_count_pad
                    for n, shift in enumerate((1, 2, 4)):
                        dst = ends[n % 2]
                        step(dve.tensor_tensor(dst[:, :, PAD_E:], src[:, :, PAD_E:],
                                               src[:, :, PAD_E - shift:PAD_E + E - shift], ALU.add))
                        src = dst
                    end = src[:, :, PAD_E:]
                    step(dve.tensor_tensor(starts, end, used_count, ALU.subtract))
                    step(dve.tensor_scalar(base, starts[:, 0, :], float(P), None, ALU.mult))
                    return end[:, 0, :]

                def place_pairs(up_to):
                    step(dve.tensor_tensor(places_f, up_to, totals, ALU.subtract))
                    step(dve.tensor_tensor(places_f, prefix_ps, places_f, ALU.add))
                    step(dve.tensor_tensor(places_f, places_f, base.unsqueeze(1).to_broadcast([P, TILES, E]), ALU.add))
                    for k, one_hot in enumerate((first_hot, second_hot)):
                        step(dve.tensor_tensor(scratch8, places_f, one_hot, ALU.mult))
                        step(dve.tensor_reduce(pos_f, scratch8, AX.X, ALU.add))
                        ins = dve.tensor_copy(meta[:, :, META + k].bitcast(I32), pos_f)
                        if k == 0:
                            step(ins)
                    ins.then_inc(routed, 1)

                def place_slots(end):
                    step(dve.tensor_tensor(slot_ge, slot_f.unsqueeze(2).to_broadcast([P, SLOTS, E]),
                                           end.unsqueeze(1).to_broadcast([P, SLOTS, E]), ALU.is_ge))
                    step(dve.tensor_reduce(slot_sum, slot_ge, AX.X, ALU.add))
                    step(dve.tensor_scalar(slot_place, slot_sum, 1.0, float(E), ALU.add, ALU.min))

                def place_pads():
                    step(dve.tensor_tensor(pad_start, base, starts[:, 1, :], ALU.subtract))
                    step(dve.tensor_tensor(pad_ge, pad_f.unsqueeze(2).to_broadcast([P, PADS, E]),
                                           pad_start.unsqueeze(1).to_broadcast([P, PADS, E]), ALU.is_ge))
                    step(dve.tensor_tensor(pad_ge, pad_ge, count.unsqueeze(1).to_broadcast([P, PADS, E]), ALU.mult))
                    step(dve.tensor_reduce(pad_sum, pad_ge, AX.X, ALU.add))
                    dve.tensor_tensor(pad_pos, pad_sum, pad_f, ALU.add).then_inc(pads_placed, 1)

                pick_first()
                split_hidden(dve, 0, silu_done, hhi_done, hidden_split, 1)

                def body(b, first, last):
                    for t in range(TI + 2 * last):
                        n = b * TI + t
                        if not (last and t == TI + 1):
                            dve.wait_ge(down_done, n)
                            split_hidden(dve, (t + 1) % 2, silu_done, hhi_done, hidden_split, n + 2)
                        dve.wait_ge(down_done, n + 1)
                        dve.wait_ge(x1_loaded[t % NROW], b * 32 + 16 * (t // NROW + 1))
                        dve.wait_ge(y_stored[t % 2], b * 48 + 16 * (t // 2))
                        dve.scalar_tensor_tensor(out=yout[:, t % 2, :], in0=down_ps[t % 2], scalar=1.0 / WSCALE,
                                                 in1=x1_rows[:, t % NROW, :], op0=ALU.mult, op1=ALU.add
                                                 ).then_inc(y_done, 1)
                        for j in CHUNKS[t]:
                            if first and j < POOL_CHUNKS:
                                continue
                            dve.wait_ge(est_hi, b * 8 + j + 1 - POOL_CHUNKS)
                            w = [weights[:, bass.ds(b + EARLY, 1), j // KB, h, j % KB, :].rearrange("p o n -> p (o n)")
                                 for h in range(2)]
                            dve.scalar_tensor_tensor(out=w[LO], in0=estage[:, j % 2, :], scalar=WSCALE, in1=w[HI],
                                                     op0=ALU.mult, op1=ALU.subtract).then_inc(est_split, 1)
                        if first and t == 0:
                            pick_second()
                        elif first and t == 1:
                            weigh()
                        elif first and t == 2:
                            up_to = sum_tiles()
                            end = start_experts(up_to)
                        elif first and t == 3:
                            place_pairs(up_to)
                        elif first and t == 4:
                            place_slots(end)
                            place_pads()

                bodies(dve, NBODY2, body)

            @block.tensor
            def _(pe):
                def turn(i, loaded):
                    pe.wait_ge(row_loaded[i % NROW], loaded)
                    transposes(pe, eturn16_ps[i % 2], parts(rows[:, i % NROW, :]), KB).then_inc(turned, 1)

                turn(0, 16)
                turn(1, 16)
                pe.wait_ge(eT_ready, 1)
                up_product(pe, up_ps[0], 0, 0).then_inc(up_done, 1)
                def body(b, first, last):
                    for t in range(TI + 2 * last):
                        n = b * TI + t
                        if not (last and t == TI + 1):
                            pe.wait_ge(eT_ready, n + 2)
                            pe.wait_ge(silu_done, n)
                            up_product(pe, up_ps[(t + 1) % 2], 0, (t + 1) % 2).then_inc(up_done, 1)
                        if not (last and t >= TI):
                            turn(t + 2, b * 32 + 16 * ((t + 2) // NROW + 1))
                        if first and t == 1:
                            pe.wait_ge(picked, 1)
                            pe.wait_ge(consts2, 2)
                            flat = picks16.rearrange("p t e -> p (t e)")
                            pe.matmul(psum[:, 6, 0:TILES * E], before, flat, start=True, stop=True)
                            pe.matmul(psum[:, 7, 0:TILES * E], ones_m, flat, start=True, stop=True
                                      ).then_inc(prefix_done, 1)
                        pe.wait_ge(hidden_split, n + 1)
                        pe.wait_ge(y_done, n)
                        down_product(pe, down_ps[t % 2], 0, t % 2).then_inc(down_done, 1)

                bodies(pe, NBODY2, body)

        slot_loaded = [sem(f"slot_loaded{i}") for i in range(NSLOT)]
        turned, eT_ready, up_done, silu_done, hhi_done, hidden_split, down_done, y_done = stage_sems("slot")
        bias_weighted = sem("bias_weighted")
        added = s2("added")
        TI = 2 * NSLOT
        BODIES = -(-SLOTS // TI)

        def slots_of(last):
            return SLOTS - (BODIES - 1) * TI if last else TI

        AHEAD = 4

        with nc.Block() as block:

            def place_of(eng, n):
                return eng.value_load(slot_place[0:1, bass.ds(n, 1)], min_val=1, max_val=E)

            @block.sync
            def _(sp):
                for i in range(AHEAD):
                    sp.dma_start(slots[:, i, :], sorted_rows[i * P:(i + 1) * P, :]).then_inc(slot_loaded[i], 16)

                def body(b, first, last):
                    for t in range(slots_of(last)):
                        if not (last and t + AHEAD >= slots_of(last)):
                            sp.wait_ge(added[t % 2], b * 96 + 16 * (t // 2))
                            settled(sp)
                            i = (t + AHEAD) % NSLOT
                            sp.dma_start(slots[:, i, :], sorted_rows[bass.ds((b * TI + t + AHEAD) * P, P), :]
                                         ).then_inc(slot_loaded[i], 16)

                bodies(sp, BODIES, body)

            @block.scalar
            def _(act):
                def turned_out(i, count, up_count=None):
                    act.wait_ge(turned, count)
                    if up_count is not None:
                        act.wait_ge(up_done, up_count)
                    act.activation(eT[:, i % 2], eturn16_ps[i % 2], ACT.Copy).then_inc(eT_ready, 1)

                def silu(i, n, count, split_count=None):
                    place = place_of(act, n)
                    act.wait_ge(up_done, count)
                    if split_count is not None:
                        act.wait_ge(hidden_split, split_count)
                    silu_blocks(act, i, lambda m: upb[:, bass.ds(place * KB + m, 1)]).then_inc(silu_done, 1)

                turned_out(0, 1)
                turned_out(1, 2)
                silu(0, 0, 1)

                def body(b, first, last):
                    for t in range(slots_of(last)):
                        n = b * TI + t
                        if not (last and t >= slots_of(last) - 2):
                            turned_out(t, n + 3, n + 1)
                        if not (last and t == slots_of(last) - 1):
                            silu(t + 1, n + 1, n + 2, n + 1)
                        place = place_of(act, n)
                        act.wait_ge(slot_loaded[t % NSLOT], b * 32 + 16 * (t // NSLOT + 1))
                        act.wait_ge(y_done, n)
                        act.activation(wbias, downb[:, bass.ds(place, 1), :].rearrange("p o n -> p (o n)"), ACT.Copy,
                                       scale=slots[:, t % NSLOT, bass.ds(D + place, 1)]).then_inc(bias_weighted, 1)

                bodies(act, BODIES, body)

            @block.gpsimd
            def _(pool):
                def body(b, first, last):
                    for t in range(slots_of(last)):
                        pool.wait_ge(y_done, b * TI + t + 1)
                        pool.wait_ge(added[(t + 1) % 2], b * 96 + 16 * ((t + 1) // 2))
                        settled(pool)
                        pool.indirect_dma_start(
                            out=out[:, :],
                            out_offset=bass.IndirectOffsetOnAxis(
                                ap=slots[:, t % NSLOT, D:D + 1].bitcast(U32), axis=0),
                            in_=yout[:, t % 2, :], in_offset=None, compute_op=ALU.add).then_inc(added[t % 2], 16)

                bodies(pool, BODIES, body)
                for i in range(2):
                    pool.wait_ge(added[i], 16 * ((SLOTS + 1 - i) // 2))

            @block.vector
            def _(dve):
                split_hidden(dve, 0, silu_done, hhi_done, hidden_split, 1)

                def body(b, first, last):
                    for t in range(slots_of(last)):
                        n = b * TI + t
                        if not (last and t == slots_of(last) - 1):
                            dve.wait_ge(down_done, n)
                            split_hidden(dve, (t + 1) % 2, silu_done, hhi_done, hidden_split, n + 2)
                        place = place_of(dve, n)
                        dve.wait_ge(down_done, n + 1)
                        dve.wait_ge(bias_weighted, n + 1)
                        dve.wait_ge(added[t % 2], b * 96 + 16 * (t // 2))
                        dve.scalar_tensor_tensor(out=yout[:, t % 2, :], in0=down_ps[t % 2],
                                                 scalar=slots[:, t % NSLOT, bass.ds(D + E + place, 1)],
                                                 in1=wbias, op0=ALU.mult, op1=ALU.add).then_inc(y_done, 1)

                bodies(dve, BODIES, body)

            @block.tensor
            def _(pe):
                def turn(i, loaded):
                    pe.wait_ge(slot_loaded[i % NSLOT], loaded)
                    transposes(pe, eturn16_ps[i % 2], parts(slots[:, i % NSLOT, :]), KB).then_inc(turned, 1)

                turn(0, 16)
                turn(1, 16)
                pe.wait_ge(eT_ready, 1)
                up_product(pe, up_ps[0], place_of(pe, 0), 0).then_inc(up_done, 1)

                def body(b, first, last):
                    place = place_of(pe, b * TI)
                    for t in range(slots_of(last)):
                        n = b * TI + t
                        if not (last and t == slots_of(last) - 1):
                            next_place = place_of(pe, n + 1)
                            pe.wait_ge(eT_ready, n + 2)
                            pe.wait_ge(silu_done, n)
                            up_product(pe, up_ps[(t + 1) % 2], next_place, (t + 1) % 2).then_inc(up_done, 1)
                        if not (last and t >= slots_of(last) - 2):
                            turn(t + 2, b * 32 + 16 * ((t + 2) // NSLOT + 1))
                        pe.wait_ge(hidden_split, n + 1)
                        pe.wait_ge(y_done, n)
                        down_product(pe, down_ps[t % 2], place, t % 2).then_inc(down_done, 1)
                        place = next_place

                bodies(pe, BODIES, body)


INPUTS = ("x", "ctxT", "tau", "delta", "wqT", "wkT", "wvT", "woT", "bq", "bk", "bv", "bo",
          "gateT", "ffn_w", "up_b", "down_b")


def layout(i):
    a = {k: np.asarray(v) for k, v in i.items()}
    ffn_w = np.empty((PLACES, 2, D, D), np.float32)
    ffn_w[0, 0], ffn_w[0, 1] = a["L0_ffn_sh_up_w"], a["L0_ffn_sh_down_w"]
    ffn_w[1:, 0], ffn_w[1:, 1] = a["L0_ffn_up_w"], a["L0_ffn_down_w"]
    t = np.ascontiguousarray

    def columns(bias):
        return t(bias.reshape(-1, P).T)

    return {
        "x": a["x"].reshape(TILES, P, D),
        "ctxT": t(a["ctx_1024"].reshape(B * SK, D).T),
        "tau": a["condB_tau"],
        "delta": a["fside_BxS2_0"].reshape(B * SK),
        "wqT": t(a["L0_xcond_Wq"].T), "wkT": t(a["L0_xcond_Wk"].T),
        "wvT": t(a["L0_xcond_Wv"].T), "woT": t(a["L0_xcond_Wo"].T),
        "bq": columns(a["L0_xcond_bq"]), "bk": columns(a["L0_xcond_bk"]),
        "bv": a["L0_xcond_bv"], "bo": a["L0_xcond_bo"],
        "gateT": t(a["L0_ffn_gate_w"].T),
        "ffn_w": ffn_w,
        "up_b": columns(np.concatenate([a["L0_ffn_sh_up_b"][None], a["L0_ffn_up_b"]])),
        "down_b": np.concatenate([a["L0_ffn_sh_down_b"][None], a["L0_ffn_down_b"]]),
    }


def kernel(**inputs):
    import concourse.bacc as bacc
    from concourse.bass_utils import run_bass_kernel_spmd

    nc = bacc.Bacc("TRN2", target_bir_lowering=False, num_devices=1)
    arrays = {f"in_{k}": v for k, v in layout(inputs).items()}
    args = [nc.dram_tensor(f"in_{k}", arrays[f"in_{k}"].shape, F32, kind="ExternalInput").ap() for k in INPUTS]
    out = nc.dram_tensor("out", (TOKENS + P, D), F32, kind="ExternalOutput").ap()
    build_program(nc, *args, out)
    r = run_bass_kernel_spmd(nc, [arrays], core_ids=[0])
    return r.results[0]["out"][:TOKENS].reshape(B, S, D)
```
